# Optimizing a Trainium2 kernel written in Bass

```python
import numpy as np
import jax
import jax.numpy as jnp

def _softmax(x, axis=-1):
    return jax.nn.softmax(x, axis=axis)

def _gelu(x):
    return jax.nn.gelu(x, approximate=True)

def _silu(x):
    return jax.nn.silu(x)

def _sigmoid(x):
    return jax.nn.sigmoid(x)

def _layernorm(x, axis=-1, eps=1e-05):
    m = jnp.mean(x, axis=axis, keepdims=True)
    v = jnp.var(x, axis=axis, keepdims=True)
    return (x - m) / jnp.sqrt(v + eps)

def _scatter_add(tgt, idx, src, axis=0):
    return tgt.at[idx].add(src)

def _segment_sum(src, seg, n):
    return jax.ops.segment_sum(src, seg, n)
kernel_name = 'mk_flamingo_gated_d2_seqx_r4_45bed9'

def setup_inputs(seed: int=0):
    np.random.seed(seed)
    _w = jnp.asarray

    def _rec_inputs():
        import jax
        import jax.numpy as jnp
        _rk = jax.random.key(seed)
        x = -0.0005207 + 1.001 * jax.random.normal(jax.random.fold_in(_rk, 1), (2, 512, 256), jnp.float32)
        _lenS = 512 - jax.random.randint(jax.random.fold_in(_rk, 7), (2,), 0, max(1, 512 // 4) + 1, jnp.int32)
        _lenS2 = 1024 - jax.random.randint(jax.random.fold_in(_rk, 8), (2,), 0, max(1, 1024 // 4) + 1, jnp.int32)
        _ctx_1024P = jax.random.normal(jax.random.fold_in(_rk, 11), (2, 16, 256), jnp.float32)
        _ctx_1024c = jax.random.dirichlet(jax.random.fold_in(_rk, 511), 0.3 * jnp.ones((16,), jnp.float32), (2, 1024))
        _ctx_1024t = jnp.einsum('bsk,bkd->bsd', _ctx_1024c, _ctx_1024P)
        _ctx_1024t = _ctx_1024t * jax.lax.rsqrt(jnp.mean(jnp.square(_ctx_1024t)) + 1e-12) * 0.953939
        ctx_1024 = -1.52775e-05 + 0.999936 * (_ctx_1024t + 0.3 * jax.random.normal(jax.random.fold_in(_rk, 611), (2, 1024, 256), jnp.float32))
        _g = jax.random.normal(jax.random.fold_in(_rk, 9001), (2, 2), jnp.float32)
        _g = jnp.sign(_g) * jnp.maximum(jnp.abs(_g), 1.0) + (_g == 0) * 1.0
        g_xattn = _g[0]
        g_ffn = _g[1]
        return (x, ctx_1024, g_xattn, g_ffn)
    x, ctx_1024, g_xattn, g_ffn = _rec_inputs()

    def _L0_xattn_setup():
        import jax, jax.numpy as jnp
        import numpy as np
        DIM = 256
        HEADS = 16
        DHEAD = 64
        INNER = HEADS * DHEAD
        EPS = 1e-05

        def layer_norm(x, g, b):
            mu = jnp.mean(x, axis=-1, keepdims=True)
            var = jnp.mean(jnp.square(x - mu), axis=-1, keepdims=True)
            return (x - mu) * jax.lax.rsqrt(var + EPS) * g + b

        def apply_rope(x, cos, sin):
            d2 = x.shape[-1] // 2
            x1, x2 = (x[..., :d2], x[..., d2:])
            return jnp.concatenate([x1 * cos - x2 * sin, x2 * cos + x1 * sin], axis=-1)
        key = jax.random.key(seed)
        ks = jax.random.split(key, 10)
        B, N, S = (8, 64, 1024)
        latents = jax.random.normal(ks[0], (B, N, DIM), dtype=jnp.float32)
        context = jax.random.normal(ks[1], (B, S, DIM), dtype=jnp.float32)
        cos = jax.random.uniform(ks[2], (S, DHEAD // 2), dtype=jnp.float32)
        sin = jax.random.uniform(ks[3], (S, DHEAD // 2), dtype=jnp.float32)
        init = lambda k, shp, fan_in: jax.random.normal(k, shp, dtype=jnp.float32) / np.sqrt(fan_in)
        return {'latents': latents, 'context': context, 'cos': cos, 'sin': sin, 'ln_lat_g': jnp.ones((DIM,), jnp.float32), 'ln_lat_b': jnp.zeros((DIM,), jnp.float32), 'ln_ctx_g': jnp.ones((DIM,), jnp.float32), 'ln_ctx_b': jnp.zeros((DIM,), jnp.float32), 'Wq': init(ks[4], (DIM, INNER), DIM), 'Wkv': init(ks[5], (DIM, 2 * INNER), DIM), 'Wo': init(ks[6], (INNER, DIM), INNER), 'bo': jnp.zeros((DIM,), jnp.float32)}
    _L0_xattn_all = _L0_xattn_setup()
    _L0_xattn_in = {k: v for k, v in _L0_xattn_all.items() if k in ('cos', 'sin', 'ln_lat_g', 'ln_lat_b', 'ln_ctx_g', 'ln_ctx_b', 'Wq', 'Wkv', 'Wo', 'bo')}
    del _L0_xattn_all

    def _L0_ffn_setup():
        import jax, jax.numpy as jnp
        import numpy as np
        EMBED = 256
        HEADS = 16
        HEAD_DIM = EMBED // HEADS
        NUM_EXPERTS = 8
        TOP_K = 2
        HIDDEN = (int(2 * (4 * EMBED) / 3) + 63) // 64 * 64
        SEQ = 512
        BATCH = 2
        ROPE_BASE = 10000.0
        EPS = 1e-06

        def _rope_tables(seq_len, dim):
            inv_freq = 1.0 / ROPE_BASE ** (np.arange(0, dim, 2, dtype=np.float32) / dim)
            t = np.arange(seq_len, dtype=np.float32)
            freqs = np.einsum('i,j->ij', t, inv_freq)
            emb = np.concatenate([freqs, freqs], axis=-1)
            return (jnp.asarray(np.cos(emb)), jnp.asarray(np.sin(emb)))

        def _rotate_half(x):
            x1, x2 = jnp.split(x, 2, axis=-1)
            return jnp.concatenate([-x2, x1], axis=-1)

        def _rmsnorm(x, w):
            return x * jax.lax.rsqrt(jnp.mean(x * x, axis=-1, keepdims=True) + EPS) * w

        def _attention(x, wq, wk, wv, wo):
            B, S, _ = x.shape
            q = (x @ wq).reshape(B, S, HEADS, HEAD_DIM).transpose(0, 2, 1, 3)
            k = (x @ wk).reshape(B, S, HEADS, HEAD_DIM).transpose(0, 2, 1, 3)
            v = (x @ wv).reshape(B, S, HEADS, HEAD_DIM).transpose(0, 2, 1, 3)
            cos, sin = _rope_tables(S, HEAD_DIM)
            cos = cos[None, None]
            sin = sin[None, None]
            q = q * cos + _rotate_half(q) * sin
            k = k * cos + _rotate_half(k) * sin
            scale = HEAD_DIM ** (-0.5)
            scores = jnp.einsum('bhqd,bhkd->bhqk', q, k) * scale
            causal = jnp.triu(jnp.ones((S, S), bool), k=1)
            scores = jnp.where(causal, -jnp.inf, scores)
            attn = jax.nn.softmax(scores, axis=-1)
            out = jnp.einsum('bhqk,bhkd->bhqd', attn, v)
            out = out.transpose(0, 2, 1, 3).reshape(B, S, EMBED)
            return out @ wo

        def _moe(x, w_router, wg, wu, wd):
            B, S, E = x.shape
            xf = x.reshape(-1, E)
            logits = xf @ w_router
            probs = jax.nn.softmax(logits, axis=-1)
            topw, topi = jax.lax.top_k(probs, TOP_K)
            topw = topw / jnp.sum(topw, axis=-1, keepdims=True)
            combine = jnp.sum(jax.nn.one_hot(topi, NUM_EXPERTS, dtype=xf.dtype) * topw[..., None], axis=1)
            g = jax.nn.silu(jnp.einsum('td,xdh->txh', xf, wg))
            u = jnp.einsum('td,xdh->txh', xf, wu)
            eo = jnp.einsum('txh,xhd->txd', g * u, wd)
            out = jnp.einsum('txd,tx->td', eo, combine)
            return out.reshape(B, S, E)
        key = jax.random.key(seed)
        ks = jax.random.split(key, 12)
        s = 0.02
        return {'x': jax.random.normal(ks[0], (BATCH, SEQ, EMBED), jnp.float32), 'wq': jax.random.normal(ks[1], (EMBED, EMBED), jnp.float32) * s, 'wk': jax.random.normal(ks[2], (EMBED, EMBED), jnp.float32) * s, 'wv': jax.random.normal(ks[3], (EMBED, EMBED), jnp.float32) * s, 'wo': jax.random.normal(ks[4], (EMBED, EMBED), jnp.float32) * s, 'w_router': jax.random.normal(ks[5], (EMBED, NUM_EXPERTS), jnp.float32) * s, 'wg': jax.random.normal(ks[6], (NUM_EXPERTS, EMBED, HIDDEN), jnp.float32) * s, 'wu': jax.random.normal(ks[7], (NUM_EXPERTS, EMBED, HIDDEN), jnp.float32) * s, 'wd': jax.random.normal(ks[8], (NUM_EXPERTS, HIDDEN, EMBED), jnp.float32) * s, 'g1': jnp.ones((EMBED,), jnp.float32), 'g2': jnp.ones((EMBED,), jnp.float32)}
    _L0_ffn_all = _L0_ffn_setup()
    _L0_ffn_in = {k: v for k, v in _L0_ffn_all.items() if k in ('wq', 'wk', 'wv', 'wo', 'w_router', 'wg', 'wu', 'wd', 'g1', 'g2')}
    del _L0_ffn_all

    def _L1_xattn_setup():
        import jax, jax.numpy as jnp
        import numpy as np
        DIM = 256
        NUM_HEADS = 16
        HEAD_DIM = DIM // NUM_HEADS

        def _split(x):
            b, l, _ = x.shape
            return x.reshape(b, l, NUM_HEADS, HEAD_DIM).transpose(0, 2, 1, 3)
        key = jax.random.key(seed)
        ks = jax.random.split(key, 8)
        B, N, M = (4, 512, 512)
        scale = DIM ** (-0.5)
        return {'input': jax.random.normal(ks[0], (B, N, DIM), dtype=jnp.float32), 'memory': jax.random.normal(ks[1], (B, M, DIM), dtype=jnp.float32), 'Wq': jax.random.normal(ks[2], (DIM, DIM), dtype=jnp.float32) * scale, 'bq': jnp.zeros((DIM,), dtype=jnp.float32), 'Wk': jax.random.normal(ks[3], (DIM, DIM), dtype=jnp.float32) * scale, 'bk': jnp.zeros((DIM,), dtype=jnp.float32), 'Wv': jax.random.normal(ks[4], (DIM, DIM), dtype=jnp.float32) * scale, 'bv': jnp.zeros((DIM,), dtype=jnp.float32)}
    _L1_xattn_all = _L1_xattn_setup()
    _L1_xattn_in = {k: v for k, v in _L1_xattn_all.items() if k in ('Wq', 'bq', 'Wk', 'bk', 'Wv', 'bv')}
    del _L1_xattn_all

    def _L1_ffn_setup():
        import jax, jax.numpy as jnp
        import numpy as np
        H = 256
        E = 8
        B, S = (4, 512)
        key = jax.random.key(seed)
        k1, k2, k3, k4 = jax.random.split(key, 4)
        x = jax.random.normal(k1, (B, S, H), dtype=jnp.float32)
        wg = jax.random.normal(k2, (H, E), dtype=jnp.float32) * 0.02
        W = jax.random.normal(k3, (E, H, H), dtype=jnp.float32) * 0.02
        b = jax.random.normal(k4, (E, H), dtype=jnp.float32) * 0.02
        return {'x': x, 'wg': wg, 'W': W, 'b': b}
    _L1_ffn_all = _L1_ffn_setup()
    _L1_ffn_in = {k: v for k, v in _L1_ffn_all.items() if k in ('wg', 'W', 'b')}
    del _L1_ffn_all
    return {'x': x, 'ctx_1024': ctx_1024, 'g_xattn': g_xattn, 'g_ffn': g_ffn, 'L0_xattn_cos': _L0_xattn_in['cos'], 'L0_xattn_sin': _L0_xattn_in['sin'], 'L0_xattn_ln_lat_g': _L0_xattn_in['ln_lat_g'], 'L0_xattn_ln_lat_b': _L0_xattn_in['ln_lat_b'], 'L0_xattn_ln_ctx_g': _L0_xattn_in['ln_ctx_g'], 'L0_xattn_ln_ctx_b': _L0_xattn_in['ln_ctx_b'], 'L0_xattn_Wq': _L0_xattn_in['Wq'], 'L0_xattn_Wkv': _L0_xattn_in['Wkv'], 'L0_xattn_Wo': _L0_xattn_in['Wo'], 'L0_xattn_bo': _L0_xattn_in['bo'], 'L0_ffn_wq': _L0_ffn_in['wq'], 'L0_ffn_wk': _L0_ffn_in['wk'], 'L0_ffn_wv': _L0_ffn_in['wv'], 'L0_ffn_wo': _L0_ffn_in['wo'], 'L0_ffn_w_router': _L0_ffn_in['w_router'], 'L0_ffn_wg': _L0_ffn_in['wg'], 'L0_ffn_wu': _L0_ffn_in['wu'], 'L0_ffn_wd': _L0_ffn_in['wd'], 'L0_ffn_g1': _L0_ffn_in['g1'], 'L0_ffn_g2': _L0_ffn_in['g2'], 'L1_xattn_Wq': _L1_xattn_in['Wq'], 'L1_xattn_bq': _L1_xattn_in['bq'], 'L1_xattn_Wk': _L1_xattn_in['Wk'], 'L1_xattn_bk': _L1_xattn_in['bk'], 'L1_xattn_Wv': _L1_xattn_in['Wv'], 'L1_xattn_bv': _L1_xattn_in['bv'], 'L1_ffn_wg': _L1_ffn_in['wg'], 'L1_ffn_W': _L1_ffn_in['W'], 'L1_ffn_b': _L1_ffn_in['b']}

def reference(x, ctx_1024, g_xattn, g_ffn, L0_xattn_cos, L0_xattn_sin, L0_xattn_ln_lat_g, L0_xattn_ln_lat_b, L0_xattn_ln_ctx_g, L0_xattn_ln_ctx_b, L0_xattn_Wq, L0_xattn_Wkv, L0_xattn_Wo, L0_xattn_bo, L0_ffn_wq, L0_ffn_wk, L0_ffn_wv, L0_ffn_wo, L0_ffn_w_router, L0_ffn_wg, L0_ffn_wu, L0_ffn_wd, L0_ffn_g1, L0_ffn_g2, L1_xattn_Wq, L1_xattn_bq, L1_xattn_Wk, L1_xattn_bk, L1_xattn_Wv, L1_xattn_bv, L1_ffn_wg, L1_ffn_W, L1_ffn_b):
    import jax
    import jax.numpy as jnp

    def _L0_xattn_ref(latents, context, cos, sin, ln_lat_g, ln_lat_b, ln_ctx_g, ln_ctx_b, Wq, Wkv, Wo, bo):
        import jax, jax.numpy as jnp
        import numpy as np
        DIM = 256
        HEADS = 16
        DHEAD = 64
        INNER = HEADS * DHEAD
        EPS = 1e-05

        def layer_norm(x, g, b):
            mu = jnp.mean(x, axis=-1, keepdims=True)
            var = jnp.mean(jnp.square(x - mu), axis=-1, keepdims=True)
            return (x - mu) * jax.lax.rsqrt(var + EPS) * g + b

        def apply_rope(x, cos, sin):
            d2 = x.shape[-1] // 2
            x1, x2 = (x[..., :d2], x[..., d2:])
            return jnp.concatenate([x1 * cos - x2 * sin, x2 * cos + x1 * sin], axis=-1)
        b, n, _ = latents.shape
        s = context.shape[1]
        lat = layer_norm(latents, ln_lat_g, ln_lat_b)
        ctx = layer_norm(context, ln_ctx_g, ln_ctx_b)
        q = (lat @ Wq).reshape(b, n, HEADS, DHEAD).transpose(0, 2, 1, 3)
        kv = ctx @ Wkv
        k, v = jnp.split(kv, 2, axis=-1)
        k = k.reshape(b, s, HEADS, DHEAD).transpose(0, 2, 1, 3)
        v = v.reshape(b, s, HEADS, DHEAD).transpose(0, 2, 1, 3)
        k = apply_rope(k, cos[None, None], sin[None, None])
        scale = DHEAD ** (-0.5)
        attn = jnp.einsum('bhnd,bhsd->bhns', q, k) * scale
        attn = jnp.clip(attn, -11.0, 11.0)
        attn = jax.nn.softmax(attn, axis=-1)
        out = jnp.einsum('bhns,bhsd->bhnd', attn, v)
        out = out.transpose(0, 2, 1, 3).reshape(b, n, INNER)
        return out @ Wo + bo

    def _L0_ffn_ref(x, wq, wk, wv, wo, w_router, wg, wu, wd, g1, g2):
        import jax, jax.numpy as jnp
        import numpy as np
        EMBED = 256
        HEADS = 16
        HEAD_DIM = EMBED // HEADS
        NUM_EXPERTS = 8
        TOP_K = 2
        HIDDEN = (int(2 * (4 * EMBED) / 3) + 63) // 64 * 64
        SEQ = 512
        BATCH = 2
        ROPE_BASE = 10000.0
        EPS = 1e-06

        def _rope_tables(seq_len, dim):
            inv_freq = 1.0 / ROPE_BASE ** (np.arange(0, dim, 2, dtype=np.float32) / dim)
            t = np.arange(seq_len, dtype=np.float32)
            freqs = np.einsum('i,j->ij', t, inv_freq)
            emb = np.concatenate([freqs, freqs], axis=-1)
            return (jnp.asarray(np.cos(emb)), jnp.asarray(np.sin(emb)))

        def _rotate_half(x):
            x1, x2 = jnp.split(x, 2, axis=-1)
            return jnp.concatenate([-x2, x1], axis=-1)

        def _rmsnorm(x, w):
            return x * jax.lax.rsqrt(jnp.mean(x * x, axis=-1, keepdims=True) + EPS) * w

        def _attention(x, wq, wk, wv, wo):
            B, S, _ = x.shape
            q = (x @ wq).reshape(B, S, HEADS, HEAD_DIM).transpose(0, 2, 1, 3)
            k = (x @ wk).reshape(B, S, HEADS, HEAD_DIM).transpose(0, 2, 1, 3)
            v = (x @ wv).reshape(B, S, HEADS, HEAD_DIM).transpose(0, 2, 1, 3)
            cos, sin = _rope_tables(S, HEAD_DIM)
            cos = cos[None, None]
            sin = sin[None, None]
            q = q * cos + _rotate_half(q) * sin
            k = k * cos + _rotate_half(k) * sin
            scale = HEAD_DIM ** (-0.5)
            scores = jnp.einsum('bhqd,bhkd->bhqk', q, k) * scale
            causal = jnp.triu(jnp.ones((S, S), bool), k=1)
            scores = jnp.where(causal, -jnp.inf, scores)
            attn = jax.nn.softmax(scores, axis=-1)
            out = jnp.einsum('bhqk,bhkd->bhqd', attn, v)
            out = out.transpose(0, 2, 1, 3).reshape(B, S, EMBED)
            return out @ wo

        def _moe(x, w_router, wg, wu, wd):
            B, S, E = x.shape
            xf = x.reshape(-1, E)
            logits = xf @ w_router
            probs = jax.nn.softmax(logits, axis=-1)
            topw, topi = jax.lax.top_k(probs, TOP_K)
            topw = topw / jnp.sum(topw, axis=-1, keepdims=True)
            combine = jnp.sum(jax.nn.one_hot(topi, NUM_EXPERTS, dtype=xf.dtype) * topw[..., None], axis=1)
            g = jax.nn.silu(jnp.einsum('td,xdh->txh', xf, wg))
            u = jnp.einsum('td,xdh->txh', xf, wu)
            eo = jnp.einsum('txh,xhd->txd', g * u, wd)
            out = jnp.einsum('txd,tx->td', eo, combine)
            return out.reshape(B, S, E)
        h = x + _attention(_rmsnorm(x, g1), wq, wk, wv, wo)
        y = h + _moe(_rmsnorm(h, g2), w_router, wg, wu, wd)
        return y

    def _L1_xattn_ref(input, memory, Wq, bq, Wk, bk, Wv, bv):
        import jax, jax.numpy as jnp
        import numpy as np
        DIM = 256
        NUM_HEADS = 16
        HEAD_DIM = DIM // NUM_HEADS

        def _split(x):
            b, l, _ = x.shape
            return x.reshape(b, l, NUM_HEADS, HEAD_DIM).transpose(0, 2, 1, 3)
        depth_scale = HEAD_DIM ** (-0.5)
        q = input @ Wq.T + bq
        k = memory @ Wk.T + bk
        v = memory @ Wv.T + bv
        q = _split(q) * depth_scale
        k = _split(k)
        v = _split(v)
        logit = jnp.einsum('bhnd,bhmd->bhnm', q, k)
        attn = jax.nn.softmax(logit, axis=-1)
        out = jnp.einsum('bhnm,bhmd->bhnd', attn, v)
        b, h, n, d = out.shape
        return out.transpose(0, 2, 1, 3).reshape(b, n, h * d)

    def _L1_ffn_ref(x, wg, W, b):
        import jax, jax.numpy as jnp
        import numpy as np
        H = 256
        E = 8
        B, S = (4, 512)
        Bb, Ss, Hh = x.shape
        Ee = wg.shape[1]
        T = Bb * Ss
        C = T // Ee
        xt = x.reshape(T, Hh)
        logits = xt @ wg
        probs = jax.nn.softmax(logits, axis=-1)
        idx = jnp.argmax(probs, axis=-1)
        mask = jax.nn.one_hot(idx, Ee, dtype=xt.dtype)
        locations = jnp.cumsum(mask, axis=0) - mask
        mask = mask * (locations < C).astype(xt.dtype)
        gate = jnp.sum(probs * mask, axis=-1)
        loc_s = jnp.sum(locations * mask, axis=-1).astype(jnp.int32)
        loc_oh = jax.nn.one_hot(loc_s, C, dtype=xt.dtype)
        dispatch = mask[:, :, None] * loc_oh[:, None, :]
        combine = gate[:, None, None] * dispatch
        exp_in = jnp.einsum('tec,th->ech', dispatch, xt)
        exp_out = jnp.einsum('ech,efh->ecf', exp_in, W) + b[:, None, :]
        out = jnp.einsum('tec,ecf->tf', combine, exp_out)
        return out.reshape(Bb, Ss, Hh)
    x = x + jnp.tanh(g_xattn[0]) * _L0_xattn_ref(_layernorm(x, axis=-1), ctx_1024, L0_xattn_cos, L0_xattn_sin, L0_xattn_ln_lat_g, L0_xattn_ln_lat_b, L0_xattn_ln_ctx_g, L0_xattn_ln_ctx_b, L0_xattn_Wq, L0_xattn_Wkv, L0_xattn_Wo, L0_xattn_bo)
    x = x + jnp.tanh(g_ffn[0]) * _L0_ffn_ref(_layernorm(x, axis=-1), L0_ffn_wq, L0_ffn_wk, L0_ffn_wv, L0_ffn_wo, L0_ffn_w_router, L0_ffn_wg, L0_ffn_wu, L0_ffn_wd, L0_ffn_g1, L0_ffn_g2)
    x = x + jnp.tanh(g_xattn[1]) * _L1_xattn_ref(_layernorm(x, axis=-1), ctx_1024, L1_xattn_Wq, L1_xattn_bq, L1_xattn_Wk, L1_xattn_bk, L1_xattn_Wv, L1_xattn_bv)
    x = x + jnp.tanh(g_ffn[1]) * _L1_ffn_ref(_layernorm(x, axis=-1), L1_ffn_wg, L1_ffn_W, L1_ffn_b)
    return x

_drawn_inputs = setup_inputs


def setup_inputs(seed=0):
    import zlib

    import numpy as np

    out = dict(_drawn_inputs(seed))
    spreads = {'g_ffn': (-1.0, 0.6),
     'L0_xattn_ln_lat_g': (1.0, 0.6),
     'L0_xattn_ln_lat_b': (0.0, 0.724),
     'L0_xattn_ln_ctx_g': (1.0, 0.2),
     'L0_xattn_ln_ctx_b': (0.0, 0.1),
     'L0_xattn_bo': (0.0, 0.1),
     'L0_ffn_g1': (1.0, 0.6),
     'L0_ffn_g2': (1.0, 0.6),
     'L1_xattn_bq': (0.0, 0.1),
     'L1_xattn_bk': (0.0, 0.8),
     'L1_xattn_bv': (0.0, 0.1)}
    factors = {'L0_xattn_cos': 6.663,
     'L0_xattn_sin': 7.841,
     'L0_ffn_wq': 8.0,
     'L0_ffn_wk': 8.0,
     'L1_ffn_b': 8.0}
    for name, (base, spread) in spreads.items():
        noise = np.random.default_rng([zlib.crc32(name.encode()), seed]).standard_normal(out[name].shape)
        drawn = base * np.exp(spread * noise) if base else spread * noise
        out[name] = jnp.asarray(drawn.astype(out[name].dtype))
    for name, factor in factors.items():
        out[name] = (out[name] * factor).astype(out[name].dtype)
    return out
```

```python
import concourse.bass as bass
from concourse import mybir
from contextlib import ExitStack

FP32 = mybir.dt.float32
F32R = mybir.dt.float32r
BF16 = mybir.dt.bfloat16
U32 = mybir.dt.uint32
ALU = mybir.AluOpType
ACT = mybir.ActivationFunctionType
AX = mybir.AxisListType

P = 128
BATCH, SEQ, CTX, DIM = 2, 512, 1024, 256
TOK = BATCH * SEQ
CTOK = BATCH * CTX
NT, NCT = TOK // P, CTOK // P
KC = DIM // P
HALF = 512
LAT_HEADS, LAT_D = 16, 64
PAIRS = LAT_HEADS // 2
CLIP = 11.0
GROUPS, GH, HD = 4, 4, 16
HPAD = 32
EXPERTS, HIDDEN = 8, 704
CAPACITY = TOK // EXPERTS
FULL_CHUNKS = HIDDEN // P
REST = HIDDEN - FULL_CHUNKS * P
HCHUNKS = FULL_CHUNKS + 1

C_IDENT, C_SELDEN, C_TRI, C_SELPAIR, C_MASK, C_SUMS, C_IOTA = 0, 128, 256, 384, 512, 516, 580
C_CAUSQ, C_CAUSK, C_COS, C_SIN, C_END = 588, 716, 844, 908, 972


class Core:

    def __init__(self, nc, ctx):
        self.nc, self.sems = nc, []
        self.x = ctx.enter_context(nc.sbuf_tensor("x_rows", [P, NT, DIM], FP32))
        self.const = ctx.enter_context(nc.sbuf_tensor("const", [P, C_END], FP32))
        self.const_bf = ctx.enter_context(nc.sbuf_tensor("const_bf", [P, 4, P], BF16))
        self.par = ctx.enter_context(nc.sbuf_tensor("params", [P, 12], FP32))
        self.gates = ctx.enter_context(nc.sbuf_tensor("gates", [P, 4], FP32))
        self.eps = ctx.enter_context(nc.sbuf_tensor("eps", [P, 2], FP32))
        self.ident = self.const[:, C_IDENT:C_IDENT + P]
        self.ident_bf, self.causq_bf = self.const_bf[:, 0, :], self.const_bf[:, 1, :]
        self.causk_bf, self.ones_bf = self.const_bf[:, 2, :], self.const_bf[:, 3, :]

    def sem(self, name):
        self.sems.append(self.nc.alloc_semaphore(name=name))
        return self.sems[-1]

    def release(self):
        self.nc.clear_and_free_semaphores(self.sems)
        self.nc.all_engine_barrier()
        self.sems = []


def wait(eng, sem, value):
    if not isinstance(value, int) or value > 0:
        eng.wait_ge(sem, value)


def repeat(eng, count, body):
    body(0)
    with eng.Fori(1, count) as i:
        body(i)


def products(nc, out, lhs, rhs, start, stop):
    nc.tensor.matmul(out, lhs[0], rhs[0], start=start, stop=False, skip_group_check=True)
    nc.tensor.matmul(out, lhs[0], rhs[1], start=False, stop=False, skip_group_check=True)
    return nc.tensor.matmul(out, lhs[1], rhs[0], start=False, stop=stop, skip_group_check=True)


def load_stage(nc, core, x, const, par, gates):
    loaded, made, tanhed = core.sem("par_loaded"), core.sem("eps_made"), core.sem("gates_tanh")
    copied = core.sem("const_copied")
    with nc.Block() as block:
        @block.sync
        def _(sp):
            sp.dma_start(core.gates[:, :], gates.partition_broadcast(P)).then_inc(loaded, 16)
            sp.dma_start(core.const[:, :], const).then_inc(loaded, 16)
            sp.dma_start(core.par[:, :], par).then_inc(loaded, 16)
            sp.dma_start(core.x[:, :, :], x.rearrange("(t p) d -> p t d", p=P)).then_inc(loaded, 16)
            sp.wait_ge(loaded, 64)

        @block.gpsimd
        def _(pool):
            nc.gpsimd.memset(core.eps[:, 0:1], 1e-5).then_inc(made, 1)
            nc.gpsimd.memset(core.eps[:, 1:2], 1e-6).then_inc(made, 1)
            nc.gpsimd.memset(core.ones_bf, 1.0).then_inc(made, 1)
            pool.wait_ge(made, 3)

        @block.scalar
        def _(act):
            act.wait_ge(loaded, 64)
            nc.scalar.activation(core.gates[:, :], core.gates[:, :], ACT.Tanh).then_inc(tanhed, 1)
            act.wait_ge(tanhed, 1)

        @block.vector
        def _(dve):
            dve.wait_ge(loaded, 64)
            for dst, c in ((core.ident_bf, C_IDENT), (core.causq_bf, C_CAUSQ), (core.causk_bf, C_CAUSK)):
                nc.vector.tensor_copy(dst, core.const[:, c:c + P]).then_inc(copied, 1)
            dve.wait_ge(copied, 3)


def norm_stage(nc, core, tag, src, n, norms, gain, bias, hi, lo, keep=None, dram=None):
    with ExitStack() as ctx:
        def sb(name, shape, dt=FP32):
            return ctx.enter_context(nc.sbuf_tensor(f"{tag}_{name}", shape, dt))

        if dram is not None:
            src = sb("rows", [P, n, DIM])
        stats, mv = sb("stats", [P, n, 6]), sb("mean_var", [P, n, 2])
        msq, std, rstd = sb("msq", [P, n]), sb("std", [P, n]), sb("rstd", [P, n])
        z = [keep if (keep is not None and k == 0) else sb(f"normed{k}", [P, n, DIM]) for k in range(len(norms))]
        whole = sb("whole", [P, 2, HALF])
        banks = [ctx.enter_context(nc.psum_tensor(f"{tag}_bank{i}", [P, HALF], FP32)) for i in range(2)]
        loaded, stats_done, aggr_done = core.sem(f"{tag}_loaded"), core.sem(f"{tag}_stats"), core.sem(f"{tag}_aggr")
        sq_done, var_ready, std_ready = core.sem(f"{tag}_sq"), core.sem(f"{tag}_var"), core.sem(f"{tag}_std")
        rstd_done, normed, turned = core.sem(f"{tag}_rstd"), core.sem(f"{tag}_normed"), core.sem(f"{tag}_turned")
        evacuated, hi_done, lo_done = core.sem(f"{tag}_evac"), core.sem(f"{tag}_hi"), core.sem(f"{tag}_lo")
        blocks = [(q, c) for q in range(n // 4) for c in range(KC)]
        K = len(norms)
        with nc.Block() as block:
            if dram is not None:
                @block.sync
                def _(sp):
                    sp.dma_start(src[:, :, :], dram.rearrange("(t p) d -> p t d", p=P)).then_inc(loaded, 16)

            @block.vector
            def _(dve):
                if dram is not None:
                    dve.wait_ge(loaded, 16)
                for k, (kind, _eps) in enumerate(norms):
                    rows = src if k == 0 else z[k - 1]
                    if k:
                        dve.wait_ge(normed, k * n)
                    for t in range(n):
                        nc.vector.bn_stats(stats[:, t, :], rows[:, t, :]).then_inc(stats_done, 1)
                    dve.wait_ge(stats_done, (k + 1) * n)
                    for t in range(n):
                        nc.vector.bn_aggr(mv[:, t, :], stats[:, t, :]).then_inc(aggr_done, 1)
                    dve.wait_ge(aggr_done, (k + 1) * n)
                    if kind == "rms":
                        nc.vector.tensor_tensor(msq[:, :], mv[:, :, 0], mv[:, :, 0], ALU.mult).then_inc(sq_done, 1)
                        dve.wait_ge(sq_done, 1)
                        nc.vector.tensor_tensor(msq[:, :], msq[:, :], mv[:, :, 1], ALU.add).then_inc(var_ready, 1)
                    else:
                        nc.vector.tensor_copy(msq[:, :], mv[:, :, 1]).then_inc(var_ready, 1)
                    dve.wait_ge(std_ready, k + 1)
                    nc.vector.reciprocal(rstd[:, :], std[:, :]).then_inc(rstd_done, 1)
                    dve.wait_ge(rstd_done, k + 1)
                    for t in range(n):
                        if kind == "rms":
                            op = nc.vector.tensor_scalar(z[k][:, t, :], rows[:, t, :], rstd[:, t:t + 1], None, ALU.mult)
                        else:
                            op = nc.vector.tensor_scalar(z[k][:, t, :], rows[:, t, :], mv[:, t, 0:1], rstd[:, t:t + 1],
                                                         ALU.subtract, ALU.mult)
                        op.then_inc(normed, 1)
                for j, (q, c) in enumerate(blocks):
                    cols = slice(HALF * q, HALF * (q + 1))
                    dve.wait_ge(evacuated, j + 1)
                    nc.vector.tensor_copy(hi[:, c, cols], whole[:, j % 2, :]).then_inc(hi_done, 1)
                    dve.wait_ge(hi_done, j + 1)
                    nc.vector.tensor_tensor(lo[:, c, cols], whole[:, j % 2, :], hi[:, c, cols].bitcast(FP32),
                                            ALU.subtract).then_inc(lo_done, 1)

            @block.tensor
            def _(pe):
                for j, (q, c) in enumerate(blocks):
                    pe.wait_ge(normed, (K - 1) * n + 4 * (q + 1))
                    if j >= 2:
                        pe.wait_ge(evacuated, j - 1)
                    for i in range(4):
                        last = nc.tensor.transpose(banks[j % 2][:, i * P:(i + 1) * P],
                                                   z[-1][:, 4 * q + i, c * P:(c + 1) * P], core.ident)
                    last.then_inc(turned, 1)

            @block.scalar
            def _(act):
                for k, (_kind, eps) in enumerate(norms):
                    act.wait_ge(var_ready, k + 1)
                    nc.scalar.activation(std[:, :], msq[:, :], ACT.Sqrt, bias=core.eps[:, eps:eps + 1]).then_inc(std_ready, 1)
                for j, (q, c) in enumerate(blocks):
                    act.wait_ge(turned, j + 1)
                    if j >= 2:
                        act.wait_ge(lo_done, j - 1)
                    scale = gain[:, c:c + 1] if gain is not None else 1.0
                    off = bias[:, c:c + 1] if bias is not None else 0.0
                    nc.scalar.activation(whole[:, j % 2, :], banks[j % 2][:, :], ACT.Identity, bias=off,
                                         scale=scale).then_inc(evacuated, 1)


def latent_stage(nc, core, lat, cn, w_dram, rope_dram, attn):
    W = 3 * P
    STEPS = BATCH * (CTX // P)
    KVB = NCT // 2
    E_LO, E_HI = float(2.718281828459045 ** -CLIP), float(2.718281828459045 ** CLIP)
    with ExitStack() as ctx:
        def sb(name, shape, dt=FP32):
            return ctx.enter_context(nc.sbuf_tensor(f"lat_{name}", shape, dt))

        def ps(name, shape):
            return ctx.enter_context(nc.psum_tensor(f"lat_{name}", shape, FP32))

        w_raw = sb("w_raw", [P, KC, W])
        w = [[sb(f"w{k}{s}", [P, KC, W], F32R) for s in ("hi", "lo")] for k in range(2)]
        kt = [[sb(f"kt{k}{s}", [P, CTOK], F32R) for s in ("hi", "lo")] for k in range(2)]
        qt = [[sb(f"qt{k}{s}", [P, TOK], F32R) for s in ("hi", "lo")] for k in range(2)]
        vals = [sb(f"v{k}", [P, NCT, P]) for k in range(2)]
        k_raw = sb("k_raw", [P, 2, 2, P])
        keys = sb("keys", [P, KVB, 2, P])
        rot_a, rot_b = sb("rot_a", [P, 2, P]), sb("rot_b", [P, 2, P])
        rope = sb("rope", [P, CTX // P, 3, 32])
        probs = sb("probs", [P, 4, 2, HALF])
        sums, inv = sb("sums", [32, HALF]), sb("inv", [P, HALF])
        scores = [ps(f"scores{i}", [P, 2, HALF]) for i in range(2)]
        outs, den, proj, turn = ps("outs", [P, HALF]), ps("den", [32, HALF]), ps("proj", [P, HALF]), ps("turn", [P, HALF])
        sum_cols = core.const[:, C_SUMS:C_SUMS + 64].rearrange("p (h m) -> p h m", h=2)
        sel_pair = core.const[0:32, C_SELPAIR:C_SELPAIR + P]

        names = ("w_loaded w_hi w_lo kv_full q_full rot_mul rope_made k_out keys_made v_made turned kt_hi kt_made qt_hi qt_made "
                 "scored exped clipped pv_done raw_done bc_full inv_q bc_done negsin").split()
        s = {n: core.sem(f"lat_{n}") for n in names}

        def pairs(eng, first, pair, end):
            first()
            pair(0, 0)
            with eng.Fori(0, (PAIRS - 2) // 2) as i:
                pair(i * 2 + 1, 1)
                pair(i * 2 + 2, 0)
            pair(PAIRS - 1, 1)
            end()

        with nc.Block() as block:
            @block.sync
            def _(sp):
                sp.dma_start(rope[:, :, 0, :], rope_dram[0]).then_inc(s["rope_made"], 16)
                sp.dma_start(rope[:, :, 2, :], rope_dram[1]).then_inc(s["rope_made"], 16)
                sp.dma_start(w_raw[:, :, :], w_dram[0]).then_inc(s["w_loaded"], 16)
                with sp.Fori(1, PAIRS) as p:
                    sp.wait_ge(s["w_lo"], p)
                    sp.dma_start(w_raw[:, :, :], w_dram[bass.ts(p, 1)].rearrange("a p k n -> p (a k) n")).then_inc(s["w_loaded"], 16)

            @block.gpsimd
            def _(pool):
                def split(p, k):
                    wait(pool, s["w_loaded"], p * 16 + 16)
                    nc.gpsimd.tensor_copy(w[k][0][:, :, :], w_raw[:, :, :]).then_inc(s["w_hi"], 1)
                    pool.wait_ge(s["w_hi"], p + 1)
                    nc.gpsimd.tensor_tensor(w[k][1][:, :, :], w_raw[:, :, :], w[k][0][:, :, :].bitcast(FP32),
                                            ALU.subtract).then_inc(s["w_lo"], 1)

                for p in range(PAIRS):
                    if p >= 2:
                        pool.wait_ge(s["q_full"], (p - 1) * 2)
                    split(p, p % 2)

            @block.tensor
            def _(pe):
                def score(p, k, n):
                    if n == 0:
                        wait(pe, s["kt_made"], p * 4 + 4)
                        wait(pe, s["qt_made"], p * 2 + 2)
                    wait(pe, s["exped"], p * STEPS + (n - 1))
                    b, c = divmod(n, STEPS // 2)
                    for h in range(2):
                        rows, ks = slice(64 * h, 64 * h + 64), slice(b * CTX + c * P, b * CTX + (c + 1) * P)
                        qs = slice(b * SEQ, (b + 1) * SEQ)
                        last = products(nc, scores[n % 2][:, h, :], [x[rows, ks] for x in kt[k]],
                                        [x[rows, qs] for x in qt[k]], True, True)
                    last.then_inc(s["scored"], 1)

                def values(p, k, n):
                    b, c = divmod(n, STEPS // 2)
                    if n == 0:
                        wait(pe, s["v_made"], p * KVB + KVB)
                    if c == 0:
                        wait(pe, s["raw_done"], p * 4 + 2 * b)
                    wait(pe, s["clipped"], p * STEPS + (n + 1))
                    for h in range(2):
                        rows = slice(64 * h, 64 * h + 64)
                        nc.tensor.matmul(outs[rows, :], vals[k][:, b * 8 + c, rows], probs[:, n % 4, h, :],
                                         start=c == 0, stop=c == 7, skip_group_check=True)
                    for h in range(2):
                        last = nc.tensor.matmul(den[:, :], sum_cols[:, h, :], probs[:, n % 4, h, :],
                                                start=c == 0 and h == 0, stop=c == 7 and h == 1, skip_group_check=True)
                    last.then_inc(s["pv_done"], 1)

                def project_kv(p, k, j):
                    if j == 0:
                        pe.wait_ge(s["w_lo"], p + 1)
                        wait(pe, s["qt_made"], p * 2)
                    else:
                        wait(pe, s["v_made"], p * KVB + j)
                    for i in range(2):
                        rows = slice((2 * j + i) * P, (2 * j + i + 1) * P)
                        for c in range(KC):
                            last = products(nc, proj[:, i * 256:(i + 1) * 256], [x[:, c, rows] for x in cn],
                                            [x[:, c, P:3 * P] for x in w[k]], c == 0, c == KC - 1)
                    last.then_inc(s["kv_full"], 1)

                def project_q(p, k, b):
                    if b == 0:
                        wait(pe, s["v_made"], p * KVB + KVB)
                    else:
                        wait(pe, s["qt_made"], p * 2 + 1)
                    for c in range(KC):
                        last = products(nc, proj[:, :], [x[:, c, 0:P] for x in w[k]],
                                        [x[:, c, b * SEQ:(b + 1) * SEQ] for x in lat], c == 0, c == KC - 1)
                    last.then_inc(s["q_full"], 1)

                def turn_keys(p, i):
                    if i:
                        wait(pe, s["kt_made"], p * 4 + i)
                    else:
                        wait(pe, s["bc_done"], p * 2 - 2)
                    wait(pe, s["keys_made"], p * KVB + (2 * i + 2))
                    for j in range(4):
                        last = nc.tensor.transpose(turn[:, j * P:(j + 1) * P], keys[:, 2 * i + j // 2, j % 2, :], core.ident)
                    last.then_inc(s["turned"], 1)

                def spread_sums(p, b):
                    if b:
                        wait(pe, s["bc_done"], p * 2 + 1)
                    elif not isinstance(p, int) or p < PAIRS - 1:
                        wait(pe, s["kt_made"], p * 4 + 8)
                    else:
                        wait(pe, s["bc_done"], p * 2)
                    wait(pe, s["raw_done"], p * 4 + (2 * b + 2))
                    nc.tensor.matmul(turn[:, :], sel_pair, sums[:, :], start=True, stop=True).then_inc(s["bc_full"], 1)

                def first():
                    for j in range(KVB):
                        project_kv(0, 0, j)
                        if j % 2:
                            turn_keys(0, j // 2)
                    for b in range(BATCH):
                        project_q(0, 0, b)
                    score(0, 0, 0)

                def pair(p, k):
                    ahead = not (isinstance(p, int) and p == PAIRS - 1)
                    for n in range(STEPS):
                        if n + 1 < STEPS:
                            score(p, k, n + 1)
                        elif ahead:
                            score(p + 1, 1 - k, 0)
                        if ahead and n < KVB:
                            project_kv(p + 1, 1 - k, n)
                        if n == 1 and not (isinstance(p, int) and p == 0):
                            spread_sums(p - 1, 1)
                        if ahead and 6 <= n < 10:
                            turn_keys(p + 1, n - 6)
                        if ahead and n in (8, 9):
                            project_q(p + 1, 1 - k, n - 8)
                        if n == 10:
                            spread_sums(p, 0)
                        values(p, k, n)

                def end():
                    spread_sums(PAIRS - 1, 1)

                pairs(pe, first, pair, end)

            @block.scalar
            def _(act):
                def exp(p, n):
                    wait(act, s["scored"], p * STEPS + (n + 1))
                    wait(act, s["pv_done"], p * STEPS + (n - 3))
                    nc.scalar.activation(probs[:, n % 4, :, :], scores[n % 2][:, :, :], ACT.Exp,
                                         scale=LAT_D ** -0.5).then_inc(s["exped"], 1)

                def values_out(p, k, j):
                    wait(act, s["kv_full"], p * KVB + (j + 1))
                    wait(act, s["keys_made"], p * KVB + (j - 1))
                    both = proj[:, :].rearrange("p (t n) -> p t n", t=2)
                    nc.scalar.copy(k_raw[:, j % 2, :, :], both[:, :, 0:P]).then_inc(s["k_out"], 1)
                    nc.scalar.copy(vals[k][:, 2 * j:2 * j + 2, :], both[:, :, P:2 * P]).then_inc(s["v_made"], 1)

                def raw_out(p, b):
                    wait(act, s["pv_done"], p * STEPS + 8 * (b + 1))
                    nc.scalar.copy(attn[:, bass.ts(p, 1), b * SEQ:(b + 1) * SEQ], outs[:, :].unsqueeze(1)).then_inc(s["raw_done"], 1)
                    nc.scalar.copy(sums[:, :], den[:, :]).then_inc(s["raw_done"], 1)

                def first():
                    for j in range(KVB):
                        values_out(0, 0, j)

                def pair(p, k):
                    ahead = not (isinstance(p, int) and p == PAIRS - 1)
                    for n in range(STEPS):
                        exp(p, n)
                        if n == 0 and not (isinstance(p, int) and p == 0):
                            raw_out(p - 1, 1)
                        if ahead and n < KVB:
                            values_out(p + 1, 1 - k, n)
                        if n == 8:
                            raw_out(p, 0)

                def end():
                    raw_out(PAIRS - 1, 1)

                pairs(act, first, pair, end)

            @block.vector
            def _(dve):
                def clip(p, n):
                    wait(dve, s["exped"], p * STEPS + (n + 1))
                    nc.vector.tensor_scalar(probs[:, n % 4, :, :], probs[:, n % 4, :, :], E_HI, E_LO,
                                            ALU.min, ALU.max).then_inc(s["clipped"], 1)

                def rotate(p, j):
                    t = (2 * j) % (CTX // P)
                    wait(dve, s["k_out"], p * KVB + (j + 1))
                    ps_k = k_raw[:, j % 2, :, :]
                    wait(dve, s["keys_made"], p * KVB + j)
                    nc.vector.tensor_tensor(rot_a[:, :, :].rearrange("p t (g d) -> p t g d", d=32),
                                            ps_k.rearrange("p t (g d) -> p t g d", d=32),
                                            rope[:, t:t + 2, 0, :].unsqueeze(2).to_broadcast([P, 2, 4, 32]),
                                            ALU.mult).then_inc(s["rot_mul"], 1)
                    for half in range(2):
                        dst = rot_b[:, :, :].rearrange("p t (g a d) -> p t g a d", a=2, d=32)[:, :, :, half, :]
                        src = ps_k.rearrange("p t (g a d) -> p t g a d", a=2, d=32)[:, :, :, 1 - half, :]
                        nc.vector.tensor_tensor(dst, src, rope[:, t:t + 2, 1 + half, :].unsqueeze(2).to_broadcast([P, 2, 2, 32]),
                                                ALU.mult).then_inc(s["rot_mul"], 1)
                    wait(dve, s["rot_mul"], p * (3 * KVB) + 3 * (j + 1))
                    nc.vector.tensor_tensor(keys[:, j, :, :], rot_a[:, :, :], rot_b[:, :, :], ALU.add).then_inc(s["keys_made"], 1)

                def split_keys(p, k, i):
                    cols = slice(i * HALF, (i + 1) * HALF)
                    wait(dve, s["turned"], p * 4 + (i + 1))
                    nc.vector.tensor_copy(kt[k][0][:, cols], turn[:, :]).then_inc(s["kt_hi"], 1)
                    wait(dve, s["kt_hi"], p * 4 + (i + 1))
                    nc.vector.tensor_tensor(kt[k][1][:, cols], turn[:, :], kt[k][0][:, cols].bitcast(FP32),
                                            ALU.subtract).then_inc(s["kt_made"], 1)

                def split_queries(p, k, b):
                    cols = slice(b * SEQ, (b + 1) * SEQ)
                    wait(dve, s["q_full"], p * 2 + (b + 1))
                    nc.vector.tensor_copy(qt[k][0][:, cols], proj[:, :]).then_inc(s["qt_hi"], 1)
                    wait(dve, s["qt_hi"], p * 2 + (b + 1))
                    nc.vector.tensor_tensor(qt[k][1][:, cols], proj[:, :], qt[k][0][:, cols].bitcast(FP32),
                                            ALU.subtract).then_inc(s["qt_made"], 1)

                def normalise(p, b, q):
                    cols = slice(q * P, (q + 1) * P)
                    wait(dve, s["bc_full"], p * 2 + (b + 1))
                    op = nc.vector.reciprocal(inv[:, cols], turn[:, cols]).then_inc(s["inv_q"], 1)
                    wait(dve, s["inv_q"], p * 8 + (4 * b + q + 1))
                    part = attn[:, bass.ts(p, 1), b * SEQ + q * P:b * SEQ + (q + 1) * P]
                    op = nc.vector.tensor_tensor(part, part, inv[:, cols].unsqueeze(1), ALU.mult)
                    if q == 3:
                        op.then_inc(s["bc_done"], 1)

                def first():
                    dve.wait_ge(s["rope_made"], 32)
                    nc.vector.tensor_scalar(rope[:, :, 1, :], rope[:, :, 2, :], -1.0, None, ALU.mult).then_inc(s["negsin"], 1)
                    dve.wait_ge(s["negsin"], 1)
                    for j in range(KVB):
                        rotate(0, j)
                        if j % 2:
                            split_keys(0, 0, j // 2)
                    for b in range(BATCH):
                        split_queries(0, 0, b)

                def pair(p, k):
                    ahead = not (isinstance(p, int) and p == PAIRS - 1)
                    for n in range(STEPS):
                        clip(p, n)
                        if ahead and n < KVB:
                            rotate(p + 1, n)
                        if 1 <= n < 5 and not (isinstance(p, int) and p == 0):
                            normalise(p - 1, 1, n - 1)
                        if ahead and 6 <= n < 10:
                            split_keys(p + 1, 1 - k, n - 6)
                        if ahead and n in (8, 9):
                            split_queries(p + 1, 1 - k, n - 8)
                        if 11 <= n < 15:
                            normalise(p, 0, n - 11)

                def end():
                    for q in range(4):
                        normalise(PAIRS - 1, 1, q)

                pairs(dve, first, pair, end)


def add_projected(nc, core, tag, attn, w_dram, n_chunks, base, out, bias_dram=None, gate=None):
    with ExitStack() as ctx:
        w = ctx.enter_context(nc.sbuf_tensor(f"{tag}_w", [P, n_chunks, DIM], FP32))
        bias = ctx.enter_context(nc.sbuf_tensor(f"{tag}_bias", [P, DIM], FP32))
        tmp = ctx.enter_context(nc.sbuf_tensor(f"{tag}_tmp", [P, NT, DIM], FP32))
        banks = [ctx.enter_context(nc.psum_tensor(f"{tag}_bank{i}", [P, DIM], FP32)) for i in range(2)]
        w_loaded, full, biased, added = (core.sem(f"{tag}_{n}") for n in ("w_loaded", "full", "biased", "added"))
        with nc.Block() as block:
            @block.sync
            def _(sp):
                sp.dma_start(w[:, :, :], w_dram).then_inc(w_loaded, 16)
                if bias_dram is not None:
                    sp.dma_start(bias[:, :], bias_dram.partition_broadcast(P)).then_inc(w_loaded, 16)

            @block.tensor
            def _(pe):
                pe.wait_ge(w_loaded, 32 if bias_dram is not None else 16)
                for t in range(NT):
                    if t >= 2:
                        pe.wait_ge(biased if bias_dram is not None else added, t - 1)
                    for c in range(n_chunks):
                        last = nc.tensor.matmul(banks[t % 2][:, :], attn[:, c, t * P:(t + 1) * P], w[:, c, :],
                                                start=c == 0, stop=c == n_chunks - 1)
                    last.then_inc(full, 1)

            @block.vector
            def _(dve):
                if bias_dram is not None:
                    dve.wait_ge(w_loaded, 32)
                for t in range(NT):
                    dve.wait_ge(full, t + 1)
                    if bias_dram is None:
                        nc.vector.tensor_tensor(out[:, t, :], banks[t % 2][:, :], base[:, t, :], ALU.add).then_inc(added, 1)
                    else:
                        nc.vector.tensor_tensor(tmp[:, t, :], banks[t % 2][:, :], bias[:, :], ALU.add).then_inc(biased, 1)
                        dve.wait_ge(biased, t + 1)
                        nc.vector.scalar_tensor_tensor(out[:, t, :], tmp[:, t, :], gate, base[:, t, :],
                                                       ALU.mult, ALU.add).then_inc(added, 1)
                dve.wait_ge(added, NT)


def small_attention(nc, core, tag, qsrc, ksrc, wq, wkv, causal, attn, rope_tab=None, bias_dram=None):
    kcols = ksrc[0].shape[2]
    nkt = kcols // P
    per_b = nkt // BATCH
    KB = nkt // 4
    QB = NT // 4
    NPROJ = QB + KB
    UNITS = NT * GH
    STEPS = BATCH * per_b * 2
    SCALE = HD ** -0.5
    with ExitStack() as ctx:
        def sb(name, shape, dt=FP32):
            return ctx.enter_context(nc.sbuf_tensor(f"{tag}_{name}", shape, dt))

        def ps(name, shape):
            return ctx.enter_context(nc.psum_tensor(f"{tag}_{name}", shape, FP32))

        qp, kp, vp = sb("qp", [P, NT, GH, HPAD]), sb("kp", [P, nkt, GH, HPAD]), sb("vp", [P, nkt, GH, HPAD])
        kt = [sb(f"kt{x}", [P, kcols], F32R) for x in ("hi", "lo")]
        qm = [sb(f"qm{x}", [P, GH, TOK], F32R) for x in ("hi", "lo")]
        mx = sb("mx", [P, UNITS])
        probs = sb("probs", [P, 4, 2, HALF])
        raw, inv = sb("raw", [P, HALF]), sb("inv", [P, HALF])
        rot_a, rot_b = sb("rot_a", [P, 4, 64]), sb("rot_b", [P, 4, 64])
        bias = sb("bias", [P, 3, DIM])
        slots = [ps(f"scores{i}", [P, 2, HALF]) for i in range(2)]
        outs, spread = ps("outs", [P, HALF]), ps("spread", [P, HALF])
        work = [ps(f"work{i}", [P, HALF]) for i in range(2)]
        sel_den = core.const[:, C_SELDEN:C_SELDEN + P]
        names = ("preset bias_loaded zeroed proj_full proj_out rot_mul turned_k kt_hi kt_made turned_q q_hi "
                 "scored_max max_done neg_done returned_q q_lo scored exped pv_done raw_done spread_full inv_done normed").split()
        s = {n: core.sem(f"{tag}_{n}") for n in names}

        def width(c):
            return c * P if causal else 0

        with nc.Block() as block:
            @block.sync
            def _(sp):
                if bias_dram is not None:
                    sp.dma_start(bias[:, :, :], bias_dram.partition_broadcast(P)).then_inc(s["bias_loaded"], 16)

            @block.gpsimd
            def _(pool):
                for buf in (qp, kp, vp):
                    nc.gpsimd.memset(buf[:, :, :, HD:HPAD], 0.0).then_inc(s["preset"], 1)
                pool.wait_ge(s["preset"], 3)
                for buf in (kp, vp):
                    nc.gpsimd.memset(buf[:, :, :, HD:HD + 1], 1.0).then_inc(s["preset"], 1)

            @block.tensor
            def _(pe):
                pe.wait_ge(s["preset"], 5)
                def group(g):
                    for u in range(NPROJ):
                        if u >= 2:
                            wait(pe, s["proj_out"], g * NPROJ + (u - 1))
                        elif u < 2:
                            wait(pe, s["q_lo"], g * QB)
                        isq = u < QB
                        src, w, n = (qsrc, wq, 64) if isq else (ksrc, wkv, 2 * 64)
                        base = 4 * (u if isq else u - QB)
                        for i in range(4):
                            for c in range(KC):
                                last = products(nc, work[u % 2][:, i * n:(i + 1) * n],
                                                [x[:, c, (base + i) * P:(base + i + 1) * P] for x in src],
                                                [x[:, c, bass.ts(g, n)] for x in w], c == 0, c == KC - 1)
                        last.then_inc(s["proj_full"], 1)
                    for j in range(KB):
                        u = NPROJ + j
                        wait(pe, s["proj_out"], g * NPROJ + NPROJ)
                        if j >= 2:
                            wait(pe, s["kt_made"], g * KB + (j - 1))
                        for i in range(4):
                            last = nc.tensor.transpose(work[u % 2][:, i * P:(i + 1) * P],
                                                       kp[:, 4 * j + i, :, :].rearrange("p h d -> p (h d)"), core.ident)
                        last.then_inc(s["turned_k"], 1)
                    for j in range(QB):
                        u = NPROJ + KB + j
                        wait(pe, s["kt_made"], g * KB + min(KB, KB - 1 + j))
                        if KB - 2 + j + 1 > KB:
                            wait(pe, s["kt_made"], g * KB + KB)
                        for i in range(4):
                            last = nc.tensor.transpose(work[u % 2][:, i * P:(i + 1) * P],
                                                       qp[:, 4 * j + i, :, :].rearrange("p h d -> p (h d)"), core.ident)
                        last.then_inc(s["turned_q"], 1)
                    wait(pe, s["kt_hi"], g * KB + KB)
                    wait(pe, s["q_hi"], g * QB + QB)
                    for m in range(UNITS):
                        t, h = divmod(m, GH)
                        b, tq = divmod(t, NT // BATCH)
                        if m >= 2:
                            wait(pe, s["max_done"], g * UNITS + (m - 1))
                        else:
                            wait(pe, s["exped"], g * STEPS)
                        keys = (tq + 1) * P if causal else per_b * P
                        k0 = b * per_b * P
                        for i, c0 in enumerate(range(0, keys, HALF)):
                            n = min(HALF, keys - c0)
                            last = nc.tensor.matmul(slots[m % 2][:, i, 0:n], qm[0][:, h, t * P:(t + 1) * P],
                                                    kt[0][:, k0 + c0:k0 + c0 + n], start=True, stop=not causal, skip_group_check=True)
                        if causal:
                            last = nc.tensor.matmul(slots[m % 2][:, 0, tq * P:(tq + 1) * P], core.ident_bf, core.causq_bf,
                                                    start=False, stop=True, skip_group_check=True)
                        last.then_inc(s["scored_max"], 1)
                    for j in range(QB):
                        pe.wait_ge(s["neg_done"], g + 1)
                        for i in range(4):
                            last = nc.tensor.transpose(work[j % 2][:, i * P:(i + 1) * P],
                                                       qp[:, 4 * j + i, :, :].rearrange("p h d -> p (h d)"), core.ident)
                        last.then_inc(s["returned_q"], 1)
                    wait(pe, s["q_lo"], g * QB + QB)

                    def score(n):
                        b, r = divmod(n, STEPS // 2)
                        c, hp = divmod(r, 2)
                        if n >= 2:
                            wait(pe, s["exped"], g * STEPS + (n - 1))
                        else:
                            wait(pe, s["max_done"], g * UNITS + UNITS)
                        w0 = width(c)
                        ks = slice((b * per_b + c) * P, (b * per_b + c + 1) * P)
                        for i in range(2):
                            h = 2 * hp + i
                            last = products(nc, slots[n % 2][:, i, w0:HALF], [x[:, ks] for x in kt],
                                            [x[:, h, b * SEQ + w0:(b + 1) * SEQ] for x in qm], True, not causal)
                            if causal:
                                last = nc.tensor.matmul(slots[n % 2][:, i, w0:w0 + P], core.ident_bf, core.causk_bf,
                                                        start=False, stop=True, skip_group_check=True)
                        last.then_inc(s["scored"], 1)

                    def values(n):
                        b, r = divmod(n, STEPS // 2)
                        c, hp = divmod(r, 2)
                        w0 = width(c)
                        if r == 0:
                            wait(pe, s["raw_done"], g * 2 + b)
                        wait(pe, s["exped"], g * STEPS + (n + 1))
                        for i in range(2):
                            h = 2 * hp + i
                            last = nc.tensor.matmul(outs[HPAD * h:HPAD * (h + 1), w0:HALF], vp[:, b * per_b + c, h, :],
                                                    probs[:, n % 4, i, w0:HALF], start=c == 0, stop=c == per_b - 1,
                                                    skip_group_check=True)
                        last.then_inc(s["pv_done"], 1)

                    def spread_sums(b):
                        wait(pe, s["raw_done"], g * 2 + (b + 1))
                        wait(pe, s["inv_done"], g * 2 + b)
                        nc.tensor.matmul(spread[:, :], sel_den, raw[:, :], start=True, stop=True).then_inc(s["spread_full"], 1)

                    score(0)
                    for n in range(STEPS):
                        if n + 1 < STEPS:
                            score(n + 1)
                        values(n)
                        if n == STEPS // 2 + 2:
                            spread_sums(0)
                    spread_sums(1)

                repeat(pe, GROUPS, group)

            @block.scalar
            def _(act):
                def group(g):
                    for j in range(KB):
                        wait(act, s["turned_k"], g * KB + (j + 1))
                        nc.scalar.copy(kt[0][:, j * HALF:(j + 1) * HALF], work[(NPROJ + j) % 2][:, :]).then_inc(s["kt_hi"], 1)
                    for j in range(QB):
                        wait(act, s["turned_q"], g * QB + (j + 1))
                        for h in range(GH):
                            last = nc.scalar.activation(qm[0][:, h, j * HALF:(j + 1) * HALF], work[(NPROJ + KB + j) % 2][:, :],
                                                        ACT.Copy, scale=core.const[:, C_MASK + h:C_MASK + h + 1])
                        last.then_inc(s["q_hi"], 1)
                    for n in range(STEPS):
                        b, r = divmod(n, STEPS // 2)
                        w0 = width(r // 2)
                        wait(act, s["scored"], g * STEPS + (n + 1))
                        if n >= 4:
                            wait(act, s["pv_done"], g * STEPS + (n - 3))
                        else:
                            wait(act, s["pv_done"], g * STEPS)
                        nc.scalar.activation(probs[:, n % 4, :, w0:HALF], slots[n % 2][:, :, w0:HALF], ACT.Exp,
                                             scale=SCALE).then_inc(s["exped"], 1)

                repeat(act, GROUPS, group)

            @block.vector
            def _(dve):
                if bias_dram is not None:
                    dve.wait_ge(s["bias_loaded"], 16)
                dve.wait_ge(s["preset"], 5)
                def group(g):
                    nc.vector.memset(qp[:, :, :, HD:HD + 1], 0.0).then_inc(s["zeroed"], 1)
                    dve.wait_ge(s["zeroed"], g + 1)

                    def take(dst, src, t0, which):
                        d = dst[:, t0:t0 + 4, :, 0:HD]
                        if bias_dram is not None:
                            return nc.vector.tensor_tensor(
                                d, src.rearrange("p t (h d) -> p t h d", d=HD),
                                bias[:, which, bass.ts(g, 64)].rearrange("p (h d) -> p h d", d=HD).unsqueeze(1)
                                .to_broadcast([P, 4, GH, HD]), ALU.add)
                        if which == 2:
                            return nc.vector.tensor_copy(d, src.rearrange("p t (h d) -> p t h d", d=HD))
                        r = take.rotated
                        take.rotated += 1
                        wait(dve, s["rot_mul"], g * 12 + 3 * r)
                        cos, sin = rope_tab
                        nc.vector.tensor_tensor(rot_a[:, :, :].rearrange("p t (h d) -> p t h d", d=HD),
                                                src.rearrange("p t (h d) -> p t h d", d=HD),
                                                cos.unsqueeze(2).to_broadcast([P, 4, GH, HD]), ALU.mult).then_inc(s["rot_mul"], 1)
                        for half in range(2):
                            dd = rot_b[:, :, :].rearrange("p t (h a d) -> p t h a d", a=2, d=HD // 2)[:, :, :, half, :]
                            ss = src.rearrange("p t (h a d) -> p t h a d", a=2, d=HD // 2)[:, :, :, 1 - half, :]
                            nc.vector.tensor_tensor(dd, ss, sin[:, :, half * 8:half * 8 + 8].unsqueeze(2)
                                                    .to_broadcast([P, 4, GH, HD // 2]), ALU.mult).then_inc(s["rot_mul"], 1)
                        wait(dve, s["rot_mul"], g * 12 + 3 * (r + 1))
                        return nc.vector.tensor_tensor(d, rot_a[:, :, :].rearrange("p t (h d) -> p t h d", d=HD),
                                                       rot_b[:, :, :].rearrange("p t (h d) -> p t h d", d=HD), ALU.add)

                    take.rotated = 0
                    for u in range(NPROJ):
                        wait(dve, s["proj_full"], g * NPROJ + (u + 1))
                        if u >= 1:
                            wait(dve, s["proj_out"], g * NPROJ + u)
                        if u < QB:
                            last = take(qp, work[u % 2][:, 0:256].rearrange("p (t n) -> p t n", t=4), 4 * u, 0)
                        else:
                            banks = work[u % 2][:, :].rearrange("p (t n) -> p t n", t=4)
                            take(vp, banks[:, :, 64:128], 4 * (u - QB), 2)
                            last = take(kp, banks[:, :, 0:64], 4 * (u - QB), 1)
                        last.then_inc(s["proj_out"], 1)
                    for j in range(KB):
                        cols = slice(j * HALF, (j + 1) * HALF)
                        wait(dve, s["kt_hi"], g * KB + (j + 1))
                        nc.vector.tensor_tensor(kt[1][:, cols], work[(NPROJ + j) % 2][:, :], kt[0][:, cols].bitcast(FP32),
                                                ALU.subtract).then_inc(s["kt_made"], 1)
                    for m in range(UNITS):
                        t, h = divmod(m, GH)
                        tq = t % (NT // BATCH)
                        wait(dve, s["scored_max"], g * UNITS + (m + 1))
                        src = slots[m % 2][:, 0, 0:(tq + 1) * P] if causal else slots[m % 2][:, :, :]
                        nc.vector.tensor_reduce(mx[:, m:m + 1], src, AX.X if causal else AX.XY, ALU.max).then_inc(s["max_done"], 1)
                    wait(dve, s["max_done"], g * UNITS + UNITS)
                    nc.vector.tensor_scalar(qp[:, :, :, HD:HD + 1].bitcast(F32R), mx[:, :].rearrange("p (t h a) -> p t h a", t=NT, a=1),
                                            -1.0, None, ALU.mult).then_inc(s["neg_done"], 1)
                    for j in range(QB):
                        wait(dve, s["returned_q"], g * QB + (j + 1))
                        for h in range(GH):
                            cols = slice(j * HALF, (j + 1) * HALF)
                            last = nc.vector.scalar_tensor_tensor(qm[1][:, h, cols], work[j % 2][:, :],
                                                                  core.const[:, C_MASK + h:C_MASK + h + 1],
                                                                  qm[0][:, h, cols].bitcast(FP32), ALU.mult, ALU.subtract)
                        last.then_inc(s["q_lo"], 1)
                    for b in range(BATCH):
                        wait(dve, s["pv_done"], g * STEPS + (b + 1) * (STEPS // 2))
                        wait(dve, s["normed"], g * 2 + b)
                        nc.vector.tensor_copy(raw[:, :], outs[:, :]).then_inc(s["raw_done"], 1)
                        wait(dve, s["spread_full"], g * 2 + (b + 1))
                        nc.vector.reciprocal(inv[:, :], spread[:, :]).then_inc(s["inv_done"], 1)
                        wait(dve, s["inv_done"], g * 2 + (b + 1))
                        nc.vector.tensor_tensor(attn[:, bass.ts(g, 1), b * SEQ:(b + 1) * SEQ], raw[:, :].unsqueeze(1),
                                                inv[:, :].unsqueeze(1), ALU.mult).then_inc(s["normed"], 1)

                repeat(dve, GROUPS, group)


def add_heads(nc, core, attn, gate):
    with ExitStack() as ctx:
        banks = [ctx.enter_context(nc.psum_tensor(f"heads_bank{i}", [P, P], FP32)) for i in range(2)]
        turned, added = core.sem("heads_turned"), core.sem("heads_added")
        with nc.Block() as block:
            @block.tensor
            def _(pe):
                for u in range(NT * GROUPS):
                    t, g = divmod(u, GROUPS)
                    if u >= 2:
                        pe.wait_ge(added, u - 1)
                    nc.tensor.transpose(banks[u % 2][:, :], attn[:, g, t * P:(t + 1) * P], core.ident).then_inc(turned, 1)

            @block.vector
            def _(dve):
                for u in range(NT * GROUPS):
                    t, g = divmod(u, GROUPS)
                    dve.wait_ge(turned, u + 1)
                    part = core.x[:, t, g * 64:(g + 1) * 64].rearrange("p (h d) -> p h d", d=HD)
                    nc.vector.scalar_tensor_tensor(part, banks[u % 2][:, :].rearrange("p (h d) -> p h d", d=HPAD)[:, :, 0:HD],
                                                   gate, part, ALU.mult, ALU.add).then_inc(added, 1)
                dve.wait_ge(added, NT * GROUPS)


class Chain:

    def __init__(self, eng, sem):
        self.eng, self.sem, self.n = eng, sem, 0

    def then(self, instruction):
        instruction.then_inc(self.sem, 1)
        self.n += 1
        self.eng.wait_ge(self.sem, self.n)


def router_probs(nc, core, dve, chain, logits_full, e_ready, exp_done, bank, buf, small):
    def wide(v):
        return v.unsqueeze(2).to_broadcast([P, NT, EXPERTS])

    dve.wait_ge(logits_full, 1)
    logits = bank[:, 0:NT * EXPERTS].rearrange("p (t e) -> p t e", e=EXPERTS)
    chain.then(nc.vector.tensor_reduce(small[:, 0, :], logits, AX.X, ALU.max))
    nc.vector.tensor_tensor(buf, logits, wide(small[:, 0, :]), ALU.subtract).then_inc(e_ready, 1)
    dve.wait_ge(exp_done, 1)
    chain.then(nc.vector.tensor_reduce(small[:, 1, :], buf, AX.X, ALU.add))
    chain.then(nc.vector.reciprocal(small[:, 2, :], small[:, 1, :]))
    chain.then(nc.vector.tensor_tensor(buf, buf, wide(small[:, 2, :]), ALU.mult))


def route_stage(nc, core, tokens, w_dram, combine):
    with ExitStack() as ctx:
        def sb(name, shape, dt=FP32):
            return ctx.enter_context(nc.sbuf_tensor(f"route_{name}", shape, dt))

        w = [sb("w_raw", [P, KC, EXPERTS]), sb("w_hi", [P, KC, EXPERTS], F32R), sb("w_lo", [P, KC, EXPERTS], F32R)]
        probs, small = sb("probs", [P, NT, EXPERTS]), sb("small", [P, 5, NT])
        top, where, wheref = sb("top", [P, NT, 8]), sb("where", [P, NT, 8], U32), sb("wheref", [P, NT, 8])
        one = [sb(f"one{i}", [P, NT, EXPERTS]) for i in range(2)]
        bank = ctx.enter_context(nc.psum_tensor("route_bank", [P, HALF], FP32))
        w_loaded, w_split, full, e_ready, exp_done, steps = (core.sem(f"route_{n}") for n in
                                                             ("w_loaded", "w_split", "full", "e_ready", "exp_done", "steps"))
        iota = core.const[:, C_IOTA:C_IOTA + EXPERTS]
        with nc.Block() as block:
            @block.sync
            def _(sp):
                sp.dma_start(w[0][:, :, :], w_dram).then_inc(w_loaded, 16)

            @block.tensor
            def _(pe):
                pe.wait_ge(w_split, 2)
                for t in range(NT):
                    for c in range(KC):
                        last = products(nc, bank[:, t * EXPERTS:(t + 1) * EXPERTS], [x[:, c, t * P:(t + 1) * P] for x in tokens],
                                        [x[:, c, :] for x in w[1:]], c == 0, c == KC - 1)
                last.then_inc(full, 1)

            @block.scalar
            def _(act):
                act.wait_ge(e_ready, 1)
                nc.scalar.activation(probs[:, :, :], probs[:, :, :], ACT.Exp).then_inc(exp_done, 1)

            @block.vector
            def _(dve):
                chain = Chain(dve, steps)
                dve.wait_ge(w_loaded, 16)
                nc.vector.tensor_copy(w[1][:, :, :], w[0][:, :, :]).then_inc(w_split, 1)
                dve.wait_ge(w_split, 1)
                nc.vector.tensor_tensor(w[2][:, :, :], w[0][:, :, :], w[1][:, :, :].bitcast(FP32), ALU.subtract).then_inc(w_split, 1)
                router_probs(nc, core, dve, chain, full, e_ready, exp_done, bank, probs[:, :, :], small)
                for t in range(NT):
                    chain.then(nc.vector.max(top[:, t, :], probs[:, t, :]))
                    chain.then(nc.vector.max_index(where[:, t, :], top[:, t, :], probs[:, t, :]))
                chain.then(nc.vector.tensor_copy(wheref[:, :, :], where[:, :, :]))
                chain.then(nc.vector.tensor_tensor(small[:, 3, :], top[:, :, 0], top[:, :, 1], ALU.add))
                chain.then(nc.vector.reciprocal(small[:, 4, :], small[:, 3, :]))
                chain.then(nc.vector.tensor_tensor(top[:, :, 0:2], top[:, :, 0:2],
                                                   small[:, 4, :].unsqueeze(2).to_broadcast([P, NT, 2]), ALU.mult))
                for i in range(2):
                    chain.then(nc.vector.tensor_tensor(one[i][:, :, :], iota.unsqueeze(1).to_broadcast([P, NT, EXPERTS]),
                                                       wheref[:, :, i:i + 1].to_broadcast([P, NT, EXPERTS]), ALU.is_equal))
                    chain.then(nc.vector.tensor_tensor(one[i][:, :, :], one[i][:, :, :],
                                                       top[:, :, i:i + 1].to_broadcast([P, NT, EXPERTS]), ALU.mult))
                chain.then(nc.vector.tensor_tensor(combine[:, :, :], one[0][:, :, :], one[1][:, :, :], ALU.add))


def experts_stage(nc, core, tokens, combine, h, gu_dram, down_dram):
    GU = 2 * HIDDEN
    with ExitStack() as ctx:
        def sb(name, shape, dt=FP32):
            return ctx.enter_context(nc.sbuf_tensor(f"moe_{name}", shape, dt))

        gu_raw, down_raw = sb("gu_raw", [P, KC, GU]), sb("down_raw", [P, HCHUNKS, DIM])
        gu = [[sb(f"gu{k}{x}", [P, KC, GU], F32R) for x in ("hi", "lo")] for k in range(2)]
        down = [[sb(f"down{k}{x}", [P, HCHUNKS, DIM], F32R) for x in ("hi", "lo")] for k in range(2)]
        silu = sb("silu", [P, 2, HALF])
        whole = sb("whole", [P, 2, HALF])
        hid = [sb(f"hid{x}", [P, HCHUNKS, HALF], F32R) for x in ("hi", "lo")]
        gbank = [ctx.enter_context(nc.psum_tensor(f"moe_g{i}", [P, HALF], FP32)) for i in range(2)]
        ubank = [ctx.enter_context(nc.psum_tensor(f"moe_u{i}", [P, HALF], FP32)) for i in range(2)]
        ybank = [ctx.enter_context(nc.psum_tensor(f"moe_y{i}", [P, DIM], FP32)) for i in range(2)]
        names = "loaded hi lo units silus wholes hid_hi hid_lo y_full y_added".split()
        s = {n: core.sem(f"moe_{n}") for n in names}
        HC = BATCH * HCHUNKS

        def rows_of(c):
            return slice(0, P) if c < FULL_CHUNKS else slice(P - REST, P)

        with nc.Block() as block:
            @block.sync
            def _(sp):
                def load(e):
                    wait(sp, s["lo"], e * 2)
                    sp.dma_start(gu_raw[:, :, :], gu_dram[bass.ts(e, 1)].rearrange("a p k n -> p (a k) n")).then_inc(s["loaded"], 16)
                    sp.dma_start(down_raw[:, :, :], down_dram[bass.ts(e, 1)].rearrange("a p k n -> p (a k) n")).then_inc(s["loaded"], 16)

                repeat(sp, EXPERTS, load)

            @block.gpsimd
            def _(pool):
                def split(e, k, prev):
                    wait(pool, s["loaded"], e * 32 + 32)
                    if prev:
                        wait(pool, s["y_full"], e * NT - NT)
                    nc.gpsimd.tensor_copy(gu[k][0][:, :, :], gu_raw[:, :, :]).then_inc(s["hi"], 1)
                    nc.gpsimd.tensor_copy(down[k][0][:, :, :], down_raw[:, :, :]).then_inc(s["hi"], 1)
                    wait(pool, s["hi"], e * 2 + 2)
                    nc.gpsimd.tensor_tensor(gu[k][1][:, :, :], gu_raw[:, :, :], gu[k][0][:, :, :].bitcast(FP32),
                                            ALU.subtract).then_inc(s["lo"], 1)
                    nc.gpsimd.tensor_tensor(down[k][1][:, :, :], down_raw[:, :, :], down[k][0][:, :, :].bitcast(FP32),
                                            ALU.subtract).then_inc(s["lo"], 1)

                for e in range(EXPERTS):
                    split(e, e % 2, e >= 2)

            @block.tensor
            def _(pe):
                def two_experts(i):
                    for k in range(2):
                        e = i * 2 + k
                        wait(pe, s["lo"], e * 2 + 2)
                        for n in range(BATCH):
                            toks = slice(n * HALF, (n + 1) * HALF)
                            for c in range(HCHUNKS):
                                u = n * HCHUNKS + c
                                if k or u >= 2:
                                    wait(pe, s["wholes"], e * HC + (u - 1))
                                else:
                                    wait(pe, s["wholes"], e * HC)
                                blocks = ([(gbank, c * P), (ubank, FULL_CHUNKS * P + c * P)] if c < FULL_CHUNKS
                                          else [(gbank, 2 * FULL_CHUNKS * P)])
                                for bank, col in blocks:
                                    for kc in range(KC):
                                        last = products(nc, bank[u % 2][:, :], [x[:, kc, col:col + P] for x in gu[k]],
                                                        [x[:, kc, toks] for x in tokens], kc == 0, kc == KC - 1)
                                last.then_inc(s["units"], 1)
                            wait(pe, s["hid_lo"], e * HC + (n + 1) * HCHUNKS)
                            for t in range(4):
                                y = n * 4 + t
                                if k or y >= 2:
                                    wait(pe, s["y_added"], e * NT + (y - 1))
                                else:
                                    wait(pe, s["y_added"], e * NT)
                                for c in range(HCHUNKS):
                                    last = products(nc, ybank[y % 2][:, :], [x[rows_of(c), c, t * P:(t + 1) * P] for x in hid],
                                                    [x[rows_of(c), c, :] for x in down[k]], c == 0, c == HCHUNKS - 1)
                                last.then_inc(s["y_full"], 1)

                repeat(pe, EXPERTS // 2, two_experts)

            @block.scalar
            def _(act):
                def expert(e):
                    for u in range(HC):
                        c = u % HCHUNKS
                        wait(act, s["units"], e * HC + (u + 1))
                        if u >= 2:
                            wait(act, s["wholes"], e * HC + (u - 1))
                        else:
                            wait(act, s["wholes"], e * HC)
                        src = gbank[u % 2][:, :] if c < FULL_CHUNKS else gbank[u % 2][0:REST, :]
                        nc.scalar.activation(silu[rows_of(c), u % 2, :], src, ACT.Silu).then_inc(s["silus"], 1)
                        wait(act, s["wholes"], e * HC + (u + 1))
                        if c == 0 and u:
                            wait(act, s["y_full"], e * NT + 4)
                        elif c == 0:
                            wait(act, s["y_full"], e * NT)
                        nc.scalar.copy(hid[0][rows_of(c), c, :], whole[rows_of(c), u % 2, :]).then_inc(s["hid_hi"], 1)

                repeat(act, EXPERTS, expert)

            @block.vector
            def _(dve):
                def expert(e):
                    for n in range(BATCH):
                        for c in range(HCHUNKS):
                            u = n * HCHUNKS + c
                            rows = rows_of(c)
                            wait(dve, s["silus"], e * HC + (u + 1))
                            if u >= 2:
                                wait(dve, s["hid_lo"], e * HC + (u - 1))
                            else:
                                wait(dve, s["hid_lo"], e * HC)
                            up = (ubank if c < FULL_CHUNKS else gbank)[u % 2][rows, :]
                            nc.vector.tensor_tensor(whole[rows, u % 2, :], up, silu[rows, u % 2, :], ALU.mult).then_inc(s["wholes"], 1)
                            wait(dve, s["hid_hi"], e * HC + (u + 1))
                            nc.vector.tensor_tensor(hid[1][rows, c, :], whole[rows, u % 2, :], hid[0][rows, c, :].bitcast(FP32),
                                                    ALU.subtract).then_inc(s["hid_lo"], 1)
                        for t in range(4):
                            y = n * 4 + t
                            wait(dve, s["y_full"], e * NT + (y + 1))
                            nc.vector.scalar_tensor_tensor(h[:, y, :], ybank[y % 2][:, :], combine[:, y, bass.ts(e, 1)], h[:, y, :],
                                                           ALU.mult, ALU.add).then_inc(s["y_added"], 1)

                repeat(dve, EXPERTS, expert)
                dve.wait_ge(s["y_added"], EXPERTS * NT)


def gated_add(nc, core, tag, h, gate):
    added = core.sem(f"{tag}_added")
    with nc.Block() as block:
        @block.vector
        def _(dve):
            nc.vector.scalar_tensor_tensor(core.x[:, :, :].rearrange("p t d -> p (t d)"), h[:, :, :].rearrange("p t d -> p (t d)"),
                                           gate, core.x[:, :, :].rearrange("p t d -> p (t d)"), ALU.mult, ALU.add).then_inc(added, 1)
            dve.wait_ge(added, 1)


def switch_stage(nc, core, tokens, wr_dram, w_dram, bias_dram, gate, out):
    with ExitStack() as ctx:
        def sb(name, shape, dt=FP32):
            return ctx.enter_context(nc.sbuf_tensor(f"switch_{name}", shape, dt))

        wr = [sb("wr_raw", [P, KC, EXPERTS]), sb("wr_hi", [P, KC, EXPERTS], F32R), sb("wr_lo", [P, KC, EXPERTS], F32R)]
        w = [sb("w_raw", [P, KC, EXPERTS, DIM]), sb("w_hi", [P, KC, EXPERTS, DIM], F32R), sb("w_lo", [P, KC, EXPERTS, DIM], F32R)]
        bias = sb("bias", [EXPERTS, DIM])
        probs, small = sb("probs", [P, NT, EXPERTS]), sb("small", [P, 3, NT])
        top, where, wheref = sb("top", [P, NT, 8]), sb("where", [P, NT, 8], U32), sb("wheref", [P, NT, 8])
        one, one_bf, kept = sb("one", [P, NT, EXPERTS]), sb("one_bf", [P, NT, EXPERTS], BF16), sb("kept", [P, NT, EXPERTS])
        tri_bf = sb("tri", [P, P], BF16)
        weights_t = sb("weights_t", [EXPERTS, TOK])
        y = sb("y", [P, NT, DIM])
        bank = ctx.enter_context(nc.psum_tensor("switch_bank", [P, HALF], FP32))
        locs = ctx.enter_context(nc.psum_tensor("switch_locs", [P, HALF], FP32))
        turn = ctx.enter_context(nc.psum_tensor("switch_turn", [EXPERTS, 2, HALF], FP32))
        acc = [ctx.enter_context(nc.psum_tensor(f"switch_acc{i}", [P, HALF], FP32)) for i in range(4)]
        names = "loaded w_hi w_lo wr_split full e_ready exp_done steps one_ready located weights_ready turned turned_out y_full y_done stored".split()
        s = {n: core.sem(f"switch_{n}") for n in names}
        iota = core.const[:, C_IOTA:C_IOTA + EXPERTS]
        UNITS = 1 + EXPERTS // 2
        with nc.Block() as block:
            @block.sync
            def _(sp):
                sp.dma_start(wr[0][:, :, :], wr_dram).then_inc(s["loaded"], 16)
                sp.dma_start(w[0][:, :, :, :], w_dram).then_inc(s["loaded"], 16)
                sp.dma_start(bias[:, :], bias_dram).then_inc(s["loaded"], 16)
                for t in range(NT):
                    sp.wait_ge(s["y_done"], (t + 1) * (UNITS + 1))
                    sp.dma_start(out[t * P:(t + 1) * P, :], core.x[:, t, :]).then_inc(s["stored"], 16)
                sp.wait_ge(s["stored"], NT * 16)

            @block.gpsimd
            def _(pool):
                pool.wait_ge(s["loaded"], 48)
                nc.gpsimd.tensor_copy(w[1][:, :, :, :], w[0][:, :, :, :]).then_inc(s["w_hi"], 1)
                pool.wait_ge(s["w_hi"], 1)
                nc.gpsimd.tensor_tensor(w[2][:, :, :, :], w[0][:, :, :, :], w[1][:, :, :, :].bitcast(FP32),
                                        ALU.subtract).then_inc(s["w_lo"], 1)

            @block.tensor
            def _(pe):
                pe.wait_ge(s["wr_split"], 3)
                for t in range(NT):
                    for c in range(KC):
                        last = products(nc, bank[:, t * EXPERTS:(t + 1) * EXPERTS], [x[:, c, t * P:(t + 1) * P] for x in tokens],
                                        [x[:, c, :] for x in wr[1:]], c == 0, c == KC - 1)
                last.then_inc(s["full"], 1)
                pe.wait_ge(s["one_ready"], 1)
                for t in range(NT):
                    for e in range(t + 1):
                        last = nc.tensor.matmul(locs[:, t * EXPERTS:(t + 1) * EXPERTS], core.ones_bf if e < t else tri_bf[:, :],
                                                one_bf[:, e, :], start=e == 0, stop=e == t, skip_group_check=True)
                last.then_inc(s["located"], 1)
                pe.wait_ge(s["weights_ready"], 1)
                for t in range(NT):
                    last = nc.tensor.transpose(turn[:, t // 4, (t % 4) * P:(t % 4 + 1) * P], kept[:, t, :], core.ident)
                last.then_inc(s["turned"], 1)
                pe.wait_ge(s["turned_out"], 1)
                pe.wait_ge(s["w_lo"], 1)
                for u in range(NT * UNITS):
                    t, i = divmod(u, UNITS)
                    if u >= 4:
                        pe.wait_ge(s["y_done"], u - 3 + (u - 4) // UNITS)
                    if i == 0:
                        last = nc.tensor.matmul(acc[u % 4][:, 0:DIM], weights_t[:, t * P:(t + 1) * P], bias[:, :], start=True, stop=True)
                    else:
                        for c in range(KC):
                            last = products(nc, acc[u % 4][:, :], [x[:, c, t * P:(t + 1) * P] for x in tokens],
                                            [x[:, c, 2 * i - 2:2 * i, :].rearrange("p e d -> p (e d)") for x in w[1:]], c == 0, c == KC - 1)
                    last.then_inc(s["y_full"], 1)

            @block.scalar
            def _(act):
                act.wait_ge(s["e_ready"], 1)
                nc.scalar.activation(probs[:, :, :], probs[:, :, :], ACT.Exp).then_inc(s["exp_done"], 1)
                act.wait_ge(s["turned"], 1)
                nc.scalar.copy(weights_t[:, :], turn[:, :, :].rearrange("p a n -> p (a n)")).then_inc(s["turned_out"], 1)

            @block.vector
            def _(dve):
                chain = Chain(dve, s["steps"])
                nc.vector.tensor_copy(tri_bf[:, :], core.const[:, C_TRI:C_TRI + P]).then_inc(s["wr_split"], 1)
                dve.wait_ge(s["loaded"], 48)
                nc.vector.tensor_copy(wr[1][:, :, :], wr[0][:, :, :]).then_inc(s["wr_split"], 1)
                dve.wait_ge(s["wr_split"], 2)
                nc.vector.tensor_tensor(wr[2][:, :, :], wr[0][:, :, :], wr[1][:, :, :].bitcast(FP32), ALU.subtract).then_inc(s["wr_split"], 1)
                router_probs(nc, core, dve, chain, s["full"], s["e_ready"], s["exp_done"], bank, probs[:, :, :], small)
                for t in range(NT):
                    chain.then(nc.vector.max(top[:, t, :], probs[:, t, :]))
                    chain.then(nc.vector.max_index(where[:, t, :], top[:, t, :], probs[:, t, :]))
                chain.then(nc.vector.tensor_copy(wheref[:, :, :], where[:, :, :]))
                chain.then(nc.vector.tensor_tensor(one[:, :, :], iota.unsqueeze(1).to_broadcast([P, NT, EXPERTS]),
                                                   wheref[:, :, 0:1].to_broadcast([P, NT, EXPERTS]), ALU.is_equal))
                nc.vector.tensor_copy(one_bf[:, :, :], one[:, :, :]).then_inc(s["one_ready"], 1)
                dve.wait_ge(s["located"], 1)
                chain.then(nc.vector.scalar_tensor_tensor(
                    kept[:, :, :].rearrange("p t e -> p (t e)"), locs[:, 0:NT * EXPERTS], float(CAPACITY),
                    one[:, :, :].rearrange("p t e -> p (t e)"), ALU.is_lt, ALU.mult))
                nc.vector.tensor_tensor(kept[:, :, :], kept[:, :, :], probs[:, :, :], ALU.mult).then_inc(s["weights_ready"], 1)
                dve.wait_ge(s["weights_ready"], 1)
                done = 0
                for u in range(NT * UNITS):
                    t, i = divmod(u, UNITS)
                    dve.wait_ge(s["y_full"], u + 1)
                    if i == 0:
                        nc.vector.tensor_copy(y[:, t, :], acc[u % 4][:, 0:DIM]).then_inc(s["y_done"], 1)
                        done += 1
                        continue
                    dve.wait_ge(s["y_done"], done)
                    e = 2 * i - 2
                    chain.then(nc.vector.scalar_tensor_tensor(y[:, t, :], acc[u % 4][:, 0:DIM], kept[:, t, e:e + 1], y[:, t, :],
                                                              ALU.mult, ALU.add))
                    nc.vector.scalar_tensor_tensor(y[:, t, :], acc[u % 4][:, DIM:2 * DIM], kept[:, t, e + 1:e + 2], y[:, t, :],
                                                   ALU.mult, ALU.add).then_inc(s["y_done"], 1)
                    done += 1
                    if i == UNITS - 1:
                        dve.wait_ge(s["y_done"], done)
                        nc.vector.scalar_tensor_tensor(core.x[:, t, :], y[:, t, :], gate, core.x[:, t, :],
                                                       ALU.mult, ALU.add).then_inc(s["y_done"], 1)
                        done += 1


def split_stage(nc, core, tag, jobs):
    with ExitStack() as ctx:
        raw = [ctx.enter_context(nc.sbuf_tensor(f"{tag}_raw{i}", list(hi.shape), FP32)) for i, (_d, hi, _l) in enumerate(jobs)]
        loaded = [core.sem(f"{tag}_loaded{i}") for i in range(len(jobs))]
        hi_done, lo_done = core.sem(f"{tag}_hi"), core.sem(f"{tag}_lo")
        with nc.Block() as block:
            @block.sync
            def _(sp):
                for i, (dram, _hi, _lo) in enumerate(jobs):
                    sp.dma_start(raw[i][:, :, :], dram).then_inc(loaded[i], 16)

            @block.scalar
            def _(act):
                for i, (_dram, hi, _lo) in enumerate(jobs):
                    act.wait_ge(loaded[i], 16)
                    nc.scalar.copy(hi[:, :, :], raw[i][:, :, :]).then_inc(hi_done, 1)

            @block.vector
            def _(dve):
                for i, (_dram, hi, lo) in enumerate(jobs):
                    dve.wait_ge(hi_done, i + 1)
                    nc.vector.tensor_tensor(lo[:, :, :], raw[i][:, :, :], hi[:, :, :].bitcast(FP32), ALU.subtract).then_inc(lo_done, 1)
                dve.wait_ge(lo_done, len(jobs))


def program(nc, a, out):
    with ExitStack() as ctx:
        core = Core(nc, ctx)
        par, gates = core.par, core.gates
        load_stage(nc, core, a["x"], a["const"], a["par"], a["gates"])

        def pair(stack, name, cols):
            return [stack.enter_context(nc.sbuf_tensor(f"{name}_{x}", [P, KC, cols], F32R)) for x in ("hi", "lo")]

        with ExitStack() as st:
            attn = st.enter_context(nc.sbuf_tensor("lat_attn", [P, PAIRS, TOK], FP32))
            with ExitStack() as src:
                lat, cn = pair(src, "lat", TOK), pair(src, "cn", CTOK)
                norm_stage(nc, core, "nc", None, NCT, [("ln", 0)], par[:, 4:6], par[:, 6:8], *cn, dram=a["ctx"])
                norm_stage(nc, core, "nl", core.x, NT, [("ln", 0), ("ln", 0)], par[:, 0:2], par[:, 2:4], *lat)
                latent_stage(nc, core, lat, cn, a["lat_w"], a["lat_rope"], attn)
            add_projected(nc, core, "lo", attn, a["lat_wo"], PAIRS, core.x, core.x, a["lat_bo"], gates[:, 0:1])
        core.release()
        with ExitStack() as st:
            h = st.enter_context(nc.sbuf_tensor("ffn_h", [P, NT, DIM], FP32))
            attn = st.enter_context(nc.sbuf_tensor("self_attn", [P, GROUPS, TOK], FP32))
            with ExitStack() as src:
                r = pair(src, "r1", TOK)
                norm_stage(nc, core, "n1", core.x, NT, [("ln", 0), ("rms", 1)], par[:, 8:10], None, *r, keep=h)
                wq, wkv = pair(src, "sq", GROUPS * 64), pair(src, "skv", GROUPS * 128)
                split_stage(nc, core, "s1", [(a["self_wq"], *wq), (a["self_wkv"], *wkv)])
                rope = [core.const[:, c:c + 64].rearrange("p (t d) -> p t d", d=HD) for c in (C_COS, C_SIN)]
                small_attention(nc, core, "self", r, r, wq, wkv, True, attn, rope_tab=rope)
            add_projected(nc, core, "so", attn, a["self_wo"], GROUPS, h, h)
            core.release()
            with ExitStack() as src:
                r = pair(src, "r2", TOK)
                combine = src.enter_context(nc.sbuf_tensor("combine", [P, NT, EXPERTS], FP32))
                norm_stage(nc, core, "n2", h, NT, [("rms", 1)], par[:, 10:12], None, *r)
                route_stage(nc, core, r, a["route_w"], combine)
                experts_stage(nc, core, r, combine, h, a["moe_gu"], a["moe_down"])
            gated_add(nc, core, "moe_add", h, gates[:, 2:3])
        core.release()
        with ExitStack() as st:
            attn = st.enter_context(nc.sbuf_tensor("ctx_attn", [P, GROUPS, TOK], FP32))
            r, c = pair(st, "r3", TOK), pair(st, "ctx", CTOK)
            wq, wkv = pair(st, "cq", GROUPS * 64), pair(st, "ckv", GROUPS * 128)
            norm_stage(nc, core, "n3", core.x, NT, [("ln", 0)], None, None, *r)
            split_stage(nc, core, "s3", [(a["ctx_wq"], *wq), (a["ctx_wkv"], *wkv), (a["ctx_t"], *c)])
            small_attention(nc, core, "cross", r, c, wq, wkv, False, attn, bias_dram=a["ctx_bias"])
            add_heads(nc, core, attn, gates[:, 1:2])
        core.release()
        with ExitStack() as st:
            r = pair(st, "r4", TOK)
            norm_stage(nc, core, "n4", core.x, NT, [("ln", 0)], None, None, *r)
            switch_stage(nc, core, r, a["sw_router"], a["sw_w"], a["sw_b"], gates[:, 3:4], out)


def constants():
    import numpy as np
    c = np.zeros((P, C_END), np.float32)
    r = np.arange(P)
    c[:, C_IDENT:C_IDENT + P] = np.eye(P)
    c[:, C_SELDEN:C_SELDEN + P] = r[:, None] == HPAD * (r[None, :] // HPAD) + HD
    c[:, C_TRI:C_TRI + P] = r[:, None] < r[None, :]
    c[0:32, C_SELPAIR:C_SELPAIR + P] = r[0:32, None] == r[None, :] // 64
    c[:, C_MASK:C_MASK + GH] = r[:, None] // HPAD == np.arange(GH)[None, :]
    c[:, C_SUMS:C_SUMS + 64] = np.eye(2, 32).reshape(1, 64)
    c[:, C_IOTA:C_IOTA + EXPERTS] = np.arange(EXPERTS)
    c[:, C_CAUSQ:C_CAUSQ + P] = np.where(r[None, :] > r[:, None], -1e30, 0.0)
    c[:, C_CAUSK:C_CAUSK + P] = np.where(r[:, None] > r[None, :], -1e30, 0.0)
    inv_freq = 1.0 / 10000.0 ** (np.arange(0, HD, 2, dtype=np.float32) / HD)
    freqs = np.einsum("i,j->ij", np.arange(SEQ, dtype=np.float32), inv_freq)
    cos = np.concatenate([np.cos(freqs), np.cos(freqs)], -1).reshape(4, P, HD).transpose(1, 0, 2)
    sin = np.concatenate([-np.sin(freqs), np.sin(freqs)], -1).reshape(4, P, HD).transpose(1, 0, 2)
    c[:, C_COS:C_COS + 64] = cos.reshape(P, 64)
    c[:, C_SIN:C_SIN + 64] = sin.reshape(P, 64)
    return c


def layouts(i):
    import numpy as np

    def chunks(w):
        return np.ascontiguousarray(w.reshape(-1, P, w.shape[-1]).transpose(1, 0, 2))

    a = {k: np.asarray(v) for k, v in i.items()}
    f = {"x": a["x"].reshape(TOK, DIM), "ctx": a["ctx_1024"].reshape(CTOK, DIM), "const": constants()}
    f["ctx_t"] = chunks(f["ctx"].T)
    f["par"] = np.concatenate([a[n].reshape(2, P).T for n in (
        "L0_xattn_ln_lat_g", "L0_xattn_ln_lat_b", "L0_xattn_ln_ctx_g", "L0_xattn_ln_ctx_b", "L0_ffn_g1", "L0_ffn_g2")], 1)
    f["gates"] = np.concatenate([a["g_xattn"], a["g_ffn"]])
    wq, (wk, wv) = a["L0_xattn_Wq"], np.split(a["L0_xattn_Wkv"], 2, axis=1)
    f["lat_w"] = np.stack([np.concatenate([chunks(w[:, p * P:(p + 1) * P]) for w in (wq, wk, wv)], 2) for p in range(PAIRS)])
    f["lat_rope"] = np.stack([a[n].reshape(8, P, 32).transpose(1, 0, 2) for n in ("L0_xattn_cos", "L0_xattn_sin")])
    f["lat_wo"], f["lat_bo"] = chunks(a["L0_xattn_Wo"]), a["L0_xattn_bo"]
    f["self_wq"] = chunks(a["L0_ffn_wq"])

    def interleave(k, v):
        return chunks(np.concatenate([k.reshape(DIM, GROUPS, 64), v.reshape(DIM, GROUPS, 64)], 2).reshape(DIM, 2 * DIM))

    f["self_wkv"] = interleave(a["L0_ffn_wk"], a["L0_ffn_wv"])
    wo = np.zeros((GROUPS, GH, HPAD, DIM), np.float32)
    wo[:, :, 0:HD] = a["L0_ffn_wo"].reshape(GROUPS, GH, HD, DIM)
    f["self_wo"] = chunks(wo.reshape(GROUPS * P, DIM))
    f["route_w"] = chunks(a["L0_ffn_w_router"])
    g, u, d = a["L0_ffn_wg"], a["L0_ffn_wu"], a["L0_ffn_wd"]
    full = FULL_CHUNKS * P
    f["moe_gu"] = np.stack([chunks(np.concatenate([g[e, :, :full], u[e, :, :full], g[e, :, full:], u[e, :, full:]], 1))
                            for e in range(EXPERTS)])
    down = np.zeros((EXPERTS, HCHUNKS, P, DIM), np.float32)
    down[:, :FULL_CHUNKS] = d[:, :full].reshape(EXPERTS, FULL_CHUNKS, P, DIM)
    down[:, FULL_CHUNKS, P - REST:] = d[:, full:]
    f["moe_down"] = down.transpose(0, 2, 1, 3)
    f["ctx_wq"] = chunks(a["L1_xattn_Wq"].T)
    f["ctx_wkv"] = interleave(a["L1_xattn_Wk"].T, a["L1_xattn_Wv"].T)
    f["ctx_bias"] = np.stack([a["L1_xattn_bq"], a["L1_xattn_bk"], a["L1_xattn_bv"]])
    f["sw_router"] = chunks(a["L1_ffn_wg"])
    f["sw_w"] = a["L1_ffn_W"].transpose(2, 0, 1).reshape(2, P, EXPERTS, DIM).transpose(1, 0, 2, 3)
    f["sw_b"] = a["L1_ffn_b"]
    return {k: np.ascontiguousarray(v) for k, v in f.items()}


def kernel(**inputs):
    import numpy as _np
    import concourse.bacc as _bacc
    from concourse import mybir as _mybir
    from concourse.bass_utils import run_bass_kernel_spmd as _run

    nc = _bacc.Bacc("TRN2", target_bir_lowering=False, num_devices=1)
    arrays, args = {}, {}
    for name, a in layouts(inputs).items():
        arrays[f"in_{name}"] = a
        args[name] = nc.dram_tensor(f"in_{name}", a.shape, _mybir.dt.from_np(a.dtype), kind="ExternalInput").ap()
    out = nc.dram_tensor("out_0", (TOK, DIM), _mybir.dt.float32, kind="ExternalOutput").ap()
    program(nc, args, out)
    r = _run(nc, [arrays], core_ids=[0])
    return _np.asarray(r.results[0]["out_0"]).reshape(BATCH, SEQ, DIM)
```

```python
import concourse.bass as bass
from concourse import mybir
from contextlib import ExitStack

FP32 = mybir.dt.float32
F32R = mybir.dt.float32r
BF16 = mybir.dt.bfloat16
U32 = mybir.dt.uint32
ALU = mybir.AluOpType
ACT = mybir.ActivationFunctionType
AX = mybir.AxisListType

P = 128
BATCH, SEQ, CTX, DIM = 2, 512, 1024, 256
TOK = BATCH * SEQ
CTOK = BATCH * CTX
NT, NCT = TOK // P, CTOK // P
KC = DIM // P
HALF = 512
LAT_HEADS, LAT_D = 16, 64
PAIRS = LAT_HEADS // 2
CLIP = 11.0
GROUPS, GH, HD = 4, 4, 16
HPAD = 32
EXPERTS, HIDDEN = 8, 704
CAPACITY = TOK // EXPERTS
FULL_CHUNKS = HIDDEN // P
REST = HIDDEN - FULL_CHUNKS * P
HCHUNKS = FULL_CHUNKS + 1

C_IDENT, C_TRI, C_MASK, C_ONES, C_IOTA = 0, 128, 256, 260, 324
C_CAUSQ, C_CAUSK, C_END = 332, 460, 588


class Core:

    def __init__(self, nc, ctx):
        self.nc, self.sems = nc, []
        self.x = ctx.enter_context(nc.sbuf_tensor("x_rows", [P, NT, DIM], FP32))
        self.const = ctx.enter_context(nc.sbuf_tensor("const", [P, C_END], FP32))
        self.const_bf = ctx.enter_context(nc.sbuf_tensor("const_bf", [P, 4, P], BF16))
        self.par = ctx.enter_context(nc.sbuf_tensor("params", [P, 12], FP32))
        self.gates = ctx.enter_context(nc.sbuf_tensor("gates", [P, 4], FP32))
        self.eps = ctx.enter_context(nc.sbuf_tensor("eps", [P, 2], FP32))
        self.ident = self.const[:, C_IDENT:C_IDENT + P]
        self.ident_bf, self.causq_bf = self.const_bf[:, 0, :], self.const_bf[:, 1, :]
        self.causk_bf, self.ones_bf = self.const_bf[:, 2, :], self.const_bf[:, 3, :]

    def sem(self, name):
        self.sems.append(self.nc.alloc_semaphore(name=name))
        return self.sems[-1]

    def release(self):
        self.nc.clear_and_free_semaphores(self.sems)
        self.nc.all_engine_barrier()
        self.sems = []


def wait(eng, sem, value):
    if not isinstance(value, int) or value > 0:
        eng.wait_ge(sem, value)


def repeat(eng, count, body):
    body(0)
    with eng.Fori(1, count) as i:
        body(i)


def products(nc, out, lhs, rhs, start, stop):
    nc.tensor.matmul(out, lhs[0], rhs[0], start=start, stop=False, skip_group_check=True)
    nc.tensor.matmul(out, lhs[0], rhs[1], start=False, stop=False, skip_group_check=True)
    return nc.tensor.matmul(out, lhs[1], rhs[0], start=False, stop=stop, skip_group_check=True)


def load_stage(nc, core, x, const, par, gates):
    loaded, made, tanhed = core.sem("par_loaded"), core.sem("eps_made"), core.sem("gates_tanh")
    copied = core.sem("const_copied")
    with nc.Block() as block:
        @block.sync
        def _(sp):
            sp.dma_start(core.gates[:, :], gates.partition_broadcast(P)).then_inc(loaded, 16)
            sp.dma_start(core.const[:, :], const).then_inc(loaded, 16)
            sp.dma_start(core.par[:, :], par).then_inc(loaded, 16)
            sp.dma_start(core.x[:, :, :], x.rearrange("(t p) d -> p t d", p=P)).then_inc(loaded, 16)
            sp.wait_ge(loaded, 64)

        @block.gpsimd
        def _(pool):
            nc.gpsimd.memset(core.eps[:, 0:1], 1e-5).then_inc(made, 1)
            nc.gpsimd.memset(core.eps[:, 1:2], 1e-6).then_inc(made, 1)
            nc.gpsimd.memset(core.ones_bf, 1.0).then_inc(made, 1)
            pool.wait_ge(made, 3)

        @block.scalar
        def _(act):
            act.wait_ge(loaded, 64)
            nc.scalar.activation(core.gates[:, :], core.gates[:, :], ACT.Tanh).then_inc(tanhed, 1)
            act.wait_ge(tanhed, 1)

        @block.vector
        def _(dve):
            dve.wait_ge(loaded, 64)
            for dst, c in ((core.ident_bf, C_IDENT), (core.causq_bf, C_CAUSQ), (core.causk_bf, C_CAUSK)):
                nc.vector.tensor_copy(dst, core.const[:, c:c + P]).then_inc(copied, 1)
            dve.wait_ge(copied, 3)


def norm_stage(nc, core, tag, src, n, norms, gain, bias, hi, lo, keep=None, dram=None, pool_work=None):
    with ExitStack() as ctx:
        def sb(name, shape, dt=FP32):
            return ctx.enter_context(nc.sbuf_tensor(f"{tag}_{name}", shape, dt))

        if dram is not None:
            src = sb("rows", [P, n, DIM])
        stats, mv = sb("stats", [P, n, 6]), sb("mean_var", [P, n, 2])
        msq, std, rstd = sb("msq", [P, n]), sb("std", [P, n]), sb("rstd", [P, n])
        z = [keep if (keep is not None and k == 0) else sb(f"normed{k}", [P, n, DIM]) for k in range(len(norms))]
        whole = sb("whole", [P, 2, HALF])
        banks = [ctx.enter_context(nc.psum_tensor(f"{tag}_bank{i}", [P, HALF], FP32)) for i in range(2)]
        loaded, stats_done, aggr_done = core.sem(f"{tag}_loaded"), core.sem(f"{tag}_stats"), core.sem(f"{tag}_aggr")
        sq_done, var_ready, std_ready = core.sem(f"{tag}_sq"), core.sem(f"{tag}_var"), core.sem(f"{tag}_std")
        rstd_done, normed, turned = core.sem(f"{tag}_rstd"), core.sem(f"{tag}_normed"), core.sem(f"{tag}_turned")
        evacuated, hi_done, lo_done = core.sem(f"{tag}_evac"), core.sem(f"{tag}_hi"), core.sem(f"{tag}_lo")
        blocks = [(q, c) for q in range(n // 4) for c in range(KC)]
        K = len(norms)
        with nc.Block() as block:
            if dram is not None:
                @block.sync
                def _(sp):
                    sp.dma_start(src[:, :, :], dram.rearrange("(t p) d -> p t d", p=P)).then_inc(loaded, 16)

            if pool_work is not None:
                block.gpsimd(pool_work)

            @block.vector
            def _(dve):
                if dram is not None:
                    dve.wait_ge(loaded, 16)
                for k, (kind, _eps) in enumerate(norms):
                    rows = src if k == 0 else z[k - 1]
                    if k:
                        dve.wait_ge(normed, k * n)
                    for t in range(n):
                        nc.vector.bn_stats(stats[:, t, :], rows[:, t, :]).then_inc(stats_done, 1)
                    dve.wait_ge(stats_done, (k + 1) * n)
                    for t in range(n):
                        nc.vector.bn_aggr(mv[:, t, :], stats[:, t, :]).then_inc(aggr_done, 1)
                    dve.wait_ge(aggr_done, (k + 1) * n)
                    if kind == "rms":
                        nc.vector.tensor_tensor(msq[:, :], mv[:, :, 0], mv[:, :, 0], ALU.mult).then_inc(sq_done, 1)
                        dve.wait_ge(sq_done, 1)
                        nc.vector.tensor_tensor(msq[:, :], msq[:, :], mv[:, :, 1], ALU.add).then_inc(var_ready, 1)
                    else:
                        nc.vector.tensor_copy(msq[:, :], mv[:, :, 1]).then_inc(var_ready, 1)
                    dve.wait_ge(std_ready, k + 1)
                    nc.vector.reciprocal(rstd[:, :], std[:, :]).then_inc(rstd_done, 1)
                    dve.wait_ge(rstd_done, k + 1)
                    for t in range(n):
                        if kind == "rms":
                            op = nc.vector.tensor_scalar(z[k][:, t, :], rows[:, t, :], rstd[:, t:t + 1], None, ALU.mult)
                        else:
                            op = nc.vector.tensor_scalar(z[k][:, t, :], rows[:, t, :], mv[:, t, 0:1], rstd[:, t:t + 1],
                                                         ALU.subtract, ALU.mult)
                        op.then_inc(normed, 1)
                for j, (q, c) in enumerate(blocks):
                    cols = slice(HALF * q, HALF * (q + 1))
                    dve.wait_ge(evacuated, j + 1)
                    nc.vector.tensor_copy(hi[:, c, cols], whole[:, j % 2, :]).then_inc(hi_done, 1)
                    dve.wait_ge(hi_done, j + 1)
                    nc.vector.tensor_tensor(lo[:, c, cols], whole[:, j % 2, :], hi[:, c, cols].bitcast(FP32),
                                            ALU.subtract).then_inc(lo_done, 1)

            @block.tensor
            def _(pe):
                for j, (q, c) in enumerate(blocks):
                    pe.wait_ge(normed, (K - 1) * n + 4 * (q + 1))
                    if j >= 2:
                        pe.wait_ge(evacuated, j - 1)
                    for i in range(4):
                        last = nc.tensor.transpose(banks[j % 2][:, i * P:(i + 1) * P],
                                                   z[-1][:, 4 * q + i, c * P:(c + 1) * P], core.ident)
                    last.then_inc(turned, 1)

            @block.scalar
            def _(act):
                for k, (_kind, eps) in enumerate(norms):
                    act.wait_ge(var_ready, k + 1)
                    nc.scalar.activation(std[:, :], msq[:, :], ACT.Sqrt, bias=core.eps[:, eps:eps + 1]).then_inc(std_ready, 1)
                for j, (q, c) in enumerate(blocks):
                    act.wait_ge(turned, j + 1)
                    if j >= 2:
                        act.wait_ge(lo_done, j - 1)
                    scale = gain[:, c:c + 1] if gain is not None else 1.0
                    off = bias[:, c:c + 1] if bias is not None else 0.0
                    nc.scalar.activation(whole[:, j % 2, :], banks[j % 2][:, :], ACT.Identity, bias=off,
                                         scale=scale).then_inc(evacuated, 1)


def latent_stage(nc, core, lat, cn, w_dram, rope_dram, attn):
    W = 3 * P
    STEPS = BATCH * (CTX // P)
    KVB = NCT // 2
    E_LO, E_HI = float(2.718281828459045 ** -CLIP), float(2.718281828459045 ** CLIP)
    with ExitStack() as ctx:
        def sb(name, shape, dt=FP32):
            return ctx.enter_context(nc.sbuf_tensor(f"lat_{name}", shape, dt))

        def ps(name, shape):
            return ctx.enter_context(nc.psum_tensor(f"lat_{name}", shape, FP32))

        w_raw = sb("w_raw", [P, KC, W])
        w = [[sb(f"w{k}{s}", [P, KC, W], F32R) for s in ("hi", "lo")] for k in range(2)]
        kt = [[sb(f"kt{k}{s}", [P, CTOK], F32R) for s in ("hi", "lo")] for k in range(2)]
        qt = [[sb(f"qt{k}{s}", [P, TOK], F32R) for s in ("hi", "lo")] for k in range(2)]
        vals = [sb(f"v{k}", [P, NCT, P]) for k in range(2)]
        k_raw = sb("k_raw", [P, 2, 2, P])
        keys = sb("keys", [P, KVB, 2, P])
        rot_a, rot_b = sb("rot_a", [P, 2, P]), sb("rot_b", [P, 2, P])
        rope = sb("rope", [P, CTX // P, 3, 32])
        probs = sb("probs", [P, 4, 2, HALF])
        acc = sb("acc", [P, 2, HALF])
        inv = sb("inv", [P, 2, P])
        scores = [ps(f"scores{i}", [P, 2, HALF]) for i in range(2)]
        outs, proj, turn = ps("outs", [P, HALF]), ps("proj", [P, HALF]), ps("turn", [P, HALF])
        ones = core.const[:, C_ONES:C_ONES + LAT_D]
        SUMS = CTX // P - 1

        names = ("w_loaded w_hi w_lo kv_full q_full rot_mul rope_made k_out keys_made v_made turned kt_hi kt_made qt_hi qt_made "
                 "scored exped clipped summed pv_done raw_done bc_full inv_q bc_done negsin").split()
        s = {n: core.sem(f"lat_{n}") for n in names}

        def freed(n):
            b, c = divmod(n, STEPS // 2)
            return b * SUMS + max(c, 1)

        def pairs(eng, first, pair, end, looped=PAIRS - 2):
            first()
            pair(0, 0)
            with eng.Fori(0, looped // 2) as i:
                pair(i * 2 + 1, 1)
                pair(i * 2 + 2, 0)
            for p in range(looped + 1, PAIRS):
                pair(p, p % 2)
            end()

        with nc.Block() as block:
            @block.sync
            def _(sp):
                sp.dma_start(rope[:, :, 0, :], rope_dram[0]).then_inc(s["rope_made"], 16)
                sp.dma_start(rope[:, :, 2, :], rope_dram[1]).then_inc(s["rope_made"], 16)
                sp.dma_start(w_raw[:, :, :], w_dram[0]).then_inc(s["w_loaded"], 16)
                with sp.Fori(1, PAIRS) as p:
                    sp.wait_ge(s["w_lo"], p)
                    sp.dma_start(w_raw[:, :, :], w_dram[bass.ts(p, 1)].rearrange("a p k n -> p (a k) n")).then_inc(s["w_loaded"], 16)

            @block.gpsimd
            def _(pool):
                def split(p, k):
                    pool.wait_ge(s["w_hi"], p + 1)
                    nc.gpsimd.tensor_tensor(w[k][1][:, :, :], w_raw[:, :, :], w[k][0][:, :, :].bitcast(FP32),
                                            ALU.subtract).then_inc(s["w_lo"], 1)

                def add_up(p, n):
                    b, c = divmod(n, STEPS // 2)
                    if c == 0:
                        return
                    if c == 1:
                        wait(pool, s["bc_full"], p * 2 + b)
                    else:
                        wait(pool, s["summed"], p * (2 * SUMS) + (b * SUMS + c - 1))
                    wait(pool, s["clipped"], p * STEPS + (n + 1))
                    first = probs[:, (n - 1) % 4, :, :] if c == 1 else acc[:, :, :]
                    nc.gpsimd.tensor_tensor(acc[:, :, :], first, probs[:, n % 4, :, :], ALU.add).then_inc(s["summed"], 1)

                def first():
                    split(0, 0)
                    split(1, 1)

                def pair(p, k):
                    for n in range(STEPS):
                        add_up(p, n)
                        if n == 8 and not (isinstance(p, int) and p + 2 >= PAIRS):
                            split(p + 2, k)

                pairs(pool, first, pair, lambda: None, PAIRS - 4)

            @block.tensor
            def _(pe):
                def score(p, k, n):
                    if n == 0:
                        wait(pe, s["kt_made"], p * 4 + 4)
                        wait(pe, s["qt_made"], p * 2 + 2)
                    wait(pe, s["exped"], p * STEPS + (n - 1))
                    b, c = divmod(n, STEPS // 2)
                    for h in range(2):
                        rows, ks = slice(64 * h, 64 * h + 64), slice(b * CTX + c * P, b * CTX + (c + 1) * P)
                        qs = slice(b * SEQ, (b + 1) * SEQ)
                        last = products(nc, scores[n % 2][:, h, :], [x[rows, ks] for x in kt[k]],
                                        [x[rows, qs] for x in qt[k]], True, True)
                    last.then_inc(s["scored"], 1)

                def values(p, k, n):
                    b, c = divmod(n, STEPS // 2)
                    if n == 0:
                        wait(pe, s["v_made"], p * KVB + KVB)
                    if c == 0:
                        wait(pe, s["raw_done"], p * 2 + b)
                    wait(pe, s["clipped"], p * STEPS + (n + 1))
                    for h in range(2):
                        rows = slice(64 * h, 64 * h + 64)
                        last = nc.tensor.matmul(outs[rows, :], vals[k][:, b * 8 + c, rows], probs[:, n % 4, h, :],
                                                start=c == 0, stop=c == 7, skip_group_check=True)
                    last.then_inc(s["pv_done"], 1)

                def project_kv(p, k, j):
                    if j == 0:
                        pe.wait_ge(s["w_lo"], p + 1)
                        wait(pe, s["qt_made"], p * 2)
                    else:
                        wait(pe, s["v_made"], p * KVB + j)
                    for i in range(2):
                        rows = slice((2 * j + i) * P, (2 * j + i + 1) * P)
                        for c in range(KC):
                            last = products(nc, proj[:, i * 256:(i + 1) * 256], [x[:, c, rows] for x in cn],
                                            [x[:, c, P:3 * P] for x in w[k]], c == 0, c == KC - 1)
                    last.then_inc(s["kv_full"], 1)

                def project_q(p, k, b):
                    if b == 0:
                        wait(pe, s["v_made"], p * KVB + KVB)
                    else:
                        wait(pe, s["qt_made"], p * 2 + 1)
                    for c in range(KC):
                        last = products(nc, proj[:, :], [x[:, c, 0:P] for x in w[k]],
                                        [x[:, c, b * SEQ:(b + 1) * SEQ] for x in lat], c == 0, c == KC - 1)
                    last.then_inc(s["q_full"], 1)

                def turn_keys(p, i):
                    if i:
                        wait(pe, s["kt_made"], p * 4 + i)
                    else:
                        wait(pe, s["bc_done"], p * 2 - 2)
                    wait(pe, s["keys_made"], p * KVB + (2 * i + 2))
                    for j in range(4):
                        last = nc.tensor.transpose(turn[:, j * P:(j + 1) * P], keys[:, 2 * i + j // 2, j % 2, :], core.ident)
                    last.then_inc(s["turned"], 1)

                def spread_sums(p, b):
                    if b:
                        wait(pe, s["bc_done"], p * 2 + 1)
                    elif not isinstance(p, int) or p < PAIRS - 1:
                        wait(pe, s["kt_made"], p * 4 + 8)
                    else:
                        wait(pe, s["bc_done"], p * 2)
                    wait(pe, s["summed"], p * (2 * SUMS) + (b + 1) * SUMS)
                    for h in range(2):
                        last = nc.tensor.matmul(turn[64 * h:64 * h + 64, :], ones, acc[:, h, :], start=True, stop=True, skip_group_check=True)
                    last.then_inc(s["bc_full"], 1)

                def first():
                    for j in range(KVB):
                        project_kv(0, 0, j)
                        if j % 2:
                            turn_keys(0, j // 2)
                    for b in range(BATCH):
                        project_q(0, 0, b)
                    score(0, 0, 0)

                def pair(p, k):
                    ahead = not (isinstance(p, int) and p == PAIRS - 1)
                    for n in range(STEPS):
                        if n + 1 < STEPS:
                            score(p, k, n + 1)
                        elif ahead:
                            score(p + 1, 1 - k, 0)
                        if ahead and n < KVB:
                            project_kv(p + 1, 1 - k, n)
                        if n == 1 and not (isinstance(p, int) and p == 0):
                            spread_sums(p - 1, 1)
                        if ahead and 5 <= n < 9:
                            turn_keys(p + 1, n - 5)
                        if ahead and n in (8, 9):
                            project_q(p + 1, 1 - k, n - 8)
                        if n == 9:
                            spread_sums(p, 0)
                        values(p, k, n)

                def end():
                    spread_sums(PAIRS - 1, 1)

                pairs(pe, first, pair, end)

            @block.scalar
            def _(act):
                def weights_hi(p, k):
                    wait(act, s["w_loaded"], p * 16 + 16)
                    wait(act, s["q_full"], p * 2 - 2)
                    nc.scalar.copy(w[k][0][:, :, :], w_raw[:, :, :]).then_inc(s["w_hi"], 1)

                def exp(p, n):
                    wait(act, s["scored"], p * STEPS + (n + 1))
                    wait(act, s["pv_done"], p * STEPS + (n - 3))
                    wait(act, s["summed"], p * (2 * SUMS) + (freed(n - 4) if n >= 4 else freed(n + STEPS - 4) - 2 * SUMS))
                    nc.scalar.activation(probs[:, n % 4, :, :], scores[n % 2][:, :, :], ACT.Exp,
                                         scale=LAT_D ** -0.5).then_inc(s["exped"], 1)

                def values_out(p, k, j):
                    wait(act, s["kv_full"], p * KVB + (j + 1))
                    wait(act, s["keys_made"], p * KVB + (j - 1))
                    both = proj[:, :].rearrange("p (t n) -> p t n", t=2)
                    nc.scalar.copy(k_raw[:, j % 2, :, :], both[:, :, 0:P]).then_inc(s["k_out"], 1)
                    nc.scalar.copy(vals[k][:, 2 * j:2 * j + 2, :], both[:, :, P:2 * P]).then_inc(s["v_made"], 1)

                def raw_out(p, b):
                    wait(act, s["pv_done"], p * STEPS + 8 * (b + 1))
                    nc.scalar.copy(attn[:, bass.ts(p, 1), b * SEQ:(b + 1) * SEQ], outs[:, :].unsqueeze(1)).then_inc(s["raw_done"], 1)

                def first():
                    weights_hi(0, 0)
                    for j in range(KVB):
                        values_out(0, 0, j)
                    weights_hi(1, 1)

                def pair(p, k):
                    ahead = not (isinstance(p, int) and p == PAIRS - 1)
                    for n in range(STEPS):
                        exp(p, n)
                        if n == 0 and not (isinstance(p, int) and p == 0):
                            raw_out(p - 1, 1)
                        if ahead and n < KVB:
                            values_out(p + 1, 1 - k, n)
                        if n == 8:
                            raw_out(p, 0)
                            if not (isinstance(p, int) and p + 2 >= PAIRS):
                                weights_hi(p + 2, k)

                def end():
                    raw_out(PAIRS - 1, 1)

                pairs(act, first, pair, end, PAIRS - 4)

            @block.vector
            def _(dve):
                def clip(p, n):
                    wait(dve, s["exped"], p * STEPS + (n + 1))
                    nc.vector.tensor_scalar(probs[:, n % 4, :, :], probs[:, n % 4, :, :], E_HI, E_LO,
                                            ALU.min, ALU.max).then_inc(s["clipped"], 1)

                def rotate(p, j):
                    t = (2 * j) % (CTX // P)
                    wait(dve, s["k_out"], p * KVB + (j + 1))
                    ps_k = k_raw[:, j % 2, :, :]
                    wait(dve, s["keys_made"], p * KVB + j)
                    nc.vector.tensor_tensor(rot_a[:, :, :].rearrange("p t (g d) -> p t g d", d=32),
                                            ps_k.rearrange("p t (g d) -> p t g d", d=32),
                                            rope[:, t:t + 2, 0, :].unsqueeze(2).to_broadcast([P, 2, 4, 32]),
                                            ALU.mult).then_inc(s["rot_mul"], 1)
                    for half in range(2):
                        dst = rot_b[:, :, :].rearrange("p t (g a d) -> p t g a d", a=2, d=32)[:, :, :, half, :]
                        src = ps_k.rearrange("p t (g a d) -> p t g a d", a=2, d=32)[:, :, :, 1 - half, :]
                        nc.vector.tensor_tensor(dst, src, rope[:, t:t + 2, 1 + half, :].unsqueeze(2).to_broadcast([P, 2, 2, 32]),
                                                ALU.mult).then_inc(s["rot_mul"], 1)
                    wait(dve, s["rot_mul"], p * (3 * KVB) + 3 * (j + 1))
                    nc.vector.tensor_tensor(keys[:, j, :, :], rot_a[:, :, :], rot_b[:, :, :], ALU.add).then_inc(s["keys_made"], 1)

                def split_keys(p, k, i):
                    cols = slice(i * HALF, (i + 1) * HALF)
                    wait(dve, s["turned"], p * 4 + (i + 1))
                    nc.vector.tensor_copy(kt[k][0][:, cols], turn[:, :]).then_inc(s["kt_hi"], 1)
                    wait(dve, s["kt_hi"], p * 4 + (i + 1))
                    nc.vector.tensor_tensor(kt[k][1][:, cols], turn[:, :], kt[k][0][:, cols].bitcast(FP32),
                                            ALU.subtract).then_inc(s["kt_made"], 1)

                def split_queries(p, k, b):
                    cols = slice(b * SEQ, (b + 1) * SEQ)
                    wait(dve, s["q_full"], p * 2 + (b + 1))
                    nc.vector.tensor_copy(qt[k][0][:, cols], proj[:, :]).then_inc(s["qt_hi"], 1)
                    wait(dve, s["qt_hi"], p * 2 + (b + 1))
                    nc.vector.tensor_tensor(qt[k][1][:, cols], proj[:, :], qt[k][0][:, cols].bitcast(FP32),
                                            ALU.subtract).then_inc(s["qt_made"], 1)

                def normalise(p, b, q):
                    cols = slice(q * P, (q + 1) * P)
                    wait(dve, s["bc_full"], p * 2 + (b + 1))
                    if q == 0:
                        wait(dve, s["raw_done"], p * 2 + (b + 1))
                    nc.vector.reciprocal(inv[:, q % 2, :], turn[:, cols]).then_inc(s["inv_q"], 1)
                    wait(dve, s["inv_q"], p * 8 + (4 * b + q + 1))
                    part = attn[:, bass.ts(p, 1), b * SEQ + q * P:b * SEQ + (q + 1) * P]
                    op = nc.vector.tensor_tensor(part, part, inv[:, q % 2, :].unsqueeze(1), ALU.mult)
                    if q == 3:
                        op.then_inc(s["bc_done"], 1)

                def first():
                    dve.wait_ge(s["rope_made"], 32)
                    nc.vector.tensor_scalar(rope[:, :, 1, :], rope[:, :, 2, :], -1.0, None, ALU.mult).then_inc(s["negsin"], 1)
                    dve.wait_ge(s["negsin"], 1)
                    for j in range(KVB):
                        rotate(0, j)
                        if j % 2:
                            split_keys(0, 0, j // 2)
                    for b in range(BATCH):
                        split_queries(0, 0, b)

                def pair(p, k):
                    ahead = not (isinstance(p, int) and p == PAIRS - 1)
                    for n in range(STEPS):
                        clip(p, n)
                        if ahead and n < KVB:
                            rotate(p + 1, n)
                        if 1 <= n < 5 and not (isinstance(p, int) and p == 0):
                            normalise(p - 1, 1, n - 1)
                        if ahead and 5 <= n < 9:
                            split_keys(p + 1, 1 - k, n - 5)
                        if ahead and n in (8, 9):
                            split_queries(p + 1, 1 - k, n - 8)
                        if 10 <= n < 14:
                            normalise(p, 0, n - 10)

                def end():
                    for q in range(4):
                        normalise(PAIRS - 1, 1, q)

                pairs(dve, first, pair, end)


def add_projected(nc, core, tag, attn, w_dram, n_chunks, base, out, bias_dram=None, gate=None):
    with ExitStack() as ctx:
        w = ctx.enter_context(nc.sbuf_tensor(f"{tag}_w", [P, n_chunks, DIM], FP32))
        bias = ctx.enter_context(nc.sbuf_tensor(f"{tag}_bias", [P, DIM], FP32))
        tmp = ctx.enter_context(nc.sbuf_tensor(f"{tag}_tmp", [P, NT, DIM], FP32))
        banks = [ctx.enter_context(nc.psum_tensor(f"{tag}_bank{i}", [P, DIM], FP32)) for i in range(2)]
        w_loaded, full, biased, added = (core.sem(f"{tag}_{n}") for n in ("w_loaded", "full", "biased", "added"))
        with nc.Block() as block:
            @block.sync
            def _(sp):
                sp.dma_start(w[:, :, :], w_dram).then_inc(w_loaded, 16)
                if bias_dram is not None:
                    sp.dma_start(bias[:, :], bias_dram.partition_broadcast(P)).then_inc(w_loaded, 16)

            @block.tensor
            def _(pe):
                pe.wait_ge(w_loaded, 32 if bias_dram is not None else 16)
                for t in range(NT):
                    if t >= 2:
                        pe.wait_ge(biased if bias_dram is not None else added, t - 1)
                    for c in range(n_chunks):
                        last = nc.tensor.matmul(banks[t % 2][:, :], attn[:, c, t * P:(t + 1) * P], w[:, c, :],
                                                start=c == 0, stop=c == n_chunks - 1)
                    last.then_inc(full, 1)

            @block.vector
            def _(dve):
                if bias_dram is not None:
                    dve.wait_ge(w_loaded, 32)
                for t in range(NT):
                    dve.wait_ge(full, t + 1)
                    if bias_dram is None:
                        nc.vector.tensor_tensor(out[:, t, :], banks[t % 2][:, :], base[:, t, :], ALU.add).then_inc(added, 1)
                    else:
                        nc.vector.tensor_tensor(tmp[:, t, :], banks[t % 2][:, :], bias[:, :], ALU.add).then_inc(biased, 1)
                        dve.wait_ge(biased, t + 1)
                        nc.vector.scalar_tensor_tensor(out[:, t, :], tmp[:, t, :], gate, base[:, t, :],
                                                       ALU.mult, ALU.add).then_inc(added, 1)
                dve.wait_ge(added, NT)


def values_stage(nc, core, tag, src, w, n, out, bias=None):
    with ExitStack() as ctx:
        banks = [ctx.enter_context(nc.psum_tensor(f"{tag}_bank{i}", [P, 2, DIM], FP32)) for i in range(2)]
        bias_sb = ctx.enter_context(nc.sbuf_tensor(f"{tag}_bias", [P, DIM], FP32))
        full, copied, bias_loaded = core.sem(f"{tag}_full"), core.sem(f"{tag}_copied"), core.sem(f"{tag}_bias")
        with nc.Block() as block:
            @block.sync
            def _(sp):
                if bias is not None:
                    sp.dma_start(bias_sb[:, :], bias.partition_broadcast(P)).then_inc(bias_loaded, 16)

            @block.tensor
            def _(pe):
                for j in range(n // 2):
                    wait(pe, copied, j - 1)
                    for i in range(2):
                        rows = slice((2 * j + i) * P, (2 * j + i + 1) * P)
                        for c in range(KC):
                            last = products(nc, banks[j % 2][:, i, :], [x[:, c, rows] for x in src],
                                            [x[:, c, :] for x in w], c == 0, c == KC - 1)
                    last.then_inc(full, 1)

            @block.vector
            def _(dve):
                if bias is not None:
                    dve.wait_ge(bias_loaded, 16)
                for j in range(n // 2):
                    dve.wait_ge(full, j + 1)
                    dst = out[:, 2 * j:2 * j + 2, :]
                    if bias is not None:
                        op = nc.vector.tensor_tensor(dst, banks[j % 2][:, :, :], bias_sb[:, :].unsqueeze(1).to_broadcast([P, 2, DIM]), ALU.add)
                    else:
                        op = nc.vector.tensor_copy(dst, banks[j % 2][:, :, :])
                    op.then_inc(copied, 1)
                dve.wait_ge(copied, n // 2)


def small_attention(nc, core, tag, qsrc, ksrc, v_all, w_dram, causal, attn, rope_dram=None, cols_dram=None):
    C = ksrc[0].shape[2] // P // BATCH
    KB = C * P // HALF
    S = 2 * C
    M = (NT // BATCH) * GH
    rotary = rope_dram is not None
    NB = KB + 1
    if rotary:
        PIECES = [(0, 0), (0, P), (1, 2 * P), (1, 3 * P)]
        NW = 4 * P
    else:
        PIECES = [(0, 0)] + [(j + 1, P) for j in range(KB)]
        NW = 2 * P
    NPJ = len(PIECES)
    X = M * KB
    turn_at = S - 4
    piece_at = [2, 4, 5, 6] if causal else [3, 6, 9]
    max_at = [x * turn_at // X for x in range(X)]
    BEFORE_TURN = sum(at <= turn_at for at in piece_at)
    SCALE = HD ** -0.5
    with ExitStack() as ctx:
        def sb(name, shape, dt=FP32):
            return ctx.enter_context(nc.sbuf_tensor(f"{tag}_{name}", shape, dt))

        def ps(name, shape):
            return ctx.enter_context(nc.psum_tensor(f"{tag}_{name}", shape, FP32))

        w_raw = sb("w_raw", [P, KC, NW])
        w = [sb(f"w{x}", [P, KC, NW], F32R) for x in ("hi", "lo")]
        cols = sb("cols", [P, GROUPS, 2])
        group_cols = sb("group_cols", [P, 1, 2])
        rope = sb("rope", [P, 2, HALF])
        rot = sb("rot", [P, 2, HALF])
        whole = sb("whole", [P, BATCH, NB, HALF])
        kt = [[sb(f"kt{k}{x}", [P, C * P], F32R) for x in ("hi", "lo")] for k in range(2)]
        q_hi, q_lo, q_low = sb("q_hi", [P, HALF], F32R), sb("q_lo", [P, HALF]), sb("q_low", [P, HALF])
        qm = [[sb(f"qm{k}{x}", [P, GH, HALF], F32R) for x in ("hi", "lo")] for k in range(2)]
        vals = [sb(f"v{k}", [P, C, GH, HPAD]) for k in range(2)]
        mx, mx_all, neg = sb("mx", [P, M, KB]), sb("mx_all", [P, M]), sb("neg", [P, NT // BATCH, GH, HPAD])
        probs = sb("probs", [P, 4, 2, HALF])
        slots = [ps(f"scores{i}", [P, 2, HALF]) for i in range(2)]
        outs, work = ps("outs", [P, HALF]), ps("work", [P, HALF])
        mbank = ps("maxima", [P, 2, HALF])
        mask = [core.const[:, C_MASK + h:C_MASK + h + 1] for h in range(GH)]
        names = ("preset tables cols_ready w_loaded w_hi w_lo v_staged proj_full proj_out whole_done hi_done lo_done qm_hi max_scored max_done max_all "
                 "neg_done neg_turned low_done qm_lo scored exped pv_done raw_done").split()
        s = {n: core.sem(f"{tag}_{n}") for n in names}

        def width(c):
            return c * P if causal else 0

        class Unit:

            def __init__(self, g, b):
                self.g, self.b = g, b
                self.first, self.last = isinstance(g, int) and (g, b) == (0, 0), isinstance(g, int) and (g, b) == (GROUPS - 1, 1)

            def count(self, per, more=0):
                return self.g * (2 * per) + (self.b * per + more)

            def next(self):
                return Unit(self.g, 1) if self.b == 0 else Unit(self.g + 1, 0)

            def after_next(self):
                return Unit(self.g + 1, self.b)

            def projects(self):
                return not (isinstance(self.g, int) and self.g == GROUPS - 1)

            def before(self):
                return Unit(self.g, 0) if self.b == 1 else Unit(self.g - 1, 1)

        def units(eng, first, unit, end=lambda u: None):
            first(Unit(0, 0))
            for b in range(BATCH):
                unit(Unit(0, b))
            with eng.Fori(1, GROUPS - 1) as g:
                for b in range(BATCH):
                    unit(Unit(g, b))
            for b in range(BATCH):
                unit(Unit(GROUPS - 1, b))
            end(Unit(GROUPS - 1, 1))

        with nc.Block() as block:
            @block.sync
            def _(sp):
                sp.dma_start(w_raw[:, :, :], w_dram[0]).then_inc(s["w_loaded"], 16)
                sp.dma_start(cols[:, :, :], cols_dram).then_inc(s["tables"], 16)
                if rotary:
                    sp.dma_start(rope[:, :, :], rope_dram).then_inc(s["tables"], 16)
                for g in range(1, GROUPS):
                    sp.wait_ge(s["w_lo"], g)
                    sp.dma_start(w_raw[:, :, :], w_dram[g]).then_inc(s["w_loaded"], 16)

            @block.gpsimd
            def _(pool):
                def split_weights(g):
                    wait(pool, s["w_hi"], g + 1)
                    nc.gpsimd.tensor_tensor(w[1][:, :, :], w_raw[:, :, :], w[0][:, :, :].bitcast(FP32), ALU.subtract).then_inc(s["w_lo"], 1)

                def add_rotated(u):
                    for j in range(NB):
                        wait(pool, s["proj_out"], u.count(NPJ, 2 * j + 2))
                        wait(pool, s["lo_done"], u.count(NB, j + 1 - 2 * NB))
                        nc.gpsimd.tensor_tensor(whole[:, u.b, j, :], rot[:, 0, :], rot[:, 1, :], ALU.add).then_inc(s["whole_done"], 1)

                def low_parts(u):
                    for j in range(NB):
                        wait(pool, s["hi_done"], u.count(NB, j + 1))
                        hi = q_hi[:, :] if j == 0 else kt[u.b][0][:, (j - 1) * HALF:j * HALF]
                        lo = q_lo[:, :] if j == 0 else kt[u.b][1][:, (j - 1) * HALF:j * HALF]
                        if j == 0:
                            wait(pool, s["low_done"], u.count(1))
                        nc.gpsimd.tensor_tensor(lo, whole[:, u.b, j, :], hi.bitcast(FP32), ALU.subtract).then_inc(s["lo_done"], 1)

                for buf in (vals[0], vals[1], neg):
                    nc.gpsimd.memset(buf[:, :, :, HD:HPAD], 0.0).then_inc(s["preset"], 1)
                pool.wait_ge(s["preset"], 3)
                for buf in vals:
                    nc.gpsimd.memset(buf[:, :, :, HD:HD + 1], 1.0).then_inc(s["preset"], 1)
                nc.gpsimd.memset(neg[:, :, :, 0:HD], 0.0).then_inc(s["preset"], 1)

                def first(u):
                    split_weights(0)
                    for v in (u, u.next()):
                        if rotary:
                            add_rotated(v)
                        low_parts(v)

                def unit(u):
                    if u.b == 0 and u.projects():
                        split_weights(u.g + 1)
                    if u.projects():
                        if rotary:
                            add_rotated(u.after_next())
                        low_parts(u.after_next())

                units(pool, first, unit)

            @block.tensor
            def _(pe):
                def project(u, i, after_turn=False):
                    j, col = PIECES[i]
                    if i == 0 and u.b == 0:
                        wait(pe, s["w_lo"], u.g + 1)
                    wait(pe, s["low_done"], u.count(1, 0 if after_turn else -1))
                    wait(pe, s["proj_out"], u.count(NPJ, i))
                    src = ksrc if j else qsrc
                    n0 = u.b * C * P + (j - 1) * HALF if j else u.b * SEQ
                    for c in range(KC):
                        last = products(nc, work[:, :], [x[:, c, col:col + P] for x in w],
                                        [x[:, c, n0:n0 + HALF] for x in src], c == 0, c == KC - 1)
                    last.then_inc(s["proj_full"], 1)

                def score_max(u, x):
                    m, j = divmod(x, KB)
                    tq, h = divmod(m, GH)
                    if x == 0:
                        wait(pe, s["qm_hi"], u.count(1, 1))
                        wait(pe, s["hi_done"], u.count(NB, NB))
                    wait(pe, s["max_done"], u.count(X, x - 1))
                    keys = (tq + 1) * P if causal else HALF
                    last = nc.tensor.matmul(mbank[:, x % 2, 0:keys], qm[u.b][0][:, h, tq * P:(tq + 1) * P],
                                            kt[u.b][0][:, j * HALF:j * HALF + keys], start=True, stop=not causal, skip_group_check=True)
                    if causal:
                        last = nc.tensor.matmul(mbank[:, x % 2, tq * P:(tq + 1) * P], core.ident_bf, core.causq_bf,
                                                start=False, stop=True, skip_group_check=True)
                    last.then_inc(s["max_scored"], 1)

                def turn_neg(u, ahead):
                    wait(pe, s["neg_done"], u.count(1, 1))
                    wait(pe, s["proj_out"], u.count(NPJ, NPJ + ahead))
                    for t in range(NT // BATCH):
                        last = nc.tensor.transpose(work[:, t * P:(t + 1) * P], neg[:, t, :, :].rearrange("p h d -> p (h d)"), core.ident)
                    last.then_inc(s["neg_turned"], 1)

                def score(u, n, between=lambda: None):
                    c, hp = divmod(n, 2)
                    if n == 0:
                        wait(pe, s["qm_lo"], u.count(1, 1))
                        wait(pe, s["lo_done"], u.count(NB, NB))
                    wait(pe, s["exped"], u.count(S, n - 1))
                    w0 = width(c)
                    for i in range(2):
                        if i:
                            between()
                        last = products(nc, slots[n % 2][:, i, w0:HALF], [x[:, c * P:(c + 1) * P] for x in kt[u.b]],
                                        [x[:, 2 * hp + i, w0:HALF] for x in qm[u.b]], True, not causal)
                        if causal:
                            last = nc.tensor.matmul(slots[n % 2][:, i, w0:w0 + P], core.ident_bf, core.causk_bf,
                                                    start=False, stop=True, skip_group_check=True)
                    last.then_inc(s["scored"], 1)

                def values(u, c):
                    w0 = width(c)
                    if c == 0:
                        wait(pe, s["v_staged"], u.count(1, 1))
                        wait(pe, s["raw_done"], u.count(1))
                    wait(pe, s["exped"], u.count(S, 2 * c + 2))
                    for h in range(GH):
                        last = nc.tensor.matmul(outs[HPAD * h:HPAD * (h + 1), w0:HALF], vals[u.b][:, c, h, :],
                                                probs[:, (2 * c + h // 2) % 4, h % 2, w0:HALF], start=c == 0, stop=c == C - 1,
                                                skip_group_check=True)
                    last.then_inc(s["pv_done"], 1)

                def first(u):
                    pe.wait_ge(s["preset"], 6)
                    for v in (u, u.next()):
                        for i in range(NPJ):
                            project(v, i)
                    for x in range(X):
                        score_max(u, x)
                    turn_neg(u, NPJ)
                    score(u, 0)

                def unit(u):
                    nxt = None if u.last else u.next()
                    for n in range(S):
                        maxima = [x for x in range(X) if nxt and max_at[x] == n]

                        def some(parts):
                            for _ in range(-(-len(maxima) // parts)):
                                score_max(nxt, maxima.pop(0))

                        if n + 1 < S:
                            score(u, n + 1, lambda: some(4))
                        elif nxt:
                            score(nxt, 0)
                        some(3)
                        if u.projects():
                            for i in range(NPJ):
                                if piece_at[i] == n:
                                    project(u.after_next(), i, piece_at[i] > turn_at)
                        if n == turn_at and nxt:
                            turn_neg(nxt, BEFORE_TURN if u.projects() else 0)
                        some(2)
                        if n % 2:
                            values(u, n // 2)
                        some(1)

                units(pe, first, unit)

            @block.scalar
            def _(act):
                def weights_hi(g):
                    wait(act, s["w_loaded"], g * 16 + 16)
                    wait(act, s["proj_full"], g * (2 * NPJ))
                    nc.scalar.copy(w[0][:, :, :], w_raw[:, :, :]).then_inc(s["w_hi"], 1)
                    if not rotary:
                        nc.scalar.copy(group_cols[:, :, :], cols[:, bass.ts(g, 1), :]).then_inc(s["cols_ready"], 1)

                def piece(u, i):
                    j = PIECES[i][0]
                    wait(act, s["proj_full"], u.count(NPJ, i + 1))
                    wait(act, s["lo_done"], u.count(NB, j + 1 - 2 * NB))
                    if i == 0 and u.b == 0:
                        wait(act, s["cols_ready"], u.g + 1)
                    nc.scalar.activation(whole[:, u.b, j, :], work[:, :], ACT.Identity,
                                         bias=group_cols[:, 0, 0:1] if j else group_cols[:, 0, 1:2]).then_inc(s["proj_out"], 1)

                def high_parts(u):
                    for j in range(NB):
                        if rotary:
                            wait(act, s["whole_done"], u.count(NB, j + 1))
                        else:
                            wait(act, s["proj_out"], u.count(NPJ, j + 1))
                        if j == 0:
                            wait(act, s["qm_hi"], u.count(1))
                            wait(act, s["lo_done"], u.count(NB, 1 - NB))
                        dst = kt[u.b][0][:, (j - 1) * HALF:j * HALF] if j else q_hi[:, :]
                        nc.scalar.copy(dst, whole[:, u.b, j, :]).then_inc(s["hi_done"], 1)

                def stage_values(u):
                    wait(act, s["pv_done"], u.count(C, -C))
                    nc.scalar.copy(vals[u.b][:, :, :, 0:HD],
                                   v_all[:, u.b * C:(u.b + 1) * C, bass.ts(u.g, GH * HD)].rearrange("p t (h d) -> p t h d", d=HD)).then_inc(s["v_staged"], 1)

                def exp(u, n):
                    c = n // 2
                    w0 = width(c)
                    wait(act, s["scored"], u.count(S, n + 1))
                    wait(act, s["pv_done"], u.count(C, c - 1))
                    nc.scalar.activation(probs[:, n % 4, :, w0:HALF], slots[n % 2][:, :, w0:HALF], ACT.Exp,
                                         scale=SCALE).then_inc(s["exped"], 1)

                def raw_out(u):
                    wait(act, s["pv_done"], u.count(C, C))
                    nc.scalar.copy(attn[:, bass.ts(u.g, 1), u.b * SEQ:(u.b + 1) * SEQ], outs[:, :].unsqueeze(1)).then_inc(s["raw_done"], 1)

                def mask_low(u):
                    wait(act, s["low_done"], u.count(1, 1))
                    for h in range(GH):
                        last = nc.scalar.activation(qm[u.b][1][:, h, :], q_low[:, :], ACT.Identity, scale=mask[h])
                    last.then_inc(s["qm_lo"], 1)

                def first(u):
                    act.wait_ge(s["preset"], 6)
                    act.wait_ge(s["tables"], 32 if rotary else 16)
                    weights_hi(0)
                    for v in (u, u.next()):
                        if not rotary:
                            for i in range(NPJ):
                                piece(v, i)
                        high_parts(v)
                    stage_values(u)
                    mask_low(u)

                def unit(u):
                    nxt = None if u.last else u.next()
                    for n in range(S):
                        if n == 0 and not u.first:
                            raw_out(u.before())
                        exp(u, n)
                        if n == 0 and u.b == 0 and u.projects():
                            weights_hi(u.g + 1)
                        if not rotary and u.projects():
                            for i in range(NPJ):
                                if piece_at[i] == n:
                                    piece(u.after_next(), i)
                        if nxt and n == turn_at - 1:
                            stage_values(nxt)
                        if nxt and n == turn_at + 1:
                            mask_low(nxt)
                        if n == S - 1 and u.projects():
                            high_parts(u.after_next())

                units(act, first, unit, raw_out)

            @block.vector
            def _(dve):
                def piece(u, i):
                    j = PIECES[i][0]
                    wait(dve, s["proj_full"], u.count(NPJ, i + 1))
                    if i % 2 == 0:
                        wait(dve, s["whole_done"], u.count(NB, j))
                    add = cols[:, bass.ts(u.g, 1), 0 if j else 1] if i % 2 == 0 else 0.0
                    nc.vector.scalar_tensor_tensor(rot[:, i % 2, :], work[:, :], add, rope[:, i % 2, :], ALU.add, ALU.mult).then_inc(s["proj_out"], 1)

                def mask_queries(u):
                    wait(dve, s["hi_done"], u.count(NB, 1))
                    wait(dve, s["scored"], u.count(S, -S))
                    for h in range(GH):
                        last = nc.vector.tensor_scalar(qm[u.b][0][:, h, :], q_hi[:, :].bitcast(FP32), mask[h], None, ALU.mult)
                    last.then_inc(s["qm_hi"], 1)

                def maximum(u, x):
                    m, j = divmod(x, KB)
                    keys = (m // GH + 1) * P if causal else HALF
                    wait(dve, s["max_scored"], u.count(X, x + 1))
                    nc.vector.tensor_reduce(mx[:, m, j:j + 1], mbank[:, x % 2, 0:keys], AX.X, ALU.max).then_inc(s["max_done"], 1)

                def negate(u):
                    wait(dve, s["max_done"], u.count(X, X))
                    nc.vector.tensor_reduce(mx_all[:, :], mx[:, :, :], AX.X, ALU.max).then_inc(s["max_all"], 1)
                    wait(dve, s["max_all"], u.count(1, 1))
                    wait(dve, s["neg_turned"], u.count(1))
                    nc.vector.tensor_scalar(neg[:, :, :, HD:HD + 1].bitcast(F32R), mx_all[:, :].rearrange("p (t h a) -> p t h a", h=GH, a=1),
                                            -1.0, None, ALU.mult).then_inc(s["neg_done"], 1)

                def add_low(u):
                    wait(dve, s["neg_turned"], u.count(1, 1))
                    wait(dve, s["lo_done"], u.count(NB, 1))
                    wait(dve, s["qm_lo"], u.count(1))
                    nc.vector.tensor_tensor(q_low[:, :], work[:, :], q_lo[:, :], ALU.add).then_inc(s["low_done"], 1)

                def first(u):
                    dve.wait_ge(s["preset"], 6)
                    dve.wait_ge(s["tables"], 32 if rotary else 16)
                    for v in (u, u.next()):
                        if rotary:
                            for i in range(NPJ):
                                piece(v, i)
                        mask_queries(v)
                    for x in range(X):
                        maximum(u, x)
                    negate(u)
                    add_low(u)

                def unit(u):
                    nxt = None if u.last else u.next()
                    for n in range(S):
                        maxima = [x for x in range(X) if nxt and max_at[x] == n]
                        before_piece = -(-len(maxima) // 2)
                        for x in maxima[:before_piece]:
                            maximum(nxt, x)
                        if rotary and u.projects():
                            for i in range(NPJ):
                                if piece_at[i] == n:
                                    piece(u.after_next(), i)
                        for x in maxima[before_piece:]:
                            maximum(nxt, x)
                        if nxt and n == turn_at:
                            negate(nxt)
                            add_low(nxt)
                        if n == S - 1 and u.projects():
                            mask_queries(u.after_next())

                units(dve, first, unit)


def add_heads(nc, core, attn, gate):
    with ExitStack() as ctx:
        banks = [ctx.enter_context(nc.psum_tensor(f"heads_bank{i}", [P, GROUPS * GH, HPAD], FP32)) for i in range(2)]
        inv = ctx.enter_context(nc.sbuf_tensor("heads_inv", [P, NT, GROUPS * GH, 1], FP32))
        normed = ctx.enter_context(nc.sbuf_tensor("heads_normed", [P, NT, GROUPS * GH, HD], FP32))
        turned, inverted, divided, added = (core.sem(f"heads_{n}") for n in ("turned", "inverted", "divided", "added"))
        with nc.Block() as block:
            @block.tensor
            def _(pe):
                for t in range(NT):
                    if t >= 2:
                        pe.wait_ge(divided, t - 1)
                    for g in range(GROUPS):
                        last = nc.tensor.transpose(banks[t % 2][:, g * GH:(g + 1) * GH, :].rearrange("p h d -> p (h d)"),
                                                   attn[:, g, t * P:(t + 1) * P], core.ident)
                    last.then_inc(turned, 1)

            @block.vector
            def _(dve):
                for t in range(NT):
                    dve.wait_ge(turned, t + 1)
                    nc.vector.reciprocal(inv[:, t, :, :], banks[t % 2][:, :, HD:HD + 1]).then_inc(inverted, 1)
                    dve.wait_ge(inverted, t + 1)
                    nc.vector.tensor_tensor(normed[:, t, :, :], banks[t % 2][:, :, 0:HD],
                                            inv[:, t, :, :].to_broadcast([P, GROUPS * GH, HD]), ALU.mult).then_inc(divided, 1)
                    dve.wait_ge(divided, t + 1)
                    nc.vector.scalar_tensor_tensor(core.x[:, t, :], normed[:, t, :, :].rearrange("p h d -> p (h d)"), gate,
                                                   core.x[:, t, :], ALU.mult, ALU.add).then_inc(added, 1)
                dve.wait_ge(added, NT)


def project_heads(nc, core, attn, w_dram, h, experts):
    HEADS = GROUPS * GH
    with ExitStack() as ctx:
        def sb(name, shape, dt=FP32):
            return ctx.enter_context(nc.sbuf_tensor(f"ph_{name}", shape, dt))

        w_raw, w = sb("w_raw", [P, KC, DIM]), [sb(f"w{x}", [P, KC, DIM], F32R) for x in ("hi", "lo")]
        inv, rows = sb("inv", [P, NT, HEADS, 1]), sb("rows", [P, NT, HEADS, HD])
        back = [sb(f"back{x}", [P, NT, KC, P], F32R) for x in ("hi", "lo")]
        turns = [ctx.enter_context(nc.psum_tensor(f"ph_turn{i}", [P, HEADS, HPAD], FP32)) for i in range(2)]
        backs = [ctx.enter_context(nc.psum_tensor(f"ph_back{i}", [P, KC, P], FP32)) for i in range(2)]
        banks = [ctx.enter_context(nc.psum_tensor(f"ph_bank{i}", [P, DIM], FP32)) for i in range(2)]
        w_loaded, w_split, turned, inverted, divided, turned_back, back_hi, back_lo, full, added = (
            core.sem(f"ph_{n}") for n in ("w_loaded", "w_split", "turned", "inverted", "divided", "turned_back",
                                          "back_hi", "back_lo", "full", "added"))
        with nc.Block() as block:
            @block.sync
            def _(sp):
                sp.dma_start(w_raw[:, :, :], w_dram).then_inc(w_loaded, 16)
                experts.load(sp, 0)

            @block.gpsimd
            def _(pool):
                pool.wait_ge(w_loaded, 16)
                nc.gpsimd.tensor_copy(w[0][:, :, :], w_raw[:, :, :]).then_inc(w_split, 1)
                pool.wait_ge(w_split, 1)
                nc.gpsimd.tensor_tensor(w[1][:, :, :], w_raw[:, :, :], w[0][:, :, :].bitcast(FP32), ALU.subtract).then_inc(w_split, 1)
                pool.wait_ge(experts.loaded, 32)
                experts.split_hi(pool, 0)

            @block.tensor
            def _(pe):
                def turn(t):
                    if t >= 2:
                        pe.wait_ge(divided, t - 1)
                    for g in range(GROUPS):
                        last = nc.tensor.transpose(turns[t % 2][:, g * GH:(g + 1) * GH, :].rearrange("p h d -> p (h d)"),
                                                   attn[:, g, t * P:(t + 1) * P], core.ident)
                    last.then_inc(turned, 1)

                def turn_back(t):
                    pe.wait_ge(divided, t + 1)
                    if t >= 2:
                        pe.wait_ge(back_lo, t - 1)
                    for c in range(KC):
                        last = nc.tensor.transpose(backs[t % 2][:, c, :],
                                                   rows[:, t, c * 8:(c + 1) * 8, :].rearrange("p h d -> p (h d)"), core.ident)
                    last.then_inc(turned_back, 1)

                def project(t):
                    pe.wait_ge(back_lo, t + 1)
                    if t == 0:
                        pe.wait_ge(w_split, 2)
                    if t >= 2:
                        pe.wait_ge(added, t - 1)
                    for c in range(KC):
                        last = products(nc, banks[t % 2][:, :], [x[:, t, c, :] for x in back], [x[:, c, :] for x in w],
                                        c == 0, c == KC - 1)
                    last.then_inc(full, 1)

                for t in range(NT + 2):
                    if t < NT:
                        turn(t)
                    if 1 <= t <= NT:
                        turn_back(t - 1)
                    if t >= 2:
                        project(t - 2)

            @block.scalar
            def _(act):
                for t in range(NT):
                    act.wait_ge(turned_back, t + 1)
                    nc.scalar.copy(back[0][:, t, :, :], backs[t % 2][:, :, :]).then_inc(back_hi, 1)

            @block.vector
            def _(dve):
                for t in range(NT + 2):
                    if t < NT:
                        dve.wait_ge(turned, t + 1)
                        nc.vector.reciprocal(inv[:, t, :, :], turns[t % 2][:, :, HD:HD + 1]).then_inc(inverted, 1)
                        dve.wait_ge(inverted, t + 1)
                        nc.vector.tensor_tensor(rows[:, t, :, :], turns[t % 2][:, :, 0:HD],
                                                inv[:, t, :, :].to_broadcast([P, HEADS, HD]), ALU.mult).then_inc(divided, 1)
                    if 1 <= t <= NT:
                        dve.wait_ge(back_hi, t)
                        nc.vector.tensor_tensor(back[1][:, t - 1, :, :], backs[(t - 1) % 2][:, :, :],
                                                back[0][:, t - 1, :, :].bitcast(FP32), ALU.subtract).then_inc(back_lo, 1)
                    if t >= 2:
                        dve.wait_ge(full, t - 1)
                        nc.vector.tensor_tensor(h[:, t - 2, :], banks[t % 2][:, :], h[:, t - 2, :], ALU.add).then_inc(added, 1)
                dve.wait_ge(added, NT)


class Chain:

    def __init__(self, eng, sem):
        self.eng, self.sem, self.n = eng, sem, 0

    def then(self, instruction):
        instruction.then_inc(self.sem, 1)
        self.n += 1
        self.eng.wait_ge(self.sem, self.n)


def router_probs(nc, core, dve, chain, logits_full, e_ready, exp_done, bank, buf, small):
    def wide(v):
        return v.unsqueeze(2).to_broadcast([P, NT, EXPERTS])

    dve.wait_ge(logits_full, 1)
    logits = bank[:, 0:NT * EXPERTS].rearrange("p (t e) -> p t e", e=EXPERTS)
    chain.then(nc.vector.tensor_reduce(small[:, 0, :], logits, AX.X, ALU.max))
    nc.vector.tensor_tensor(buf, logits, wide(small[:, 0, :]), ALU.subtract).then_inc(e_ready, 1)
    dve.wait_ge(exp_done, 1)
    chain.then(nc.vector.tensor_reduce(small[:, 1, :], buf, AX.X, ALU.add))
    chain.then(nc.vector.reciprocal(small[:, 2, :], small[:, 1, :]))
    chain.then(nc.vector.tensor_tensor(buf, buf, wide(small[:, 2, :]), ALU.mult))


def route_stage(nc, core, tokens, w_dram, combine):
    with ExitStack() as ctx:
        def sb(name, shape, dt=FP32):
            return ctx.enter_context(nc.sbuf_tensor(f"route_{name}", shape, dt))

        w = [sb("w_raw", [P, KC, EXPERTS]), sb("w_hi", [P, KC, EXPERTS], F32R), sb("w_lo", [P, KC, EXPERTS], F32R)]
        probs, small = sb("probs", [P, NT, EXPERTS]), sb("small", [P, 5, NT])
        top, where, wheref = sb("top", [P, NT, 8]), sb("where", [P, NT, 8], U32), sb("wheref", [P, NT, 8])
        one = [sb(f"one{i}", [P, NT, EXPERTS]) for i in range(2)]
        bank = ctx.enter_context(nc.psum_tensor("route_bank", [P, HALF], FP32))
        w_loaded, w_split, full, e_ready, exp_done, steps = (core.sem(f"route_{n}") for n in
                                                             ("w_loaded", "w_split", "full", "e_ready", "exp_done", "steps"))
        iota = core.const[:, C_IOTA:C_IOTA + EXPERTS]
        with nc.Block() as block:
            @block.sync
            def _(sp):
                sp.dma_start(w[0][:, :, :], w_dram).then_inc(w_loaded, 16)

            @block.tensor
            def _(pe):
                pe.wait_ge(w_split, 2)
                for t in range(NT):
                    for c in range(KC):
                        last = products(nc, bank[:, t * EXPERTS:(t + 1) * EXPERTS], [x[:, c, t * P:(t + 1) * P] for x in tokens],
                                        [x[:, c, :] for x in w[1:]], c == 0, c == KC - 1)
                last.then_inc(full, 1)

            @block.scalar
            def _(act):
                act.wait_ge(e_ready, 1)
                nc.scalar.activation(probs[:, :, :], probs[:, :, :], ACT.Exp).then_inc(exp_done, 1)

            @block.vector
            def _(dve):
                chain = Chain(dve, steps)
                dve.wait_ge(w_loaded, 16)
                nc.vector.tensor_copy(w[1][:, :, :], w[0][:, :, :]).then_inc(w_split, 1)
                dve.wait_ge(w_split, 1)
                nc.vector.tensor_tensor(w[2][:, :, :], w[0][:, :, :], w[1][:, :, :].bitcast(FP32), ALU.subtract).then_inc(w_split, 1)
                router_probs(nc, core, dve, chain, full, e_ready, exp_done, bank, probs[:, :, :], small)
                for t in range(NT):
                    chain.then(nc.vector.max(top[:, t, :], probs[:, t, :]))
                    chain.then(nc.vector.max_index(where[:, t, :], top[:, t, :], probs[:, t, :]))
                chain.then(nc.vector.tensor_copy(wheref[:, :, :], where[:, :, :]))
                chain.then(nc.vector.tensor_tensor(small[:, 3, :], top[:, :, 0], top[:, :, 1], ALU.add))
                chain.then(nc.vector.reciprocal(small[:, 4, :], small[:, 3, :]))
                chain.then(nc.vector.tensor_tensor(top[:, :, 0:2], top[:, :, 0:2],
                                                   small[:, 4, :].unsqueeze(2).to_broadcast([P, NT, 2]), ALU.mult))
                for i in range(2):
                    chain.then(nc.vector.tensor_tensor(one[i][:, :, :], iota.unsqueeze(1).to_broadcast([P, NT, EXPERTS]),
                                                       wheref[:, :, i:i + 1].to_broadcast([P, NT, EXPERTS]), ALU.is_equal))
                    chain.then(nc.vector.tensor_tensor(one[i][:, :, :], one[i][:, :, :],
                                                       top[:, :, i:i + 1].to_broadcast([P, NT, EXPERTS]), ALU.mult))
                chain.then(nc.vector.tensor_tensor(combine[:, :, :], one[0][:, :, :], one[1][:, :, :], ALU.add))


class Experts:

    def __init__(self, nc, core, stack, gu_dram, down_dram):
        self.nc, self.gu_dram, self.down_dram = nc, gu_dram, down_dram

        def sb(name, shape, dt=FP32):
            return stack.enter_context(nc.sbuf_tensor(f"moe_{name}", shape, dt))

        GU = 2 * HIDDEN
        self.gu_raw, self.down_raw = sb("gu_raw", [P, KC, GU]), sb("down_raw", [P, HCHUNKS, DIM])
        self.gu = [[sb(f"gu{k}{x}", [P, KC, GU], F32R) for x in ("hi", "lo")] for k in range(2)]
        self.down = [[sb(f"down{k}{x}", [P, HCHUNKS, DIM], F32R) for x in ("hi", "lo")] for k in range(2)]
        self.loaded, self.gu_hi, self.down_hi, self.lo = (core.sem(f"moe_{n}") for n in ("loaded", "gu_hi", "down_hi", "w_lo"))

    def load(self, sp, e):
        wait(sp, self.lo, e * 2)
        sp.dma_start(self.gu_raw[:, :, :], self.gu_dram[bass.ts(e, 1)].rearrange("a p k n -> p (a k) n")).then_inc(self.loaded, 16)
        sp.dma_start(self.down_raw[:, :, :], self.down_dram[bass.ts(e, 1)].rearrange("a p k n -> p (a k) n")).then_inc(self.loaded, 16)

    def split_hi(self, pool, e):
        self.nc.gpsimd.tensor_copy(self.gu[e % 2][0][:, :, :], self.gu_raw[:, :, :]).then_inc(self.gu_hi, 1)
        self.nc.gpsimd.tensor_copy(self.down[e % 2][0][:, :, :], self.down_raw[:, :, :]).then_inc(self.down_hi, 1)

    def split_lo(self, pool, e):
        gu, down = self.gu[e % 2], self.down[e % 2]
        pool.wait_ge(self.gu_hi, e + 1)
        self.nc.gpsimd.tensor_tensor(gu[1][:, :, :], self.gu_raw[:, :, :], gu[0][:, :, :].bitcast(FP32), ALU.subtract).then_inc(self.lo, 1)
        pool.wait_ge(self.down_hi, e + 1)
        self.nc.gpsimd.tensor_tensor(down[1][:, :, :], self.down_raw[:, :, :], down[0][:, :, :].bitcast(FP32), ALU.subtract).then_inc(self.lo, 1)


def experts_stage(nc, core, weights, tokens, combine, h):
    with ExitStack() as ctx:
        def sb(name, shape, dt=FP32):
            return ctx.enter_context(nc.sbuf_tensor(f"moe_{name}", shape, dt))

        silu, whole = sb("silu", [P, 2, HALF]), sb("whole", [P, 2, HALF])
        hid = [[sb(f"hid{n}{x}", [P, HCHUNKS, HALF], F32R) for x in ("hi", "lo")] for n in range(BATCH)]
        gbank = [ctx.enter_context(nc.psum_tensor(f"moe_g{i}", [P, HALF], FP32)) for i in range(2)]
        ubank = [ctx.enter_context(nc.psum_tensor(f"moe_u{i}", [P, HALF], FP32)) for i in range(2)]
        ybank = [ctx.enter_context(nc.psum_tensor(f"moe_y{i}", [P, DIM], FP32)) for i in range(2)]
        units, silus, wholes, hid_hi, hid_lo, y_full, y_added = (
            core.sem(f"moe_{n}") for n in ("units", "silus", "wholes", "hid_hi", "hid_lo", "y_full", "y_added"))
        HC = BATCH * HCHUNKS
        TILES = HALF // P
        DOWN_AFTER = 1

        def rows_of(c):
            return slice(0, P) if c < FULL_CHUNKS else slice(P - REST, P)

        def tile_after(c):
            return c - DOWN_AFTER if 0 <= c - DOWN_AFTER < TILES else None

        with nc.Block() as block:
            @block.sync
            def _(sp):
                with sp.Fori(1, EXPERTS) as e:
                    weights.load(sp, e)

            @block.gpsimd
            def _(pool):
                for e in range(1, EXPERTS):
                    pool.wait_ge(weights.loaded, (e + 1) * 32)
                    if e >= 2:
                        pool.wait_ge(units, (e - 1) * HC)
                        pool.wait_ge(y_full, (e - 1) * NT)
                    weights.split_hi(pool, e)
                    weights.split_lo(pool, e)

            @block.tensor
            def _(pe):
                def unit(e, k, u):
                    n, c = divmod(u, HCHUNKS)
                    toks = slice(n * HALF, (n + 1) * HALF)
                    wait(pe, wholes, e * HC + (u - 1))
                    blocks = ([(gbank, c * P), (ubank, FULL_CHUNKS * P + c * P)] if c < FULL_CHUNKS
                              else [(gbank, 2 * FULL_CHUNKS * P)])
                    for bank, col in blocks:
                        for kc in range(KC):
                            last = products(nc, bank[u % 2][:, :], [x[:, kc, col:col + P] for x in weights.gu[k]],
                                            [x[:, kc, toks] for x in tokens], kc == 0, kc == KC - 1)
                    last.then_inc(units, 1)

                def down(e, k, n, t):
                    y = n * TILES + t
                    if t == 0:
                        wait(pe, hid_lo, e * HC + (n + 1) * HCHUNKS)
                    wait(pe, y_added, e * NT + (y - 1))
                    for c in range(HCHUNKS):
                        last = products(nc, ybank[y % 2][:, :], [x[rows_of(c), c, t * P:(t + 1) * P] for x in hid[n]],
                                        [x[rows_of(c), c, :] for x in weights.down[k]], c == 0, c == HCHUNKS - 1)
                    last.then_inc(y_full, 1)

                def expert(e, k):
                    wait(pe, weights.lo, e * 2 + 2)
                    for n in range(BATCH):
                        for c in range(HCHUNKS):
                            unit(e, k, n * HCHUNKS + c)
                            t = tile_after(c)
                            if t is not None and n:
                                down(e, k, 0, t)
                            elif t is not None and not (isinstance(e, int) and e == 0):
                                down(e - 1, 1 - k, 1, t)

                def two_experts(i):
                    for k in range(2):
                        expert(i * 2 + k, k)

                repeat(pe, EXPERTS // 2, two_experts)
                for t in range(TILES):
                    down(EXPERTS - 1, 1, 1, t)

            @block.scalar
            def _(act):
                def expert(e):
                    for u in range(HC):
                        n, c = divmod(u, HCHUNKS)
                        wait(act, units, e * HC + (u + 1))
                        wait(act, wholes, e * HC + (u - 1))
                        src = gbank[u % 2][:, :] if c < FULL_CHUNKS else gbank[u % 2][0:REST, :]
                        nc.scalar.activation(silu[rows_of(c), u % 2, :], src, ACT.Silu).then_inc(silus, 1)
                        wait(act, wholes, e * HC + (u + 1))
                        if c == 0:
                            wait(act, y_full, e * NT + (n - 1) * TILES)
                        nc.scalar.copy(hid[n][0][rows_of(c), c, :], whole[rows_of(c), u % 2, :]).then_inc(hid_hi, 1)

                repeat(act, EXPERTS, expert)

            @block.vector
            def _(dve):
                def add(e, n, t):
                    y = n * TILES + t
                    wait(dve, y_full, e * NT + (y + 1))
                    nc.vector.scalar_tensor_tensor(h[:, y, :], ybank[y % 2][:, :], combine[:, y, bass.ts(e, 1)], h[:, y, :],
                                                   ALU.mult, ALU.add).then_inc(y_added, 1)

                def expert(e):
                    for u in range(HC):
                        n, c = divmod(u, HCHUNKS)
                        rows = rows_of(c)
                        wait(dve, silus, e * HC + (u + 1))
                        wait(dve, hid_lo, e * HC + (u - 1))
                        up = (ubank if c < FULL_CHUNKS else gbank)[u % 2][rows, :]
                        nc.vector.tensor_tensor(whole[rows, u % 2, :], up, silu[rows, u % 2, :], ALU.mult).then_inc(wholes, 1)
                        wait(dve, hid_hi, e * HC + (u + 1))
                        nc.vector.tensor_tensor(hid[n][1][rows, c, :], whole[rows, u % 2, :], hid[n][0][rows, c, :].bitcast(FP32),
                                                ALU.subtract).then_inc(hid_lo, 1)
                        t = tile_after(c)
                        if t is not None and n:
                            add(e, 0, t)
                        elif t is not None and not (isinstance(e, int) and e == 0):
                            add(e - 1, 1, t)

                repeat(dve, EXPERTS, expert)
                for t in range(TILES):
                    add(EXPERTS - 1, 1, t)
                dve.wait_ge(y_added, EXPERTS * NT)


def gated_add(nc, core, tag, h, gate):
    added = core.sem(f"{tag}_added")
    with nc.Block() as block:
        @block.vector
        def _(dve):
            nc.vector.scalar_tensor_tensor(core.x[:, :, :].rearrange("p t d -> p (t d)"), h[:, :, :].rearrange("p t d -> p (t d)"),
                                           gate, core.x[:, :, :].rearrange("p t d -> p (t d)"), ALU.mult, ALU.add).then_inc(added, 1)
            dve.wait_ge(added, 1)


def switch_stage(nc, core, tokens, wr_dram, w_dram, bias_dram, gate, out):
    with ExitStack() as ctx:
        def sb(name, shape, dt=FP32):
            return ctx.enter_context(nc.sbuf_tensor(f"switch_{name}", shape, dt))

        wr = [sb("wr_raw", [P, KC, EXPERTS]), sb("wr_hi", [P, KC, EXPERTS], F32R), sb("wr_lo", [P, KC, EXPERTS], F32R)]
        w = [sb("w_raw", [P, KC, EXPERTS, DIM]), sb("w_hi", [P, KC, EXPERTS, DIM], F32R), sb("w_lo", [P, KC, EXPERTS, DIM], F32R)]
        bias = sb("bias", [EXPERTS, DIM])
        probs, small = sb("probs", [P, NT, EXPERTS]), sb("small", [P, 3, NT])
        top, where, wheref = sb("top", [P, NT, 8]), sb("where", [P, NT, 8], U32), sb("wheref", [P, NT, 8])
        one, one_bf, kept = sb("one", [P, NT, EXPERTS]), sb("one_bf", [P, NT, EXPERTS], BF16), sb("kept", [P, NT, EXPERTS])
        tri_bf = sb("tri", [P, P], BF16)
        weights_t = sb("weights_t", [EXPERTS, TOK])
        y = sb("y", [P, NT, DIM])
        bank = ctx.enter_context(nc.psum_tensor("switch_bank", [P, HALF], FP32))
        locs = ctx.enter_context(nc.psum_tensor("switch_locs", [P, HALF], FP32))
        turn = ctx.enter_context(nc.psum_tensor("switch_turn", [EXPERTS, 2, HALF], FP32))
        acc = [ctx.enter_context(nc.psum_tensor(f"switch_acc{i}", [P, HALF], FP32)) for i in range(4)]
        names = "loaded w_hi w_lo wr_split full e_ready exp_done steps one_ready located weights_ready turned turned_out y_full y_done stored".split()
        s = {n: core.sem(f"switch_{n}") for n in names}
        iota = core.const[:, C_IOTA:C_IOTA + EXPERTS]
        UNITS = 1 + EXPERTS // 2
        with nc.Block() as block:
            @block.sync
            def _(sp):
                sp.dma_start(wr[0][:, :, :], wr_dram).then_inc(s["loaded"], 16)
                sp.dma_start(w[0][:, :, :, :], w_dram).then_inc(s["loaded"], 16)
                sp.dma_start(bias[:, :], bias_dram).then_inc(s["loaded"], 16)
                for t in range(NT):
                    sp.wait_ge(s["y_done"], (t + 1) * (UNITS + 1))
                    sp.dma_start(out[t * P:(t + 1) * P, :], core.x[:, t, :]).then_inc(s["stored"], 16)
                sp.wait_ge(s["stored"], NT * 16)

            @block.gpsimd
            def _(pool):
                pool.wait_ge(s["loaded"], 48)
                nc.gpsimd.tensor_copy(w[1][:, :, :, :], w[0][:, :, :, :]).then_inc(s["w_hi"], 1)
                pool.wait_ge(s["w_hi"], 1)
                nc.gpsimd.tensor_tensor(w[2][:, :, :, :], w[0][:, :, :, :], w[1][:, :, :, :].bitcast(FP32),
                                        ALU.subtract).then_inc(s["w_lo"], 1)

            @block.tensor
            def _(pe):
                pe.wait_ge(s["wr_split"], 3)
                for t in range(NT):
                    for c in range(KC):
                        last = products(nc, bank[:, t * EXPERTS:(t + 1) * EXPERTS], [x[:, c, t * P:(t + 1) * P] for x in tokens],
                                        [x[:, c, :] for x in wr[1:]], c == 0, c == KC - 1)
                last.then_inc(s["full"], 1)
                pe.wait_ge(s["one_ready"], 1)
                for t in range(NT):
                    for e in range(t + 1):
                        last = nc.tensor.matmul(locs[:, t * EXPERTS:(t + 1) * EXPERTS], core.ones_bf if e < t else tri_bf[:, :],
                                                one_bf[:, e, :], start=e == 0, stop=e == t, skip_group_check=True)
                last.then_inc(s["located"], 1)
                pe.wait_ge(s["weights_ready"], 1)
                for t in range(NT):
                    last = nc.tensor.transpose(turn[:, t // 4, (t % 4) * P:(t % 4 + 1) * P], kept[:, t, :], core.ident)
                last.then_inc(s["turned"], 1)
                pe.wait_ge(s["turned_out"], 1)
                pe.wait_ge(s["w_lo"], 1)
                for u in range(NT * UNITS):
                    t, i = divmod(u, UNITS)
                    if u >= 4:
                        pe.wait_ge(s["y_done"], u - 3 + (u - 4) // UNITS)
                    if i == 0:
                        last = nc.tensor.matmul(acc[u % 4][:, 0:DIM], weights_t[:, t * P:(t + 1) * P], bias[:, :], start=True, stop=True)
                    else:
                        for c in range(KC):
                            last = products(nc, acc[u % 4][:, :], [x[:, c, t * P:(t + 1) * P] for x in tokens],
                                            [x[:, c, 2 * i - 2:2 * i, :].rearrange("p e d -> p (e d)") for x in w[1:]], c == 0, c == KC - 1)
                    last.then_inc(s["y_full"], 1)

            @block.scalar
            def _(act):
                act.wait_ge(s["e_ready"], 1)
                nc.scalar.activation(probs[:, :, :], probs[:, :, :], ACT.Exp).then_inc(s["exp_done"], 1)
                act.wait_ge(s["turned"], 1)
                nc.scalar.copy(weights_t[:, :], turn[:, :, :].rearrange("p a n -> p (a n)")).then_inc(s["turned_out"], 1)

            @block.vector
            def _(dve):
                chain = Chain(dve, s["steps"])
                nc.vector.tensor_copy(tri_bf[:, :], core.const[:, C_TRI:C_TRI + P]).then_inc(s["wr_split"], 1)
                dve.wait_ge(s["loaded"], 48)
                nc.vector.tensor_copy(wr[1][:, :, :], wr[0][:, :, :]).then_inc(s["wr_split"], 1)
                dve.wait_ge(s["wr_split"], 2)
                nc.vector.tensor_tensor(wr[2][:, :, :], wr[0][:, :, :], wr[1][:, :, :].bitcast(FP32), ALU.subtract).then_inc(s["wr_split"], 1)
                router_probs(nc, core, dve, chain, s["full"], s["e_ready"], s["exp_done"], bank, probs[:, :, :], small)
                for t in range(NT):
                    chain.then(nc.vector.max(top[:, t, :], probs[:, t, :]))
                    chain.then(nc.vector.max_index(where[:, t, :], top[:, t, :], probs[:, t, :]))
                chain.then(nc.vector.tensor_copy(wheref[:, :, :], where[:, :, :]))
                chain.then(nc.vector.tensor_tensor(one[:, :, :], iota.unsqueeze(1).to_broadcast([P, NT, EXPERTS]),
                                                   wheref[:, :, 0:1].to_broadcast([P, NT, EXPERTS]), ALU.is_equal))
                nc.vector.tensor_copy(one_bf[:, :, :], one[:, :, :]).then_inc(s["one_ready"], 1)
                dve.wait_ge(s["located"], 1)
                chain.then(nc.vector.scalar_tensor_tensor(
                    kept[:, :, :].rearrange("p t e -> p (t e)"), locs[:, 0:NT * EXPERTS], float(CAPACITY),
                    one[:, :, :].rearrange("p t e -> p (t e)"), ALU.is_lt, ALU.mult))
                nc.vector.tensor_tensor(kept[:, :, :], kept[:, :, :], probs[:, :, :], ALU.mult).then_inc(s["weights_ready"], 1)
                dve.wait_ge(s["weights_ready"], 1)
                done = 0
                for u in range(NT * UNITS):
                    t, i = divmod(u, UNITS)
                    dve.wait_ge(s["y_full"], u + 1)
                    if i == 0:
                        nc.vector.tensor_copy(y[:, t, :], acc[u % 4][:, 0:DIM]).then_inc(s["y_done"], 1)
                        done += 1
                        continue
                    dve.wait_ge(s["y_done"], done)
                    e = 2 * i - 2
                    chain.then(nc.vector.scalar_tensor_tensor(y[:, t, :], acc[u % 4][:, 0:DIM], kept[:, t, e:e + 1], y[:, t, :],
                                                              ALU.mult, ALU.add))
                    nc.vector.scalar_tensor_tensor(y[:, t, :], acc[u % 4][:, DIM:2 * DIM], kept[:, t, e + 1:e + 2], y[:, t, :],
                                                   ALU.mult, ALU.add).then_inc(s["y_done"], 1)
                    done += 1
                    if i == UNITS - 1:
                        dve.wait_ge(s["y_done"], done)
                        nc.vector.scalar_tensor_tensor(core.x[:, t, :], y[:, t, :], gate, core.x[:, t, :],
                                                       ALU.mult, ALU.add).then_inc(s["y_done"], 1)
                        done += 1


def split_stage(nc, core, tag, jobs):
    with ExitStack() as ctx:
        raw = [ctx.enter_context(nc.sbuf_tensor(f"{tag}_raw{i}", list(hi.shape), FP32)) for i, (_d, hi, _l) in enumerate(jobs)]
        loaded = [core.sem(f"{tag}_loaded{i}") for i in range(len(jobs))]
        hi_done, lo_done = core.sem(f"{tag}_hi"), core.sem(f"{tag}_lo")
        with nc.Block() as block:
            @block.sync
            def _(sp):
                for i, (dram, _hi, _lo) in enumerate(jobs):
                    sp.dma_start(raw[i][:, :, :], dram).then_inc(loaded[i], 16)

            @block.scalar
            def _(act):
                for i, (_dram, hi, _lo) in enumerate(jobs):
                    act.wait_ge(loaded[i], 16)
                    nc.scalar.copy(hi[:, :, :], raw[i][:, :, :]).then_inc(hi_done, 1)

            @block.vector
            def _(dve):
                for i, (_dram, hi, lo) in enumerate(jobs):
                    dve.wait_ge(hi_done, i + 1)
                    nc.vector.tensor_tensor(lo[:, :, :], raw[i][:, :, :], hi[:, :, :].bitcast(FP32), ALU.subtract).then_inc(lo_done, 1)
                dve.wait_ge(lo_done, len(jobs))


def program(nc, a, out):
    with ExitStack() as ctx:
        core = Core(nc, ctx)
        par, gates = core.par, core.gates
        load_stage(nc, core, a["x"], a["const"], a["par"], a["gates"])

        def pair(stack, name, cols):
            return [stack.enter_context(nc.sbuf_tensor(f"{name}_{x}", [P, KC, cols], F32R)) for x in ("hi", "lo")]

        with ExitStack() as st:
            attn = st.enter_context(nc.sbuf_tensor("lat_attn", [P, PAIRS, TOK], FP32))
            with ExitStack() as src:
                lat, cn = pair(src, "lat", TOK), pair(src, "cn", CTOK)
                norm_stage(nc, core, "nc", None, NCT, [("ln", 0)], par[:, 4:6], par[:, 6:8], *cn, dram=a["ctx"])
                norm_stage(nc, core, "nl", core.x, NT, [("ln", 0), ("ln", 0)], par[:, 0:2], par[:, 2:4], *lat)
                latent_stage(nc, core, lat, cn, a["lat_w"], a["lat_rope"], attn)
            add_projected(nc, core, "lo", attn, a["lat_wo"], PAIRS, core.x, core.x, a["lat_bo"], gates[:, 0:1])
        core.release()
        with ExitStack() as st:
            h = st.enter_context(nc.sbuf_tensor("ffn_h", [P, NT, DIM], FP32))
            attn = st.enter_context(nc.sbuf_tensor("self_attn", [P, GROUPS, TOK], FP32))
            with ExitStack() as src:
                r = pair(src, "r1", TOK)
                norm_stage(nc, core, "n1", core.x, NT, [("ln", 0), ("rms", 1)], par[:, 8:10], None, *r, keep=h)
                v_all = src.enter_context(nc.sbuf_tensor("self_v", [P, NT, DIM], FP32))
                with ExitStack() as sw:
                    wv = pair(sw, "self_wv", DIM)
                    split_stage(nc, core, "s1", [(a["self_wv"], *wv)])
                    values_stage(nc, core, "self_v", r, wv, NT, v_all)
                small_attention(nc, core, "self", r, r, v_all, a["self_w"], True, attn, rope_dram=a["self_rope"], cols_dram=a["self_cols"])
            core.release()
            experts = Experts(nc, core, st, a["moe_gu"], a["moe_down"])
            project_heads(nc, core, attn, a["self_wo"], h, experts)
            with ExitStack() as src:
                r = pair(src, "r2", TOK)
                combine = src.enter_context(nc.sbuf_tensor("combine", [P, NT, EXPERTS], FP32))
                norm_stage(nc, core, "n2", h, NT, [("rms", 1)], par[:, 10:12], None, *r,
                           pool_work=lambda pool: experts.split_lo(pool, 0))
                route_stage(nc, core, r, a["route_w"], combine)
                experts_stage(nc, core, experts, r, combine, h)
            gated_add(nc, core, "moe_add", h, gates[:, 2:3])
        core.release()
        with ExitStack() as st:
            attn = st.enter_context(nc.sbuf_tensor("ctx_attn", [P, GROUPS, TOK], FP32))
            r, c = pair(st, "r3", TOK), pair(st, "ctx", CTOK)
            norm_stage(nc, core, "n3", core.x, NT, [("ln", 0)], None, None, *r)
            v_all = st.enter_context(nc.sbuf_tensor("cross_v", [P, NCT, DIM], FP32))
            with ExitStack() as sw:
                wv = pair(sw, "cross_wv", DIM)
                split_stage(nc, core, "s3", [(a["ctx_wv"], *wv), (a["ctx_t"], *c)])
                values_stage(nc, core, "cross_v", c, wv, NCT, v_all, a["ctx_bv"])
            small_attention(nc, core, "cross", r, c, v_all, a["ctx_w"], False, attn, cols_dram=a["ctx_cols"])
            add_heads(nc, core, attn, gates[:, 1:2])
        core.release()
        with ExitStack() as st:
            r = pair(st, "r4", TOK)
            norm_stage(nc, core, "n4", core.x, NT, [("ln", 0)], None, None, *r)
            switch_stage(nc, core, r, a["sw_router"], a["sw_w"], a["sw_b"], gates[:, 3:4], out)


def constants():
    import numpy as np
    c = np.zeros((P, C_END), np.float32)
    r = np.arange(P)
    c[:, C_IDENT:C_IDENT + P] = np.eye(P)
    c[:, C_TRI:C_TRI + P] = r[:, None] < r[None, :]
    c[:, C_MASK:C_MASK + GH] = r[:, None] // HPAD == np.arange(GH)[None, :]
    c[:, C_ONES:C_ONES + LAT_D] = 1.0
    c[:, C_IOTA:C_IOTA + EXPERTS] = np.arange(EXPERTS)
    c[:, C_CAUSQ:C_CAUSQ + P] = np.where(r[None, :] > r[:, None], -1e30, 0.0)
    c[:, C_CAUSK:C_CAUSK + P] = np.where(r[:, None] > r[None, :], -1e30, 0.0)
    return c


def rotary_table():
    import numpy as np
    inv_freq = 1.0 / 10000.0 ** (np.arange(0, HD, 2, dtype=np.float32) / HD)
    freqs = np.einsum("i,j->ij", np.arange(SEQ, dtype=np.float32), inv_freq).T
    table = np.zeros((GH, HPAD, 2, SEQ), np.float32)
    table[:, 0:HD, 0] = np.concatenate([np.cos(freqs), np.cos(freqs)])
    table[:, 0:HD, 1] = np.concatenate([-np.sin(freqs), np.sin(freqs)])
    table[:, HD, 0] = 1.0
    return table.reshape(P, 2, SEQ)


def layouts(i):
    import numpy as np

    def chunks(w):
        return np.ascontiguousarray(w.reshape(-1, P, w.shape[-1]).transpose(1, 0, 2))

    a = {k: np.asarray(v) for k, v in i.items()}
    f = {"x": a["x"].reshape(TOK, DIM), "ctx": a["ctx_1024"].reshape(CTOK, DIM), "const": constants()}
    f["ctx_t"] = chunks(f["ctx"].T)
    f["par"] = np.concatenate([a[n].reshape(2, P).T for n in (
        "L0_xattn_ln_lat_g", "L0_xattn_ln_lat_b", "L0_xattn_ln_ctx_g", "L0_xattn_ln_ctx_b", "L0_ffn_g1", "L0_ffn_g2")], 1)
    f["gates"] = np.concatenate([a["g_xattn"], a["g_ffn"]])
    wq, (wk, wv) = a["L0_xattn_Wq"], np.split(a["L0_xattn_Wkv"], 2, axis=1)
    f["lat_w"] = np.stack([np.concatenate([chunks(w[:, p * P:(p + 1) * P]) for w in (wq, wk, wv)], 2) for p in range(PAIRS)])
    f["lat_rope"] = np.stack([a[n].reshape(8, P, 32).transpose(1, 0, 2) for n in ("L0_xattn_cos", "L0_xattn_sin")])
    f["lat_wo"], f["lat_bo"] = chunks(a["L0_xattn_Wo"]), a["L0_xattn_bo"]

    def padded(w, swap=False):
        w = w.reshape(*w.shape[:-1], GROUPS, GH, 2, HD // 2)
        out = np.zeros((*w.shape[:-2], HPAD), w.dtype)
        out[..., 0:HD] = (w[..., ::-1, :] if swap else w).reshape(*w.shape[:-2], HD)
        return np.moveaxis(out.reshape(*w.shape[:-3], P), -2, 0)

    def by_group(*ws):
        return np.stack([np.concatenate([chunks(w[g]) for w in ws], 2) for g in range(GROUPS)])

    def columns(k, q):
        both = np.stack([padded(k), padded(q)], -1)
        both[:, HD::HPAD, 0] = 1.0
        return both.transpose(1, 0, 2)

    f["self_w"] = by_group(padded(a["L0_ffn_wq"]), padded(a["L0_ffn_wq"], True), padded(a["L0_ffn_wk"]), padded(a["L0_ffn_wk"], True))
    f["self_wv"] = chunks(a["L0_ffn_wv"])
    f["self_cols"] = columns(np.zeros(DIM, np.float32), np.zeros(DIM, np.float32))
    f["self_rope"] = rotary_table()
    f["self_wo"] = chunks(a["L0_ffn_wo"])
    f["route_w"] = chunks(a["L0_ffn_w_router"])
    g, u, d = a["L0_ffn_wg"], a["L0_ffn_wu"], a["L0_ffn_wd"]
    full = FULL_CHUNKS * P
    f["moe_gu"] = np.stack([chunks(np.concatenate([g[e, :, :full], u[e, :, :full], g[e, :, full:], u[e, :, full:]], 1))
                            for e in range(EXPERTS)])
    down = np.zeros((EXPERTS, HCHUNKS, P, DIM), np.float32)
    down[:, :FULL_CHUNKS] = d[:, :full].reshape(EXPERTS, FULL_CHUNKS, P, DIM)
    down[:, FULL_CHUNKS, P - REST:] = d[:, full:]
    f["moe_down"] = down.transpose(0, 2, 1, 3)
    f["ctx_w"] = by_group(padded(a["L1_xattn_Wq"].T), padded(a["L1_xattn_Wk"].T))
    f["ctx_wv"], f["ctx_bv"] = chunks(a["L1_xattn_Wv"].T), a["L1_xattn_bv"]
    f["ctx_cols"] = columns(a["L1_xattn_bk"], a["L1_xattn_bq"])
    f["sw_router"] = chunks(a["L1_ffn_wg"])
    f["sw_w"] = a["L1_ffn_W"].transpose(2, 0, 1).reshape(2, P, EXPERTS, DIM).transpose(1, 0, 2, 3)
    f["sw_b"] = a["L1_ffn_b"]
    return {k: np.ascontiguousarray(v) for k, v in f.items()}


def kernel(**inputs):
    import numpy as _np
    import concourse.bacc as _bacc
    from concourse import mybir as _mybir
    from concourse.bass_utils import run_bass_kernel_spmd as _run

    nc = _bacc.Bacc("TRN2", target_bir_lowering=False, num_devices=1)
    arrays, args = {}, {}
    for name, a in layouts(inputs).items():
        arrays[f"in_{name}"] = a
        args[name] = nc.dram_tensor(f"in_{name}", a.shape, _mybir.dt.from_np(a.dtype), kind="ExternalInput").ap()
    out = nc.dram_tensor("out_0", (TOK, DIM), _mybir.dt.float32, kind="ExternalOutput").ap()
    program(nc, args, out)
    r = _run(nc, [arrays], core_ids=[0])
    return _np.asarray(r.results[0]["out_0"]).reshape(BATCH, SEQ, DIM)
```

```python
import concourse.bass as bass
from concourse import mybir
from contextlib import ExitStack

FP32 = mybir.dt.float32
F32R = mybir.dt.float32r
BF16 = mybir.dt.bfloat16
U32 = mybir.dt.uint32
ALU = mybir.AluOpType
ACT = mybir.ActivationFunctionType
AX = mybir.AxisListType

P = 128
BATCH, SEQ, CTX, DIM = 2, 512, 1024, 256
TOK = BATCH * SEQ
CTOK = BATCH * CTX
NT, NCT = TOK // P, CTOK // P
KC = DIM // P
HALF = 512
LAT_HEADS, LAT_D = 16, 64
PAIRS = LAT_HEADS // 2
CLIP = 11.0
GROUPS, GH, HD = 4, 4, 16
HPAD = 32
QPAD = 64
EXPERTS, HIDDEN = 8, 704
CAPACITY = TOK // EXPERTS
FULL_CHUNKS = HIDDEN // P
REST = HIDDEN - FULL_CHUNKS * P
HCHUNKS = FULL_CHUNKS + 1

C_IDENT, C_TRI, C_MASK, C_LOW, C_ONES, C_IOTA = 0, 128, 256, 260, 262, 326
C_CAUSQ, C_CAUSK, C_END = 334, 462, 590


class Core:

    def __init__(self, nc, ctx):
        self.nc, self.sems = nc, []
        self.x_loaded = self.sem("x_loaded")
        self.x = ctx.enter_context(nc.sbuf_tensor("x_rows", [P, NT, DIM], FP32))
        self.const = ctx.enter_context(nc.sbuf_tensor("const", [P, C_END], FP32))
        self.const_bf = ctx.enter_context(nc.sbuf_tensor("const_bf", [P, 4, P], BF16))
        self.par = ctx.enter_context(nc.sbuf_tensor("params", [P, 12], FP32))
        self.gates = ctx.enter_context(nc.sbuf_tensor("gates", [P, 4], FP32))
        self.eps = ctx.enter_context(nc.sbuf_tensor("eps", [P, 2], FP32))
        self.ident = self.const[:, C_IDENT:C_IDENT + P]
        self.ident_bf, self.causq_bf = self.const_bf[:, 0, :], self.const_bf[:, 1, :]
        self.causk_bf, self.ones_bf = self.const_bf[:, 2, :], self.const_bf[:, 3, :]

    def sem(self, name):
        self.sems.append(self.nc.alloc_semaphore(name=name))
        return self.sems[-1]

    def release(self):
        self.nc.clear_and_free_semaphores(self.sems)
        self.nc.all_engine_barrier()
        self.sems = []


def wait(eng, sem, value):
    if not isinstance(value, int) or value > 0:
        eng.wait_ge(sem, value)


def repeat(eng, count, body):
    body(0)
    with eng.Fori(1, count) as i:
        body(i)


def products(nc, out, lhs, rhs, start, stop):
    nc.tensor.matmul(out, lhs[0], rhs[0], start=start, stop=False, skip_group_check=True)
    nc.tensor.matmul(out, lhs[0], rhs[1], start=False, stop=False, skip_group_check=True)
    return nc.tensor.matmul(out, lhs[1], rhs[0], start=False, stop=stop, skip_group_check=True)


def load_stage(nc, core, x, const, par, gates, more):
    loaded, made, tanhed = core.sem("par_loaded"), core.sem("eps_made"), core.sem("gates_tanh")
    copied, x_loaded = core.sem("const_copied"), core.x_loaded
    with nc.Block() as block:
        @block.sync
        def _(sp):
            sp.dma_start(core.gates[:, :], gates.partition_broadcast(P)).then_inc(loaded, 16)
            sp.dma_start(core.const[:, :], const).then_inc(loaded, 16)
            sp.dma_start(core.par[:, :], par).then_inc(loaded, 16)
            sp.dma_start(core.x[:, :, :], x.rearrange("(t p) d -> p t d", p=P)).then_inc(x_loaded, 16)
            for dst, src, sem in more:
                sp.dma_start(dst, src).then_inc(sem, 16)

        @block.gpsimd
        def _(pool):
            nc.gpsimd.memset(core.eps[:, 0:1], 1e-5).then_inc(made, 1)
            nc.gpsimd.memset(core.eps[:, 1:2], 1e-6).then_inc(made, 1)
            nc.gpsimd.memset(core.ones_bf, 1.0).then_inc(made, 1)
            pool.wait_ge(made, 3)

        @block.scalar
        def _(act):
            act.wait_ge(loaded, 48)
            nc.scalar.activation(core.gates[:, :], core.gates[:, :], ACT.Tanh).then_inc(tanhed, 1)
            act.wait_ge(tanhed, 1)

        @block.vector
        def _(dve):
            dve.wait_ge(loaded, 48)
            for dst, c in ((core.ident_bf, C_IDENT), (core.causq_bf, C_CAUSQ), (core.causk_bf, C_CAUSK)):
                nc.vector.tensor_copy(dst, core.const[:, c:c + P]).then_inc(copied, 1)
            dve.wait_ge(copied, 3)


def norm_stage(nc, core, tag, src, n, norms, gain, bias, hi, lo, keep=None, loaded=None, ahead=None):
    with ExitStack() as ctx:
        def sb(name, shape, dt=FP32):
            return ctx.enter_context(nc.sbuf_tensor(f"{tag}_{name}", shape, dt))

        stats, mv = sb("stats", [P, n, 6]), sb("mean_var", [P, n, 2])
        msq, std, rstd = sb("msq", [P, n]), sb("std", [P, n]), sb("rstd", [P, n])
        z = [keep if (keep is not None and k == 0) else sb(f"normed{k}", [P, n, DIM]) for k in range(len(norms))]
        whole = sb("whole", [P, 2, HALF])
        banks = [ctx.enter_context(nc.psum_tensor(f"{tag}_bank{i}", [P, HALF], FP32)) for i in range(2)]
        stats_done, aggr_done = core.sem(f"{tag}_stats"), core.sem(f"{tag}_aggr")
        sq_done, var_ready, std_ready = core.sem(f"{tag}_sq"), core.sem(f"{tag}_var"), core.sem(f"{tag}_std")
        rstd_done, normed, turned = core.sem(f"{tag}_rstd"), core.sem(f"{tag}_normed"), core.sem(f"{tag}_turned")
        evacuated, hi_done, lo_done = core.sem(f"{tag}_evac"), core.sem(f"{tag}_hi"), core.sem(f"{tag}_lo")
        blocks = [(q, c) for q in range(n // 4) for c in range(KC)]
        K = len(norms)
        with nc.Block() as block:
            if ahead is not None:
                block.sync(ahead.sync)
                block.gpsimd(ahead.gpsimd)

            @block.vector
            def _(dve):
                if loaded is not None:
                    dve.wait_ge(loaded, 16)
                for k, (kind, _eps) in enumerate(norms):
                    rows = src if k == 0 else z[k - 1]
                    if k:
                        dve.wait_ge(normed, k * n)
                    for t in range(n):
                        nc.vector.bn_stats(stats[:, t, :], rows[:, t, :]).then_inc(stats_done, 1)
                    dve.wait_ge(stats_done, (k + 1) * n)
                    for t in range(n):
                        nc.vector.bn_aggr(mv[:, t, :], stats[:, t, :]).then_inc(aggr_done, 1)
                    dve.wait_ge(aggr_done, (k + 1) * n)
                    if kind == "rms":
                        nc.vector.tensor_tensor(msq[:, :], mv[:, :, 0], mv[:, :, 0], ALU.mult).then_inc(sq_done, 1)
                        dve.wait_ge(sq_done, 1)
                        nc.vector.tensor_tensor(msq[:, :], msq[:, :], mv[:, :, 1], ALU.add).then_inc(var_ready, 1)
                    else:
                        nc.vector.tensor_copy(msq[:, :], mv[:, :, 1]).then_inc(var_ready, 1)
                    dve.wait_ge(std_ready, k + 1)
                    nc.vector.reciprocal(rstd[:, :], std[:, :]).then_inc(rstd_done, 1)
                    dve.wait_ge(rstd_done, k + 1)
                    for t in range(n):
                        if kind == "rms":
                            op = nc.vector.tensor_scalar(z[k][:, t, :], rows[:, t, :], rstd[:, t:t + 1], None, ALU.mult)
                        else:
                            op = nc.vector.tensor_scalar(z[k][:, t, :], rows[:, t, :], mv[:, t, 0:1], rstd[:, t:t + 1],
                                                         ALU.subtract, ALU.mult)
                        op.then_inc(normed, 1)
                for j, (q, c) in enumerate(blocks):
                    cols = slice(HALF * q, HALF * (q + 1))
                    dve.wait_ge(evacuated, j + 1)
                    nc.vector.tensor_copy(hi[:, c, cols], whole[:, j % 2, :]).then_inc(hi_done, 1)
                    dve.wait_ge(hi_done, j + 1)
                    nc.vector.tensor_tensor(lo[:, c, cols], whole[:, j % 2, :], hi[:, c, cols].bitcast(FP32),
                                            ALU.subtract).then_inc(lo_done, 1)

            @block.tensor
            def _(pe):
                for j, (q, c) in enumerate(blocks):
                    pe.wait_ge(normed, (K - 1) * n + 4 * (q + 1))
                    if j >= 2:
                        pe.wait_ge(evacuated, j - 1)
                    for i in range(4):
                        last = nc.tensor.transpose(banks[j % 2][:, i * P:(i + 1) * P],
                                                   z[-1][:, 4 * q + i, c * P:(c + 1) * P], core.ident)
                    last.then_inc(turned, 1)

            @block.scalar
            def _(act):
                if ahead is not None:
                    ahead.scalar(act)
                for k, (_kind, eps) in enumerate(norms):
                    act.wait_ge(var_ready, k + 1)
                    nc.scalar.activation(std[:, :], msq[:, :], ACT.Sqrt, bias=core.eps[:, eps:eps + 1]).then_inc(std_ready, 1)
                for j, (q, c) in enumerate(blocks):
                    act.wait_ge(turned, j + 1)
                    if j >= 2:
                        act.wait_ge(lo_done, j - 1)
                    scale = gain[:, c:c + 1] if gain is not None else 1.0
                    off = bias[:, c:c + 1] if bias is not None else 0.0
                    nc.scalar.activation(whole[:, j % 2, :], banks[j % 2][:, :], ACT.Identity, bias=off,
                                         scale=scale).then_inc(evacuated, 1)


def latent_stage(nc, core, lat, cn, w_dram, w_raw, w_loaded, rope, rope_loaded, attn, wo_dram, wo_loaded):
    W = 3 * P
    STEPS = BATCH * (CTX // P)
    KVB = NCT // 2
    E_LO, E_HI = float(2.718281828459045 ** -CLIP), float(2.718281828459045 ** CLIP)
    with ExitStack() as ctx:
        def sb(name, shape, dt=FP32):
            return ctx.enter_context(nc.sbuf_tensor(f"lat_{name}", shape, dt))

        def ps(name, shape):
            return ctx.enter_context(nc.psum_tensor(f"lat_{name}", shape, FP32))

        w = [[sb(f"w{k}{s}", [P, KC, W], F32R) for s in ("hi", "lo")] for k in range(2)]
        kt = [[sb(f"kt{k}{s}", [P, CTOK], F32R) for s in ("hi", "lo")] for k in range(2)]
        qt = [[sb(f"qt{k}{s}", [P, TOK], F32R) for s in ("hi", "lo")] for k in range(2)]
        vals = [sb(f"v{k}", [P, NCT, P]) for k in range(2)]
        wo_raw = vals[0][:, :, :].rearrange("p (k t) d -> p k (t d)", k=PAIRS)
        k_raw = sb("k_raw", [P, 2, 2, P])
        keys = sb("keys", [P, KVB, 2, P])
        rot_a, rot_b = sb("rot_a", [P, 2, P]), sb("rot_b", [P, 2, P])
        probs = sb("probs", [P, 4, 2, HALF])
        acc = sb("acc", [P, 2, HALF])
        inv = sb("inv", [P, 2, P])
        scores = [ps(f"scores{i}", [P, 2, HALF]) for i in range(2)]
        outs, proj, turn = ps("outs", [P, HALF]), ps("proj", [P, HALF]), ps("turn", [P, HALF])
        ones = core.const[:, C_ONES:C_ONES + LAT_D]
        SUMS = CTX // P - 1

        names = ("wo_hi wo_lo w_hi w_lo kv_full q_full rot_mul k_out keys_made v_made turned kt_hi kt_made qt_hi qt_made "
                 "scored exped clipped summed pv_done raw_done bc_full inv_q bc_done negsin").split()
        s = {n: core.sem(f"lat_{n}") for n in names}
        s["w_loaded"] = w_loaded

        proj_banks, turn_banks = [proj[:, :], scores[1][:, 0, :]], [turn[:, :], outs[:, :]]

        def bank(banks, p, i):
            return banks[i % 2 if isinstance(p, int) and p == 0 else 0]

        def banks_free(p, i):
            return i - 1 if isinstance(p, int) and p == 0 else i

        def freed(n):
            b, c = divmod(n, STEPS // 2)
            return b * SUMS + max(c, 1)

        def pairs(eng, first, pair, end, looped=PAIRS - 2):
            first()
            pair(0, 0)
            with eng.Fori(0, looped // 2) as i:
                pair(i * 2 + 1, 1)
                pair(i * 2 + 2, 0)
            for p in range(looped + 1, PAIRS):
                pair(p, p % 2)
            end()

        with nc.Block() as block:
            @block.sync
            def _(sp):
                with sp.Fori(1, PAIRS) as p:
                    sp.wait_ge(s["w_lo"], p)
                    sp.dma_start(w_raw[:, :, :], w_dram[bass.ts(p, 1)].rearrange("a p k n -> p (a k) n")).then_inc(s["w_loaded"], 16)
                sp.wait_ge(s["pv_done"], (PAIRS - 1) * STEPS)
                sp.dma_start(wo_raw, wo_dram).then_inc(wo_loaded, 16)

            @block.gpsimd
            def _(pool):
                def split(p, k):
                    pool.wait_ge(s["w_hi"], p + 1)
                    nc.gpsimd.tensor_tensor(w[k][1][:, :, :], w_raw[:, :, :], w[k][0][:, :, :].bitcast(FP32),
                                            ALU.subtract).then_inc(s["w_lo"], 1)

                def add_up(p, n):
                    b, c = divmod(n, STEPS // 2)
                    if c == 0:
                        return
                    if c == 1:
                        wait(pool, s["bc_full"], p * 2 + b)
                    else:
                        wait(pool, s["summed"], p * (2 * SUMS) + (b * SUMS + c - 1))
                    wait(pool, s["clipped"], p * STEPS + (n + 1))
                    first = probs[:, (n - 1) % 4, :, :] if c == 1 else acc[:, :, :]
                    nc.gpsimd.tensor_tensor(acc[:, :, :], first, probs[:, n % 4, :, :], ALU.add).then_inc(s["summed"], 1)

                def first():
                    split(0, 0)
                    split(1, 1)

                def pair(p, k):
                    for n in range(STEPS):
                        add_up(p, n)
                        if n == 8 and not (isinstance(p, int) and p + 2 >= PAIRS):
                            split(p + 2, k)

                def end():
                    pool.wait_ge(s["wo_hi"], 1)
                    hi, lo = latent_wo(cn)
                    nc.gpsimd.tensor_tensor(lo, wo_raw, hi.bitcast(FP32), ALU.subtract).then_inc(s["wo_lo"], 1)
                    pool.wait_ge(s["wo_lo"], 1)

                pairs(pool, first, pair, end, PAIRS - 4)

            @block.tensor
            def _(pe):
                def score(p, k, n):
                    if n == 0:
                        wait(pe, s["kt_made"], p * 4 + 4)
                        wait(pe, s["qt_made"], p * 2 + 2)
                    wait(pe, s["exped"], p * STEPS + (n - 1))
                    b, c = divmod(n, STEPS // 2)
                    for h in range(2):
                        rows, ks = slice(64 * h, 64 * h + 64), slice(b * CTX + c * P, b * CTX + (c + 1) * P)
                        qs = slice(b * SEQ, (b + 1) * SEQ)
                        last = products(nc, scores[n % 2][:, h, :], [x[rows, ks] for x in kt[k]],
                                        [x[rows, qs] for x in qt[k]], True, True)
                    last.then_inc(s["scored"], 1)

                def values(p, k, n):
                    b, c = divmod(n, STEPS // 2)
                    if n == 0:
                        wait(pe, s["v_made"], p * KVB + KVB)
                    if c == 0:
                        wait(pe, s["raw_done"], p * 2 + b)
                    wait(pe, s["clipped"], p * STEPS + (n + 1))
                    for h in range(2):
                        rows = slice(64 * h, 64 * h + 64)
                        last = nc.tensor.matmul(outs[rows, :], vals[k][:, b * 8 + c, rows], probs[:, n % 4, h, :],
                                                start=c == 0, stop=c == 7, skip_group_check=True)
                    last.then_inc(s["pv_done"], 1)

                def project_kv(p, k, j):
                    if j == 0:
                        pe.wait_ge(s["w_lo"], p + 1)
                        wait(pe, s["qt_made"], p * 2)
                    else:
                        wait(pe, s["v_made"], p * KVB + banks_free(p, j))
                    for i in range(2):
                        rows = slice((2 * j + i) * P, (2 * j + i + 1) * P)
                        for c in range(KC):
                            last = products(nc, bank(proj_banks, p, j)[:, i * 256:(i + 1) * 256], [x[:, c, rows] for x in cn],
                                            [x[:, c, P:3 * P] for x in w[k]], c == 0, c == KC - 1)
                    last.then_inc(s["kv_full"], 1)

                def project_q(p, k, b):
                    if b == 0:
                        wait(pe, s["v_made"], p * KVB + banks_free(p, KVB))
                    elif isinstance(p, int) and p == 0:
                        wait(pe, s["v_made"], KVB)
                    else:
                        wait(pe, s["qt_made"], p * 2 + 1)
                    for c in range(KC):
                        last = products(nc, bank(proj_banks, p, b), [x[:, c, 0:P] for x in w[k]],
                                        [x[:, c, b * SEQ:(b + 1) * SEQ] for x in lat], c == 0, c == KC - 1)
                    last.then_inc(s["q_full"], 1)

                def turn_keys(p, i):
                    if i:
                        wait(pe, s["kt_made"], p * 4 + banks_free(p, i))
                    else:
                        wait(pe, s["bc_done"], p * 2 - 2)
                    wait(pe, s["keys_made"], p * KVB + (2 * i + 2))
                    for j in range(4):
                        last = nc.tensor.transpose(bank(turn_banks, p, i)[:, j * P:(j + 1) * P], keys[:, 2 * i + j // 2, j % 2, :], core.ident)
                    last.then_inc(s["turned"], 1)

                def spread_sums(p, b):
                    if b:
                        wait(pe, s["bc_done"], p * 2 + 1)
                    elif not isinstance(p, int) or p < PAIRS - 1:
                        wait(pe, s["kt_made"], p * 4 + 8)
                    else:
                        wait(pe, s["bc_done"], p * 2)
                    wait(pe, s["summed"], p * (2 * SUMS) + (b + 1) * SUMS)
                    for h in range(2):
                        last = nc.tensor.matmul(turn[64 * h:64 * h + 64, :], ones, acc[:, h, :], start=True, stop=True, skip_group_check=True)
                    last.then_inc(s["bc_full"], 1)

                def first():
                    for j in range(KVB):
                        project_kv(0, 0, j)
                        if j % 2 == 0 and j:
                            turn_keys(0, j // 2 - 1)
                    project_q(0, 0, 0)
                    turn_keys(0, KVB // 2 - 1)
                    project_q(0, 0, 1)
                    score(0, 0, 0)

                def pair(p, k):
                    ahead = not (isinstance(p, int) and p == PAIRS - 1)
                    for n in range(STEPS):
                        if n + 1 < STEPS:
                            score(p, k, n + 1)
                        elif ahead:
                            score(p + 1, 1 - k, 0)
                        if ahead and n < KVB:
                            project_kv(p + 1, 1 - k, n)
                        if n == 1 and not (isinstance(p, int) and p == 0):
                            spread_sums(p - 1, 1)
                        if ahead and 5 <= n < 9:
                            turn_keys(p + 1, n - 5)
                        if ahead and n in (8, 9):
                            project_q(p + 1, 1 - k, n - 8)
                        if n == 9:
                            spread_sums(p, 0)
                        values(p, k, n)

                def end():
                    spread_sums(PAIRS - 1, 1)

                pairs(pe, first, pair, end)

            @block.scalar
            def _(act):
                def weights_hi(p, k):
                    wait(act, s["w_loaded"], p * 16 + 16)
                    wait(act, s["q_full"], p * 2 - 2)
                    nc.scalar.copy(w[k][0][:, :, :], w_raw[:, :, :]).then_inc(s["w_hi"], 1)

                def exp(p, n):
                    wait(act, s["scored"], p * STEPS + (n + 1))
                    wait(act, s["pv_done"], p * STEPS + (n - 3))
                    wait(act, s["summed"], p * (2 * SUMS) + (freed(n - 4) if n >= 4 else freed(n + STEPS - 4) - 2 * SUMS))
                    nc.scalar.activation(probs[:, n % 4, :, :], scores[n % 2][:, :, :], ACT.Exp,
                                         scale=LAT_D ** -0.5).then_inc(s["exped"], 1)

                def values_out(p, k, j):
                    wait(act, s["kv_full"], p * KVB + (j + 1))
                    wait(act, s["keys_made"], p * KVB + (j - 1))
                    both = bank(proj_banks, p, j).rearrange("p (t n) -> p t n", t=2)
                    nc.scalar.copy(k_raw[:, j % 2, :, :], both[:, :, 0:P]).then_inc(s["k_out"], 1)
                    nc.scalar.copy(vals[k][:, 2 * j:2 * j + 2, :], both[:, :, P:2 * P]).then_inc(s["v_made"], 1)

                def raw_out(p, b):
                    wait(act, s["pv_done"], p * STEPS + 8 * (b + 1))
                    nc.scalar.copy(attn[:, bass.ts(p, 1), b * SEQ:(b + 1) * SEQ], outs[:, :].unsqueeze(1)).then_inc(s["raw_done"], 1)

                def first():
                    weights_hi(0, 0)
                    for j in range(KVB):
                        values_out(0, 0, j)
                    weights_hi(1, 1)

                def pair(p, k):
                    ahead = not (isinstance(p, int) and p == PAIRS - 1)
                    for n in range(STEPS):
                        exp(p, n)
                        if n == 0 and not (isinstance(p, int) and p == 0):
                            raw_out(p - 1, 1)
                        if ahead and n < KVB:
                            values_out(p + 1, 1 - k, n)
                        if n == 8:
                            raw_out(p, 0)
                            if not (isinstance(p, int) and p + 2 >= PAIRS):
                                weights_hi(p + 2, k)

                def end():
                    act.wait_ge(s["kv_full"], PAIRS * KVB)
                    act.wait_ge(wo_loaded, 16)
                    nc.scalar.copy(latent_wo(cn)[0], wo_raw).then_inc(s["wo_hi"], 1)
                    raw_out(PAIRS - 1, 1)

                pairs(act, first, pair, end, PAIRS - 4)

            @block.vector
            def _(dve):
                def clip(p, n):
                    wait(dve, s["exped"], p * STEPS + (n + 1))
                    nc.vector.tensor_scalar(probs[:, n % 4, :, :], probs[:, n % 4, :, :], E_HI, E_LO,
                                            ALU.min, ALU.max).then_inc(s["clipped"], 1)

                def rotate(p, j):
                    t = (2 * j) % (CTX // P)
                    wait(dve, s["k_out"], p * KVB + (j + 1))
                    ps_k = k_raw[:, j % 2, :, :]
                    wait(dve, s["keys_made"], p * KVB + j)
                    nc.vector.tensor_tensor(rot_a[:, :, :].rearrange("p t (g d) -> p t g d", d=32),
                                            ps_k.rearrange("p t (g d) -> p t g d", d=32),
                                            rope[:, t:t + 2, 0, :].unsqueeze(2).to_broadcast([P, 2, 4, 32]),
                                            ALU.mult).then_inc(s["rot_mul"], 1)
                    for half in range(2):
                        dst = rot_b[:, :, :].rearrange("p t (g a d) -> p t g a d", a=2, d=32)[:, :, :, half, :]
                        src = ps_k.rearrange("p t (g a d) -> p t g a d", a=2, d=32)[:, :, :, 1 - half, :]
                        nc.vector.tensor_tensor(dst, src, rope[:, t:t + 2, 1 + half, :].unsqueeze(2).to_broadcast([P, 2, 2, 32]),
                                                ALU.mult).then_inc(s["rot_mul"], 1)
                    wait(dve, s["rot_mul"], p * (3 * KVB) + 3 * (j + 1))
                    nc.vector.tensor_tensor(keys[:, j, :, :], rot_a[:, :, :], rot_b[:, :, :], ALU.add).then_inc(s["keys_made"], 1)

                def split_keys(p, k, i):
                    cols = slice(i * HALF, (i + 1) * HALF)
                    wait(dve, s["turned"], p * 4 + (i + 1))
                    src = bank(turn_banks, p, i)
                    nc.vector.tensor_copy(kt[k][0][:, cols], src).then_inc(s["kt_hi"], 1)
                    wait(dve, s["kt_hi"], p * 4 + (i + 1))
                    nc.vector.tensor_tensor(kt[k][1][:, cols], src, kt[k][0][:, cols].bitcast(FP32),
                                            ALU.subtract).then_inc(s["kt_made"], 1)

                def split_queries(p, k, b):
                    cols = slice(b * SEQ, (b + 1) * SEQ)
                    wait(dve, s["q_full"], p * 2 + (b + 1))
                    src = bank(proj_banks, p, b)
                    nc.vector.tensor_copy(qt[k][0][:, cols], src).then_inc(s["qt_hi"], 1)
                    wait(dve, s["qt_hi"], p * 2 + (b + 1))
                    nc.vector.tensor_tensor(qt[k][1][:, cols], src, qt[k][0][:, cols].bitcast(FP32),
                                            ALU.subtract).then_inc(s["qt_made"], 1)

                def normalise(p, b, q):
                    cols = slice(q * P, (q + 1) * P)
                    wait(dve, s["bc_full"], p * 2 + (b + 1))
                    if q == 0:
                        wait(dve, s["raw_done"], p * 2 + (b + 1))
                    nc.vector.reciprocal(inv[:, q % 2, :], turn[:, cols]).then_inc(s["inv_q"], 1)
                    wait(dve, s["inv_q"], p * 8 + (4 * b + q + 1))
                    part = attn[:, bass.ts(p, 1), b * SEQ + q * P:b * SEQ + (q + 1) * P]
                    op = nc.vector.tensor_tensor(part, part, inv[:, q % 2, :].unsqueeze(1), ALU.mult)
                    if q == 3:
                        op.then_inc(s["bc_done"], 1)

                def first():
                    dve.wait_ge(rope_loaded, 32)
                    nc.vector.tensor_scalar(rope[:, :, 1, :], rope[:, :, 2, :], -1.0, None, ALU.mult).then_inc(s["negsin"], 1)
                    dve.wait_ge(s["negsin"], 1)
                    for j in range(KVB):
                        rotate(0, j)
                        if j % 2 == 0 and j:
                            split_keys(0, 0, j // 2 - 1)
                    split_queries(0, 0, 0)
                    split_keys(0, 0, KVB // 2 - 1)
                    split_queries(0, 0, 1)

                def pair(p, k):
                    ahead = not (isinstance(p, int) and p == PAIRS - 1)
                    for n in range(STEPS):
                        clip(p, n)
                        if ahead and n < KVB:
                            rotate(p + 1, n)
                        if 1 <= n < 5 and not (isinstance(p, int) and p == 0):
                            normalise(p - 1, 1, n - 1)
                        if ahead and 5 <= n < 9:
                            split_keys(p + 1, 1 - k, n - 5)
                        if ahead and n in (8, 9):
                            split_queries(p + 1, 1 - k, n - 8)
                        if 10 <= n < 14:
                            normalise(p, 0, n - 10)

                def end():
                    for q in range(4):
                        normalise(PAIRS - 1, 1, q)

                pairs(dve, first, pair, end)


def latent_wo(cn):
    return [x[:, 0, :].rearrange("p (k d) -> p k d", d=DIM) for x in cn]


def latent_out(nc, core, attn, wo, bias_dram, gate):
    with ExitStack() as ctx:
        def sb(name, shape, dt=FP32):
            return ctx.enter_context(nc.sbuf_tensor(f"lo_{name}", shape, dt))

        bias, tmp = sb("bias", [P, DIM]), sb("tmp", [P, NT, DIM])
        parts = [[sb(f"attn{k}{x}", [P, PAIRS, P], F32R) for x in ("hi", "lo")] for k in range(2)]
        banks = [ctx.enter_context(nc.psum_tensor(f"lo_bank{i}", [P, DIM], FP32)) for i in range(2)]
        loaded, hi_done, lo_done, full, biased, added = (
            core.sem(f"lo_{n}") for n in ("loaded", "hi_done", "lo_done", "full", "biased", "added"))
        with nc.Block() as block:
            @block.sync
            def _(sp):
                sp.dma_start(bias[:, :], bias_dram.partition_broadcast(P)).then_inc(loaded, 16)

            @block.tensor
            def _(pe):
                for t in range(NT):
                    pe.wait_ge(lo_done, t + 1)
                    if t >= 2:
                        pe.wait_ge(biased, t - 1)
                    for c in range(PAIRS):
                        last = products(nc, banks[t % 2][:, :], [x[:, c, :] for x in parts[t % 2]], [x[:, c, :] for x in wo],
                                        c == 0, c == PAIRS - 1)
                    last.then_inc(full, 1)

            @block.scalar
            def _(act):
                for t in range(NT):
                    if t >= 2:
                        act.wait_ge(full, t - 1)
                        act.wait_ge(lo_done, t - 1)
                    nc.scalar.copy(parts[t % 2][0][:, :, :], attn[:, :, t * P:(t + 1) * P]).then_inc(hi_done, 1)

            @block.vector
            def _(dve):
                for t in range(NT + 1):
                    if t < NT:
                        dve.wait_ge(hi_done, t + 1)
                        nc.vector.tensor_tensor(parts[t % 2][1][:, :, :], attn[:, :, t * P:(t + 1) * P],
                                                parts[t % 2][0][:, :, :].bitcast(FP32), ALU.subtract).then_inc(lo_done, 1)
                    if t == 0:
                        dve.wait_ge(loaded, 16)
                        continue
                    dve.wait_ge(full, t)
                    nc.vector.tensor_tensor(tmp[:, t - 1, :], banks[(t - 1) % 2][:, :], bias[:, :], ALU.add).then_inc(biased, 1)
                    dve.wait_ge(biased, t)
                    nc.vector.scalar_tensor_tensor(core.x[:, t - 1, :], tmp[:, t - 1, :], gate, core.x[:, t - 1, :],
                                                   ALU.mult, ALU.add).then_inc(added, 1)
                dve.wait_ge(added, NT)


def causal_attention(nc, core, tag, src, v_all, wv, w_dram, attn, cols_dram, rope_dram):
    C = src[0].shape[2] // P // BATCH
    KB = C * P // HALF
    S = 2 * C
    M = (NT // BATCH) * GH
    NB = KB + 1
    PIECES = [(0, 0), (0, P), (1, 2 * P), (1, 3 * P)]
    NW = 4 * P
    NPJ = len(PIECES)
    X = M * KB
    turn_at = S - 4
    piece_at = [2, 3, 5, 6]
    max_at = [x * turn_at // X for x in range(X)]
    values_at = [j * X // C for j in range(C)]
    with_max = [2 + i * (X - 2) // NPJ for i in range(NPJ)]
    BEFORE_TURN = sum(at <= turn_at for at in piece_at)
    SCALE = HD ** -0.5
    with ExitStack() as ctx:
        def sb(name, shape, dt=FP32):
            return ctx.enter_context(nc.sbuf_tensor(f"{tag}_{name}", shape, dt))

        def ps(name, shape):
            return ctx.enter_context(nc.psum_tensor(f"{tag}_{name}", shape, FP32))

        w_raw = sb("w_raw", [P, KC, NW])
        w = [sb(f"w{x}", [P, KC, NW], F32R) for x in ("hi", "lo")]
        ones_row = sb("ones_row", [P, 1])
        rope, rot = sb("rope", [P, 2, HALF]), sb("rot", [P, 2, HALF])
        whole = sb("whole", [P, BATCH, NB, HALF])
        kt = [[sb(f"kt{k}{x}", [P, C * P], F32R) for x in ("hi", "lo")] for k in range(2)]
        q_hi, q_lo, q_low = sb("q_hi", [P, HALF], F32R), sb("q_lo", [P, HALF]), sb("q_low", [P, HALF])
        qm = [[sb(f"qm{k}{x}", [P, GH, HALF], F32R) for x in ("hi", "lo")] for k in range(2)]
        vals = [sb(f"v{k}", [P, C, GH, HPAD]) for k in range(2)]
        mx, mx_all, neg = sb("mx", [P, M, KB]), sb("mx_all", [P, M]), sb("neg", [P, NT // BATCH, GH, HPAD])
        probs = sb("probs", [P, 4, 2, HALF])
        slots = [ps(f"scores{i}", [P, 2, HALF]) for i in range(2)]
        outs, work = ps("outs", [P, HALF]), ps("work", [P, HALF])
        mbank = ps("maxima", [P, 2, HALF])
        mask = [core.const[:, C_MASK + h:C_MASK + h + 1] for h in range(GH)]
        names = ("preset tables v_full v_copied w_loaded w_hi w_lo v_staged proj_full proj_out whole_done hi_done lo_done qm_hi max_scored max_done max_all "
                 "neg_done neg_turned low_done qm_lo scored exped pv_done raw_done").split()
        s = {n: core.sem(f"{tag}_{n}") for n in names}

        def width(c):
            return c * P

        class Unit:

            def __init__(self, g, b):
                self.g, self.b = g, b
                self.first, self.last = isinstance(g, int) and (g, b) == (0, 0), isinstance(g, int) and (g, b) == (GROUPS - 1, 1)

            def count(self, per, more=0):
                return self.g * (2 * per) + (self.b * per + more)

            def next(self):
                return Unit(self.g, 1) if self.b == 0 else Unit(self.g + 1, 0)

            def after_next(self):
                return Unit(self.g + 1, self.b)

            def projects(self):
                return not (isinstance(self.g, int) and self.g == GROUPS - 1)

            def before(self):
                return Unit(self.g, 0) if self.b == 1 else Unit(self.g - 1, 1)

        def units(eng, first, unit, end=lambda u: None):
            first(Unit(0, 0))
            for b in range(BATCH):
                unit(Unit(0, b))
            with eng.Fori(1, GROUPS - 1) as g:
                for b in range(BATCH):
                    unit(Unit(g, b))
            for b in range(BATCH):
                unit(Unit(GROUPS - 1, b))
            end(Unit(GROUPS - 1, 1))

        with nc.Block() as block:
            @block.sync
            def _(sp):
                sp.dma_start(w_raw[:, :, :], w_dram[0]).then_inc(s["w_loaded"], 16)
                sp.dma_start(ones_row[:, :], cols_dram).then_inc(s["tables"], 16)
                sp.dma_start(rope[:, :, :], rope_dram).then_inc(s["tables"], 16)
                for g in range(1, GROUPS):
                    sp.wait_ge(s["w_lo"], g)
                    sp.dma_start(w_raw[:, :, :], w_dram[g]).then_inc(s["w_loaded"], 16)

            @block.gpsimd
            def _(pool):
                def split_weights(g):
                    wait(pool, s["w_hi"], g + 1)
                    nc.gpsimd.tensor_tensor(w[1][:, :, :], w_raw[:, :, :], w[0][:, :, :].bitcast(FP32), ALU.subtract).then_inc(s["w_lo"], 1)

                def add_rotated(u):
                    for j in range(NB):
                        wait(pool, s["proj_out"], u.count(NPJ, 2 * j + 2))
                        wait(pool, s["lo_done"], u.count(NB, j + 1 - 2 * NB))
                        nc.gpsimd.tensor_tensor(whole[:, u.b, j, :], rot[:, 0, :], rot[:, 1, :], ALU.add).then_inc(s["whole_done"], 1)

                def low_parts(u):
                    for j in range(NB):
                        wait(pool, s["hi_done"], u.count(NB, j + 1))
                        hi = q_hi[:, :] if j == 0 else kt[u.b][0][:, (j - 1) * HALF:j * HALF]
                        lo = q_lo[:, :] if j == 0 else kt[u.b][1][:, (j - 1) * HALF:j * HALF]
                        if j == 0:
                            wait(pool, s["low_done"], u.count(1))
                        nc.gpsimd.tensor_tensor(lo, whole[:, u.b, j, :], hi.bitcast(FP32), ALU.subtract).then_inc(s["lo_done"], 1)

                for buf in (vals[0], vals[1], neg):
                    nc.gpsimd.memset(buf[:, :, :, HD:HPAD], 0.0).then_inc(s["preset"], 1)
                pool.wait_ge(s["preset"], 3)
                for buf in vals:
                    nc.gpsimd.memset(buf[:, :, :, HD:HD + 1], 1.0).then_inc(s["preset"], 1)
                nc.gpsimd.memset(neg[:, :, :, 0:HD], 0.0).then_inc(s["preset"], 1)

                def first(u):
                    split_weights(0)
                    for v in (u, u.next()):
                        add_rotated(v)
                        low_parts(v)

                def unit(u):
                    if u.b == 0 and u.projects():
                        split_weights(u.g + 1)
                    if u.projects():
                        add_rotated(u.after_next())
                        low_parts(u.after_next())

                units(pool, first, unit)

            @block.tensor
            def _(pe):
                def project(u, i, after_turn=False):
                    j, col = PIECES[i]
                    if i == 0 and u.b == 0:
                        wait(pe, s["w_lo"], u.g + 1)
                    wait(pe, s["low_done"], u.count(1, 0 if after_turn else -1))
                    wait(pe, s["proj_out"], u.count(NPJ, i))
                    n0 = u.b * C * P + (j - 1) * HALF if j else u.b * SEQ
                    for c in range(KC):
                        last = products(nc, work[:, :], [x[:, c, col:col + P] for x in w],
                                        [x[:, c, n0:n0 + HALF] for x in src], c == 0, c == KC - 1)
                    last.then_inc(s["proj_full"], 1)

                def score_max(u, x):
                    m, j = divmod(x, KB)
                    tq, h = divmod(m, GH)
                    if x == 0:
                        wait(pe, s["qm_hi"], u.count(1, 1))
                        wait(pe, s["hi_done"], u.count(NB, NB))
                    wait(pe, s["max_done"], u.count(X, x - 1))
                    keys = (tq + 1) * P
                    last = nc.tensor.matmul(mbank[:, x % 2, 0:keys], qm[u.b][0][:, h, tq * P:(tq + 1) * P],
                                            kt[u.b][0][:, j * HALF:j * HALF + keys], start=True, stop=False, skip_group_check=True)
                    last = nc.tensor.matmul(mbank[:, x % 2, tq * P:(tq + 1) * P], core.ident_bf, core.causq_bf,
                                            start=False, stop=True, skip_group_check=True)
                    last.then_inc(s["max_scored"], 1)

                def turn_neg(u, ahead):
                    wait(pe, s["neg_done"], u.count(1, 1))
                    wait(pe, s["proj_out"], u.count(NPJ, NPJ + ahead))
                    for t in range(NT // BATCH):
                        last = nc.tensor.transpose(work[:, t * P:(t + 1) * P], neg[:, t, :, :].rearrange("p h d -> p (h d)"), core.ident)
                    last.then_inc(s["neg_turned"], 1)

                def score(u, n, between=lambda: None):
                    c, hp = divmod(n, 2)
                    if n == 0:
                        wait(pe, s["qm_lo"], u.count(1, 1))
                        wait(pe, s["lo_done"], u.count(NB, NB))
                    wait(pe, s["exped"], u.count(S, n - 1))
                    w0 = width(c)
                    for i in range(2):
                        if i:
                            between()
                        last = products(nc, slots[n % 2][:, i, w0:HALF], [x[:, c * P:(c + 1) * P] for x in kt[u.b]],
                                        [x[:, 2 * hp + i, w0:HALF] for x in qm[u.b]], True, False)
                        last = nc.tensor.matmul(slots[n % 2][:, i, w0:w0 + P], core.ident_bf, core.causk_bf,
                                                start=False, stop=True, skip_group_check=True)
                    last.then_inc(s["scored"], 1)

                def values(u, c):
                    w0 = width(c)
                    if c == 0:
                        wait(pe, s["v_staged"], u.count(1, 1))
                        wait(pe, s["raw_done"], u.count(1))
                    wait(pe, s["exped"], u.count(S, 2 * c + 2))
                    for h in range(GH):
                        last = nc.tensor.matmul(outs[HPAD * h:HPAD * (h + 1), w0:HALF], vals[u.b][:, c, h, :],
                                                probs[:, (2 * c + h // 2) % 4, h % 2, w0:HALF], start=c == 0, stop=c == C - 1,
                                                skip_group_check=True)
                    last.then_inc(s["pv_done"], 1)

                def all_values(j):
                    wait(pe, s["v_copied"], j - 1)
                    for i in range(2):
                        rows = slice((2 * j + i) * P, (2 * j + i + 1) * P)
                        for c in range(KC):
                            last = products(nc, slots[j % 2][:, 0, i * DIM:(i + 1) * DIM], [x[:, c, rows] for x in src],
                                            [x[:, c, :] for x in wv], c == 0, c == KC - 1)
                    last.then_inc(s["v_full"], 1)

                def first(u):
                    for i in range(NPJ):
                        project(u, i)
                    for x in range(X):
                        for j in range(C):
                            if values_at[j] == x:
                                all_values(j)
                        for i in range(NPJ):
                            if with_max[i] == x:
                                project(u.next(), i)
                        score_max(u, x)
                    turn_neg(u, NPJ)
                    pe.wait_ge(s["v_copied"], C)
                    pe.wait_ge(s["preset"], 6)
                    score(u, 0)

                def unit(u):
                    nxt = None if u.last else u.next()
                    for n in range(S):
                        maxima = [x for x in range(X) if nxt and max_at[x] == n]

                        def some(parts):
                            for _ in range(-(-len(maxima) // parts)):
                                score_max(nxt, maxima.pop(0))

                        if n + 1 < S:
                            score(u, n + 1, lambda: some(4))
                        elif nxt:
                            score(nxt, 0)
                        some(3)
                        if u.projects():
                            for i in range(NPJ):
                                if piece_at[i] == n:
                                    project(u.after_next(), i, piece_at[i] > turn_at)
                        if n == turn_at and nxt:
                            turn_neg(nxt, BEFORE_TURN if u.projects() else 0)
                        some(2)
                        if n % 2:
                            values(u, n // 2)
                        some(1)

                units(pe, first, unit)

            @block.scalar
            def _(act):
                def weights_hi(g):
                    wait(act, s["w_loaded"], g * 16 + 16)
                    wait(act, s["proj_full"], g * (2 * NPJ))
                    nc.scalar.copy(w[0][:, :, :], w_raw[:, :, :]).then_inc(s["w_hi"], 1)

                def high_parts(u):
                    for j in range(NB):
                        wait(act, s["whole_done"], u.count(NB, j + 1))
                        if j == 0:
                            wait(act, s["qm_hi"], u.count(1))
                            wait(act, s["lo_done"], u.count(NB, 1 - NB))
                        dst = kt[u.b][0][:, (j - 1) * HALF:j * HALF] if j else q_hi[:, :]
                        nc.scalar.copy(dst, whole[:, u.b, j, :]).then_inc(s["hi_done"], 1)

                def stage_values(u):
                    wait(act, s["pv_done"], u.count(C, -C))
                    nc.scalar.copy(vals[u.b][:, :, :, 0:HD],
                                   v_all[:, u.b * C:(u.b + 1) * C, bass.ts(u.g, GH * HD)].rearrange("p t (h d) -> p t h d", d=HD)).then_inc(s["v_staged"], 1)

                def exp(u, n):
                    c = n // 2
                    w0 = width(c)
                    wait(act, s["scored"], u.count(S, n + 1))
                    wait(act, s["pv_done"], u.count(C, c - 1))
                    nc.scalar.activation(probs[:, n % 4, :, w0:HALF], slots[n % 2][:, :, w0:HALF], ACT.Exp,
                                         scale=SCALE).then_inc(s["exped"], 1)

                def raw_out(u):
                    wait(act, s["pv_done"], u.count(C, C))
                    nc.scalar.copy(attn[:, bass.ts(u.g, 1), u.b * SEQ:(u.b + 1) * SEQ], outs[:, :].unsqueeze(1)).then_inc(s["raw_done"], 1)

                def mask_low(u):
                    wait(act, s["low_done"], u.count(1, 1))
                    for h in range(GH):
                        last = nc.scalar.activation(qm[u.b][1][:, h, :], q_low[:, :], ACT.Identity, scale=mask[h])
                    last.then_inc(s["qm_lo"], 1)

                def first(u):
                    act.wait_ge(s["tables"], 32)
                    weights_hi(0)
                    for v in (u, u.next()):
                        high_parts(v)
                    act.wait_ge(s["v_copied"], C)
                    act.wait_ge(s["preset"], 6)
                    stage_values(u)
                    mask_low(u)

                def unit(u):
                    nxt = None if u.last else u.next()
                    for n in range(S):
                        if n == 0 and not u.first:
                            raw_out(u.before())
                        exp(u, n)
                        if n == 0 and u.b == 0 and u.projects():
                            weights_hi(u.g + 1)
                        if nxt and n == turn_at - 1:
                            stage_values(nxt)
                        if nxt and n == turn_at + 1:
                            mask_low(nxt)
                        if n == S - 1 and u.projects():
                            high_parts(u.after_next())

                units(act, first, unit, raw_out)

            @block.vector
            def _(dve):
                def piece(u, i):
                    j = PIECES[i][0]
                    wait(dve, s["proj_full"], u.count(NPJ, i + 1))
                    if i % 2 == 0:
                        wait(dve, s["whole_done"], u.count(NB, j))
                    add = ones_row[:, :] if i == 2 else 0.0
                    nc.vector.scalar_tensor_tensor(rot[:, i % 2, :], work[:, :], add, rope[:, i % 2, :], ALU.add, ALU.mult).then_inc(s["proj_out"], 1)

                def mask_queries(u):
                    wait(dve, s["hi_done"], u.count(NB, 1))
                    wait(dve, s["scored"], u.count(S, -S))
                    for h in range(GH):
                        last = nc.vector.tensor_scalar(qm[u.b][0][:, h, :], q_hi[:, :].bitcast(FP32), mask[h], None, ALU.mult)
                    last.then_inc(s["qm_hi"], 1)

                def maximum(u, x):
                    m, j = divmod(x, KB)
                    keys = (m // GH + 1) * P
                    wait(dve, s["max_scored"], u.count(X, x + 1))
                    nc.vector.tensor_reduce(mx[:, m, j:j + 1], mbank[:, x % 2, 0:keys], AX.X, ALU.max).then_inc(s["max_done"], 1)

                def negate(u):
                    wait(dve, s["max_done"], u.count(X, X))
                    nc.vector.tensor_reduce(mx_all[:, :], mx[:, :, :], AX.X, ALU.max).then_inc(s["max_all"], 1)
                    wait(dve, s["max_all"], u.count(1, 1))
                    wait(dve, s["neg_turned"], u.count(1))
                    nc.vector.tensor_scalar(neg[:, :, :, HD:HD + 1].bitcast(F32R), mx_all[:, :].rearrange("p (t h a) -> p t h a", h=GH, a=1),
                                            -1.0, None, ALU.mult).then_inc(s["neg_done"], 1)

                def add_low(u):
                    wait(dve, s["neg_turned"], u.count(1, 1))
                    wait(dve, s["lo_done"], u.count(NB, 1))
                    wait(dve, s["qm_lo"], u.count(1))
                    nc.vector.tensor_tensor(q_low[:, :], work[:, :], q_lo[:, :], ALU.add).then_inc(s["low_done"], 1)

                def values_out(j):
                    dve.wait_ge(s["v_full"], j + 1)
                    nc.vector.tensor_copy(v_all[:, 2 * j:2 * j + 2, :],
                                          slots[j % 2][:, 0, :].rearrange("p (t d) -> p t d", d=DIM)).then_inc(s["v_copied"], 1)

                def first(u):
                    dve.wait_ge(s["tables"], 32)
                    for i in range(NPJ):
                        piece(u, i)
                    mask_queries(u)
                    for x in range(X):
                        for j in range(C):
                            if values_at[j] == x:
                                values_out(j)
                        for i in range(NPJ):
                            if with_max[i] == x:
                                piece(u.next(), i)
                        maximum(u, x)
                    dve.wait_ge(s["preset"], 6)
                    negate(u)
                    mask_queries(u.next())
                    add_low(u)

                def unit(u):
                    nxt = None if u.last else u.next()
                    for n in range(S):
                        maxima = [x for x in range(X) if nxt and max_at[x] == n]
                        before_piece = -(-len(maxima) // 2)
                        for x in maxima[:before_piece]:
                            maximum(nxt, x)
                        if u.projects():
                            for i in range(NPJ):
                                if piece_at[i] == n:
                                    piece(u.after_next(), i)
                        for x in maxima[before_piece:]:
                            maximum(nxt, x)
                        if nxt and n == turn_at:
                            negate(nxt)
                            add_low(nxt)
                        if n == S - 1 and u.projects():
                            mask_queries(u.after_next())

                units(dve, first, unit)


def cross_attention(nc, core, tag, qsrc, ksrc, v_all, wv, w_dram, attn, cols_dram, bv_dram, loads):
    C = ksrc[0].shape[2] // P // BATCH
    KB = C * P // HALF
    S = 2 * C
    M = (NT // BATCH) * GH
    NB = 2 * (KB + 1)
    W_COLS = [(min(z // 2, 1) * 2 + z % 2) * P for z in range(NB)]
    X = M * KB
    turn_at = S - 4
    piece_at = [1, 3, 5, 8, 10, 12]
    max_at = [1 + x * (turn_at - 1) // X for x in range(X)]
    values_at = [j * X // C for j in range(C)]
    with_max = [2 + i * (X - 2) // NB for i in range(NB)]
    SCALE = HD ** -0.5
    with ExitStack() as ctx:
        def sb(name, shape, dt=FP32):
            return ctx.enter_context(nc.sbuf_tensor(f"{tag}_{name}", shape, dt))

        def ps(name, shape):
            return ctx.enter_context(nc.psum_tensor(f"{tag}_{name}", shape, FP32))

        v_bias = sb("v_bias", [P, DIM])
        w_raw = sb("w_raw", [P, KC, 4 * P])
        w = [sb(f"w{x}", [P, KC, 4 * P], F32R) for x in ("hi", "lo")]
        cols = sb("cols", [P, GROUPS, 4])
        group_cols = sb("group_cols", [P, 1, 4])
        whole = sb("whole", [P, NB, HALF])
        high = sb("high", [P, NB, HALF], F32R)
        kt = [sb(f"kt{k}", [P, 2, C * P], F32R) for k in range(2)]
        q0 = sb("q0", [P, 2, HALF], F32R)
        qt = [sb(f"qt{k}", [P, 2, HALF], F32R) for k in range(2)]
        vals = [sb(f"v{k}", [P, C, GH, HPAD]) for k in range(2)]
        mx, mx_all, neg = sb("mx", [P, M, KB]), sb("mx_all", [P, M]), sb("neg", [P, NT // BATCH, GH, QPAD])
        probs = sb("probs", [P, 4, 2, HALF])
        slots = [ps(f"scores{i}", [P, 2, HALF]) for i in range(2)]
        outs, work = ps("outs", [P, HALF]), ps("work", [P, HALF])
        mbank = ps("maxima", [P, 2, HALF])
        minus_low = [core.const[:, C_LOW + i:C_LOW + i + 1] for i in range(2)]
        names = ("preset tables v_full v_copied cols_ready w_loaded w_hi w_lo v_staged proj_full proj_out hi_done parted "
                 "max_scored max_done max_all neg_done neg_turned q_done scored exped pv_done raw_done").split()
        s = {n: core.sem(f"{tag}_{n}") for n in names}

        class Unit:

            def __init__(self, g, b):
                self.g, self.b = g, b
                self.first, self.last = isinstance(g, int) and (g, b) == (0, 0), isinstance(g, int) and (g, b) == (GROUPS - 1, 1)

            def count(self, per, more=0):
                return self.g * (2 * per) + (self.b * per + more)

            def next(self):
                return Unit(self.g, 1) if self.b == 0 else Unit(self.g + 1, 0)

            def after_next(self):
                return Unit(self.g + 1, self.b)

            def projects(self):
                return not (isinstance(self.g, int) and self.g == GROUPS - 1)

            def before(self):
                return Unit(self.g, 0) if self.b == 1 else Unit(self.g - 1, 1)

        def units(eng, first, unit, end=lambda u: None):
            first(Unit(0, 0))
            for b in range(BATCH):
                unit(Unit(0, b))
            with eng.Fori(1, GROUPS - 1) as g:
                for b in range(BATCH):
                    unit(Unit(g, b))
            for b in range(BATCH):
                unit(Unit(GROUPS - 1, b))
            end(Unit(GROUPS - 1, 1))

        with nc.Block() as block:
            @block.sync
            def _(sp):
                sp.dma_start(w_raw[:, :, :], w_dram[0]).then_inc(s["w_loaded"], 16)
                sp.dma_start(cols[:, :, :], cols_dram).then_inc(s["tables"], 16)
                sp.dma_start(v_bias[:, :], bv_dram.partition_broadcast(P)).then_inc(s["tables"], 16)
                for g in range(1, GROUPS):
                    sp.wait_ge(s["w_lo"], g)
                    sp.dma_start(w_raw[:, :, :], w_dram[g]).then_inc(s["w_loaded"], 16)
                sp.wait_ge(s["v_staged"], BATCH * GROUPS)
                for dst, src, sem in loads:
                    sp.dma_start(dst, src).then_inc(sem, 16)

            @block.gpsimd
            def _(pool):
                def split_weights(g):
                    wait(pool, s["w_hi"], g + 1)
                    nc.gpsimd.tensor_tensor(w[1][:, :, :], w_raw[:, :, :], w[0][:, :, :].bitcast(FP32), ALU.subtract).then_inc(s["w_lo"], 1)

                for buf in vals:
                    nc.gpsimd.memset(buf[:, :, :, HD:HPAD], 0.0).then_inc(s["preset"], 1)
                nc.gpsimd.memset(neg[:, :, :, :], 0.0).then_inc(s["preset"], 1)
                pool.wait_ge(s["preset"], 3)
                for buf in vals:
                    nc.gpsimd.memset(buf[:, :, :, HD:HD + 1], 1.0).then_inc(s["preset"], 1)

                def first(u):
                    split_weights(0)

                def unit(u):
                    if u.b == 0 and u.projects():
                        split_weights(u.g + 1)

                units(pool, first, unit)

            @block.tensor
            def _(pe):
                def project(u, z, between=lambda: None):
                    if z == 0 and u.b == 0:
                        wait(pe, s["w_lo"], u.g + 1)
                    wait(pe, s["proj_out"], u.count(NB, z))
                    src = ksrc if z >= 2 else qsrc
                    n0 = u.b * C * P + (z // 2 - 1) * HALF if z >= 2 else u.b * SEQ
                    for c in range(KC):
                        if c:
                            between()
                        last = products(nc, work[:, :], [x[:, c, W_COLS[z]:W_COLS[z] + P] for x in w],
                                        [x[:, c, n0:n0 + HALF] for x in src], c == 0, c == KC - 1)
                    last.then_inc(s["proj_full"], 1)

                def score_max(u, x):
                    m, j = divmod(x, KB)
                    tq, h = divmod(m, GH)
                    rows, pair = slice(QPAD * (h % 2), QPAD * (h % 2 + 1)), h // 2
                    if x == 0:
                        wait(pe, s["parted"], u.count(NB, NB))
                        wait(pe, s["q_done"], u.count(2))
                    wait(pe, s["max_done"], u.count(X, x - 1))
                    nc.tensor.matmul(mbank[:, x % 2, :], q0[rows, pair, tq * P:(tq + 1) * P],
                                     kt[u.b][rows, pair, j * HALF:(j + 1) * HALF], start=True, stop=True,
                                     skip_group_check=True).then_inc(s["max_scored"], 1)

                def turn_neg(u):
                    wait(pe, s["neg_done"], u.count(1, 1))
                    for pair in range(2):
                        for t in range(NT // BATCH):
                            last = nc.tensor.transpose(mbank[:, pair, t * P:(t + 1) * P],
                                                       neg[:, t, 2 * pair:2 * pair + 2, :].rearrange("p h d -> p (h d)"), core.ident)
                        last.then_inc(s["neg_turned"], 1)

                def score(u, n, between=lambda: None):
                    c, pair = divmod(n, 2)
                    if n == 0:
                        wait(pe, s["q_done"], u.count(2, 2))
                    wait(pe, s["exped"], u.count(S, n - 1))
                    for i in range(2):
                        if i:
                            between()
                        rows = slice(QPAD * i, QPAD * (i + 1))
                        last = nc.tensor.matmul(slots[n % 2][:, i, :], kt[u.b][rows, pair, c * P:(c + 1) * P],
                                                qt[u.b][rows, pair, :], start=True, stop=True, skip_group_check=True)
                    last.then_inc(s["scored"], 1)

                def values(u, c):
                    if c == 0:
                        wait(pe, s["v_staged"], u.count(1, 1))
                        wait(pe, s["raw_done"], u.count(1))
                    wait(pe, s["exped"], u.count(S, 2 * c + 2))
                    for h in range(GH):
                        last = nc.tensor.matmul(outs[HPAD * h:HPAD * (h + 1), :], vals[u.b][:, c, h, :],
                                                probs[:, (2 * c + h // 2) % 4, h % 2, :], start=c == 0, stop=c == C - 1,
                                                skip_group_check=True)
                    last.then_inc(s["pv_done"], 1)

                def all_values(j):
                    wait(pe, s["v_copied"], j - 1)
                    for i in range(2):
                        rows = slice((2 * j + i) * P, (2 * j + i + 1) * P)
                        for c in range(KC):
                            last = products(nc, slots[j % 2][:, 0, i * DIM:(i + 1) * DIM], [x[:, c, rows] for x in ksrc],
                                            [x[:, c, :] for x in wv], c == 0, c == KC - 1)
                    last.then_inc(s["v_full"], 1)

                def first(u):
                    for z in range(NB):
                        project(u, z)
                    for x in range(X):
                        for j in range(C):
                            if values_at[j] == x:
                                all_values(j)
                        for z in range(NB):
                            if with_max[z] == x:
                                project(u.next(), z)
                        score_max(u, x)
                    turn_neg(u)
                    pe.wait_ge(s["v_copied"], C)
                    pe.wait_ge(s["preset"], 5)
                    score(u, 0)

                def unit(u):
                    nxt = None if u.last else u.next()
                    for n in range(S):
                        maxima = [x for x in range(X) if nxt and max_at[x] == n]

                        def some(parts):
                            for _ in range(-(-len(maxima) // parts)):
                                score_max(nxt, maxima.pop(0))

                        if n + 1 < S:
                            score(u, n + 1, lambda: some(4))
                        elif nxt:
                            score(nxt, 0)
                        some(3)
                        if n == 0 and not u.first:
                            values(u.before(), C - 1)
                        elif n and n % 2 == 0:
                            values(u, n // 2 - 1)
                        if u.projects():
                            for z in range(NB):
                                if piece_at[z] == n:
                                    project(u.after_next(), z, lambda: some(2))
                        if n == turn_at and nxt:
                            turn_neg(nxt)
                        some(2)
                        some(1)

                units(pe, first, unit, lambda u: values(u, C - 1))

            @block.scalar
            def _(act):
                def weights_hi(g):
                    wait(act, s["w_loaded"], g * 16 + 16)
                    wait(act, s["proj_full"], g * (2 * NB))
                    nc.scalar.copy(w[0][:, :, :], w_raw[:, :, :]).then_inc(s["w_hi"], 1)
                    nc.scalar.copy(group_cols[:, :, :], cols[:, bass.ts(g, 1), :]).then_inc(s["cols_ready"], 1)

                def piece(u, z):
                    wait(act, s["proj_full"], u.count(NB, z + 1))
                    wait(act, s["parted"], u.count(NB, z + 1 - NB))
                    if z == 0 and u.b == 0:
                        wait(act, s["cols_ready"], u.g + 1)
                    both = group_cols[:, 0, 2:4] if z >= 2 else group_cols[:, 0, 0:2]
                    nc.scalar.activation(whole[:, z, :], work[:, :], ACT.Identity, bias=both[:, z % 2:z % 2 + 1]).then_inc(s["proj_out"], 1)

                def high_part(u, z):
                    wait(act, s["proj_out"], u.count(NB, z + 1))
                    wait(act, s["parted"], u.count(NB, z + 1 - NB))
                    nc.scalar.copy(high[:, z, :], whole[:, z, :]).then_inc(s["hi_done"], 1)

                def stage_values(u):
                    wait(act, s["pv_done"], u.count(C, -C))
                    nc.scalar.copy(vals[u.b][:, :, :, 0:HD],
                                   v_all[:, u.b * C:(u.b + 1) * C, bass.ts(u.g, GH * HD)].rearrange("p t (h d) -> p t h d", d=HD)).then_inc(s["v_staged"], 1)

                def exp(u, n):
                    c = n // 2
                    wait(act, s["scored"], u.count(S, n + 1))
                    wait(act, s["pv_done"], u.count(C, c - 1))
                    nc.scalar.activation(probs[:, n % 4, :, :], slots[n % 2][:, :, :], ACT.Exp,
                                         scale=SCALE).then_inc(s["exped"], 1)

                def raw_out(u):
                    wait(act, s["pv_done"], u.count(C, C))
                    nc.scalar.copy(attn[:, bass.ts(u.g, 1), u.b * SEQ:(u.b + 1) * SEQ], outs[:, :].unsqueeze(1)).then_inc(s["raw_done"], 1)

                def first(u):
                    act.wait_ge(s["tables"], 32)
                    weights_hi(0)
                    for v in (u, u.next()):
                        for z in range(NB):
                            piece(v, z)
                            high_part(v, z)
                    act.wait_ge(s["v_copied"], C)
                    act.wait_ge(s["preset"], 5)
                    stage_values(u)

                def unit(u):
                    nxt = None if u.last else u.next()
                    for n in range(S):
                        if n == 1 and not u.first:
                            raw_out(u.before())
                        exp(u, n)
                        if n == 0 and u.b == 0 and u.projects():
                            weights_hi(u.g + 1)
                        if u.projects():
                            for z in range(NB):
                                if piece_at[z] + 1 == n:
                                    piece(u.after_next(), z)
                                    high_part(u.after_next(), z)
                        if nxt and n == turn_at - 1:
                            stage_values(nxt)

                units(act, first, unit, raw_out)

            @block.vector
            def _(dve):
                def part(u):
                    for z in range(NB):
                        wait(dve, s["hi_done"], u.count(NB, z + 1))
                        if z == 0:
                            wait(dve, s["scored"], u.count(S, -S))
                            wait(dve, s["q_done"], u.count(2))
                        dst = q0[:, z, :] if z < 2 else kt[u.b][:, z % 2, (z // 2 - 1) * HALF:(z // 2) * HALF]
                        nc.vector.scalar_tensor_tensor(dst, high[:, z, :].bitcast(FP32), minus_low[min(z // 2, 1)],
                                                       whole[:, z, :], ALU.mult, ALU.add).then_inc(s["parted"], 1)

                def maximum(u, x):
                    m, j = divmod(x, KB)
                    wait(dve, s["max_scored"], u.count(X, x + 1))
                    nc.vector.tensor_reduce(mx[:, m, j:j + 1], mbank[:, x % 2, :], AX.X, ALU.max).then_inc(s["max_done"], 1)

                def negate(u):
                    wait(dve, s["max_done"], u.count(X, X))
                    nc.vector.tensor_reduce(mx_all[:, :], mx[:, :, :], AX.X, ALU.max).then_inc(s["max_all"], 1)
                    wait(dve, s["max_all"], u.count(1, 1))
                    wait(dve, s["neg_turned"], u.count(2))
                    nc.vector.tensor_scalar(neg[:, :, :, 3 * HD:3 * HD + 1].bitcast(F32R), mx_all[:, :].rearrange("p (t h a) -> p t h a", h=GH, a=1),
                                            -1.0, None, ALU.mult).then_inc(s["neg_done"], 1)

                def add_maxima(u):
                    for pair in range(2):
                        wait(dve, s["neg_turned"], u.count(2, pair + 1))
                        nc.vector.tensor_tensor(qt[u.b][:, pair, :], mbank[:, pair, :], q0[:, pair, :].bitcast(FP32),
                                                ALU.add).then_inc(s["q_done"], 1)

                def values_out(j):
                    dve.wait_ge(s["v_full"], j + 1)
                    nc.vector.tensor_tensor(v_all[:, 2 * j:2 * j + 2, :], slots[j % 2][:, 0, :].rearrange("p (t d) -> p t d", d=DIM),
                                            v_bias[:, :].unsqueeze(1).to_broadcast([P, 2, DIM]), ALU.add).then_inc(s["v_copied"], 1)

                def first(u):
                    dve.wait_ge(s["tables"], 32)
                    part(u)
                    for x in range(X):
                        for j in range(C):
                            if values_at[j] == x:
                                values_out(j)
                        maximum(u, x)
                    dve.wait_ge(s["preset"], 5)
                    negate(u)
                    add_maxima(u)
                    part(u.next())

                def unit(u):
                    nxt = None if u.last else u.next()
                    for n in range(S):
                        for x in range(X):
                            if nxt and max_at[x] == n:
                                maximum(nxt, x)
                        if nxt and n == turn_at:
                            negate(nxt)
                            add_maxima(nxt)
                        if n == S - 2 and u.projects():
                            part(u.after_next())

                units(dve, first, unit)


def add_heads(nc, core, attn, gate):
    with ExitStack() as ctx:
        banks = [ctx.enter_context(nc.psum_tensor(f"heads_bank{i}", [P, GROUPS * GH, HPAD], FP32)) for i in range(2)]
        inv = ctx.enter_context(nc.sbuf_tensor("heads_inv", [P, NT, GROUPS * GH, 1], FP32))
        normed = ctx.enter_context(nc.sbuf_tensor("heads_normed", [P, NT, GROUPS * GH, HD], FP32))
        turned, inverted, divided, added = (core.sem(f"heads_{n}") for n in ("turned", "inverted", "divided", "added"))
        with nc.Block() as block:
            @block.tensor
            def _(pe):
                for t in range(NT):
                    if t >= 2:
                        pe.wait_ge(divided, t - 1)
                    for g in range(GROUPS):
                        last = nc.tensor.transpose(banks[t % 2][:, g * GH:(g + 1) * GH, :].rearrange("p h d -> p (h d)"),
                                                   attn[:, g, t * P:(t + 1) * P], core.ident)
                    last.then_inc(turned, 1)

            @block.vector
            def _(dve):
                for t in range(NT):
                    dve.wait_ge(turned, t + 1)
                    nc.vector.reciprocal(inv[:, t, :, :], banks[t % 2][:, :, HD:HD + 1]).then_inc(inverted, 1)
                    dve.wait_ge(inverted, t + 1)
                    nc.vector.tensor_tensor(normed[:, t, :, :], banks[t % 2][:, :, 0:HD],
                                            inv[:, t, :, :].to_broadcast([P, GROUPS * GH, HD]), ALU.mult).then_inc(divided, 1)
                    dve.wait_ge(divided, t + 1)
                    nc.vector.scalar_tensor_tensor(core.x[:, t, :], normed[:, t, :, :].rearrange("p h d -> p (h d)"), gate,
                                                   core.x[:, t, :], ALU.mult, ALU.add).then_inc(added, 1)
                dve.wait_ge(added, NT)


def project_heads(nc, core, attn, w_dram, h, experts, loads):
    HEADS = GROUPS * GH
    with ExitStack() as ctx:
        def sb(name, shape, dt=FP32):
            return ctx.enter_context(nc.sbuf_tensor(f"ph_{name}", shape, dt))

        w_raw, w = sb("w_raw", [P, KC, DIM]), [sb(f"w{x}", [P, KC, DIM], F32R) for x in ("hi", "lo")]
        inv, rows = sb("inv", [P, NT, HEADS, 1]), sb("rows", [P, NT, HEADS, HD])
        back = [sb(f"back{x}", [P, NT, KC, P], F32R) for x in ("hi", "lo")]
        turns = [ctx.enter_context(nc.psum_tensor(f"ph_turn{i}", [P, HEADS, HPAD], FP32)) for i in range(2)]
        backs = [ctx.enter_context(nc.psum_tensor(f"ph_back{i}", [P, KC, P], FP32)) for i in range(2)]
        banks = [ctx.enter_context(nc.psum_tensor(f"ph_bank{i}", [P, DIM], FP32)) for i in range(2)]
        w_loaded, w_split, turned, inverted, divided, turned_back, back_hi, back_lo, full, added = (
            core.sem(f"ph_{n}") for n in ("w_loaded", "w_split", "turned", "inverted", "divided", "turned_back",
                                          "back_hi", "back_lo", "full", "added"))
        with nc.Block() as block:
            @block.sync
            def _(sp):
                sp.dma_start(w_raw[:, :, :], w_dram).then_inc(w_loaded, 16)
                experts.load(sp, 0)
                for dst, src, sem in loads:
                    sp.dma_start(dst, src).then_inc(sem, 16)

            @block.gpsimd
            def _(pool):
                pool.wait_ge(w_loaded, 16)
                nc.gpsimd.tensor_copy(w[0][:, :, :], w_raw[:, :, :]).then_inc(w_split, 1)
                pool.wait_ge(w_split, 1)
                nc.gpsimd.tensor_tensor(w[1][:, :, :], w_raw[:, :, :], w[0][:, :, :].bitcast(FP32), ALU.subtract).then_inc(w_split, 1)
                pool.wait_ge(experts.loaded, 32)
                experts.split_gu(pool, 0)

            @block.tensor
            def _(pe):
                def turn(t):
                    if t >= 2:
                        pe.wait_ge(divided, t - 1)
                    for g in range(GROUPS):
                        last = nc.tensor.transpose(turns[t % 2][:, g * GH:(g + 1) * GH, :].rearrange("p h d -> p (h d)"),
                                                   attn[:, g, t * P:(t + 1) * P], core.ident)
                    last.then_inc(turned, 1)

                def turn_back(t):
                    pe.wait_ge(divided, t + 1)
                    if t >= 2:
                        pe.wait_ge(back_lo, t - 1)
                    for c in range(KC):
                        last = nc.tensor.transpose(backs[t % 2][:, c, :],
                                                   rows[:, t, c * 8:(c + 1) * 8, :].rearrange("p h d -> p (h d)"), core.ident)
                    last.then_inc(turned_back, 1)

                def project(t):
                    pe.wait_ge(back_lo, t + 1)
                    if t == 0:
                        pe.wait_ge(w_split, 2)
                    if t >= 2:
                        pe.wait_ge(added, t - 1)
                    for c in range(KC):
                        last = products(nc, banks[t % 2][:, :], [x[:, t, c, :] for x in back], [x[:, c, :] for x in w],
                                        c == 0, c == KC - 1)
                    last.then_inc(full, 1)

                for t in range(NT + 2):
                    if t < NT:
                        turn(t)
                    if 1 <= t <= NT:
                        turn_back(t - 1)
                    if t >= 2:
                        project(t - 2)

            @block.scalar
            def _(act):
                for t in range(NT):
                    act.wait_ge(turned_back, t + 1)
                    nc.scalar.copy(back[0][:, t, :, :], backs[t % 2][:, :, :]).then_inc(back_hi, 1)

            @block.vector
            def _(dve):
                for t in range(NT + 2):
                    if t < NT:
                        dve.wait_ge(turned, t + 1)
                        nc.vector.reciprocal(inv[:, t, :, :], turns[t % 2][:, :, HD:HD + 1]).then_inc(inverted, 1)
                        dve.wait_ge(inverted, t + 1)
                        nc.vector.tensor_tensor(rows[:, t, :, :], turns[t % 2][:, :, 0:HD],
                                                inv[:, t, :, :].to_broadcast([P, HEADS, HD]), ALU.mult).then_inc(divided, 1)
                    if 1 <= t <= NT:
                        dve.wait_ge(back_hi, t)
                        nc.vector.tensor_tensor(back[1][:, t - 1, :, :], backs[(t - 1) % 2][:, :, :],
                                                back[0][:, t - 1, :, :].bitcast(FP32), ALU.subtract).then_inc(back_lo, 1)
                    if t >= 2:
                        dve.wait_ge(full, t - 1)
                        nc.vector.tensor_tensor(h[:, t - 2, :], banks[t % 2][:, :], h[:, t - 2, :], ALU.add).then_inc(added, 1)
                dve.wait_ge(added, NT)


class Chain:

    def __init__(self, eng, sem):
        self.eng, self.sem, self.n = eng, sem, 0

    def then(self, instruction):
        instruction.then_inc(self.sem, 1)
        self.n += 1
        self.eng.wait_ge(self.sem, self.n)


def logits_by_expert(nc, pe, rows, w, tokens, done):
    for i in range(2):
        for c in range(KC):
            last = products(nc, rows[:, i, :], [x[:, c, :] for x in w], [x[:, c, i * HALF:(i + 1) * HALF] for x in tokens],
                            c == 0, c == KC - 1)
        last.then_inc(done, 1)


def logits_by_token(nc, core, bank, rows, done):
    for t in range(NT):
        last = nc.tensor.transpose(bank[:, t * EXPERTS:(t + 1) * EXPERTS], rows[:, t * P:(t + 1) * P],
                                   core.ident[0:EXPERTS, 0:EXPERTS])
    last.then_inc(done, 1)


def router_probs(nc, core, dve, chain, logits_full, e_ready, exp_done, bank, buf, small):
    def wide(v):
        return v.unsqueeze(2).to_broadcast([P, NT, EXPERTS])

    dve.wait_ge(logits_full, 1)
    logits = bank[:, 0:NT * EXPERTS].rearrange("p (t e) -> p t e", e=EXPERTS)
    chain.then(nc.vector.tensor_reduce(small[:, 0, :], logits, AX.X, ALU.max))
    nc.vector.tensor_tensor(buf, logits, wide(small[:, 0, :]), ALU.subtract).then_inc(e_ready, 1)
    dve.wait_ge(exp_done, 1)
    chain.then(nc.vector.tensor_reduce(small[:, 1, :], buf, AX.X, ALU.add))
    chain.then(nc.vector.reciprocal(small[:, 2, :], small[:, 1, :]))
    chain.then(nc.vector.tensor_tensor(buf, buf, wide(small[:, 2, :]), ALU.mult))


def best_experts(nc, chain, probs, top, where, tiles):
    for t in tiles:
        chain.then(nc.vector.max(top[:, t, :], probs[:, t, :]))
        chain.then(nc.vector.max_index(where[:, t, :], top[:, t, :], probs[:, t, :]))


class Experts:

    def __init__(self, nc, core, stack, gu_dram, down_dram):
        self.nc, self.gu_dram, self.down_dram = nc, gu_dram, down_dram

        def sb(name, shape, dt=FP32):
            return stack.enter_context(nc.sbuf_tensor(f"moe_{name}", shape, dt))

        GU = 2 * HIDDEN
        self.gu_raw, self.down_raw = sb("gu_raw", [P, KC, GU]), sb("down_raw", [P, HCHUNKS, DIM])
        self.gu = [[sb(f"gu{k}{x}", [P, KC, GU], F32R) for x in ("hi", "lo")] for k in range(2)]
        self.down = [[sb(f"down{k}{x}", [P, HCHUNKS, DIM], F32R) for x in ("hi", "lo")] for k in range(2)]
        self.loaded, self.gu_hi, self.down_hi, self.lo = (core.sem(f"moe_{n}") for n in ("loaded", "gu_hi", "down_hi", "w_lo"))

    def load(self, sp, e):
        wait(sp, self.lo, e * 2)
        sp.dma_start(self.gu_raw[:, :, :], self.gu_dram[bass.ts(e, 1)].rearrange("a p k n -> p (a k) n")).then_inc(self.loaded, 16)
        sp.dma_start(self.down_raw[:, :, :], self.down_dram[bass.ts(e, 1)].rearrange("a p k n -> p (a k) n")).then_inc(self.loaded, 16)

    def _split(self, pool, raw, hi, lo, hi_sem, e):
        self.nc.gpsimd.tensor_copy(hi[:, :, :], raw[:, :, :]).then_inc(hi_sem, 1)
        pool.wait_ge(hi_sem, e + 1)
        self.nc.gpsimd.tensor_tensor(lo[:, :, :], raw[:, :, :], hi[:, :, :].bitcast(FP32), ALU.subtract).then_inc(self.lo, 1)

    def split_gu(self, pool, e):
        self._split(pool, self.gu_raw, *self.gu[e % 2], self.gu_hi, e)

    def split_down(self, pool, e):
        self._split(pool, self.down_raw, *self.down[e % 2], self.down_hi, e)


def experts_stage(nc, core, weights, tokens, w_router, router_loaded, h, scratch):
    with ExitStack() as ctx:
        def sb(name, shape, dt=FP32):
            return ctx.enter_context(nc.sbuf_tensor(f"moe_{name}", shape, dt))

        silu, whole = (scratch[:, i, :].rearrange("p (k n) -> p k n", k=2) for i in range(2))
        hid = [[sb(f"hid{n}{x}", [P, HCHUNKS, HALF], F32R) for x in ("hi", "lo")] for n in range(BATCH)]
        combine, probs, small = sb("combine", [P, NT, EXPERTS]), sb("probs", [P, NT, EXPERTS]), sb("small", [P, 5, NT])
        top, where, wheref = sb("top", [P, NT, 8]), sb("where", [P, NT, 8], U32), sb("wheref", [P, NT, 8])
        one = [sb(f"one{i}", [P, NT, EXPERTS]) for i in range(2)]
        wr = [sb(f"wr{x}", [P, KC, EXPERTS], F32R) for x in ("hi", "lo")]
        logit_rows = scratch[0:EXPERTS, 2, :]
        iota = core.const[:, C_IOTA:C_IOTA + EXPERTS]
        by_expert = ctx.enter_context(nc.psum_tensor("moe_logits", [EXPERTS, 2, HALF], FP32))
        gbank = [ctx.enter_context(nc.psum_tensor(f"moe_g{i}", [P, HALF], FP32)) for i in range(2)]
        ubank = [ctx.enter_context(nc.psum_tensor(f"moe_u{i}", [P, HALF], FP32)) for i in range(2)]
        ybank = [ctx.enter_context(nc.psum_tensor(f"moe_y{i}", [P, DIM], FP32)) for i in range(2)]
        units, silus, wholes, hid_hi, hid_lo, y_full, y_added = (
            core.sem(f"moe_{n}") for n in ("units", "silus", "wholes", "hid_hi", "hid_lo", "y_full", "y_added"))
        wr_split, by_expert_full, rows_out, logits_full, e_ready, exp_done, steps, combined = (
            core.sem(f"route_{n}") for n in ("wr_split", "by_expert", "rows_out", "logits", "e_ready", "exp_done", "steps", "combined"))
        HC = BATCH * HCHUNKS
        TILES = HALF // P
        DOWN_AFTER = 1

        def rows_of(c):
            return slice(0, P) if c < FULL_CHUNKS else slice(P - REST, P)

        def tile_after(c):
            return c - DOWN_AFTER if 0 <= c - DOWN_AFTER < TILES else None

        with nc.Block() as block:
            @block.sync
            def _(sp):
                with sp.Fori(1, EXPERTS) as e:
                    weights.load(sp, e)

            @block.gpsimd
            def _(pool):
                for e in range(1, EXPERTS):
                    pool.wait_ge(weights.loaded, (e + 1) * 32)
                    if e >= 2:
                        pool.wait_ge(units, (e - 1) * HC)
                    weights.split_gu(pool, e)
                    if e >= 2:
                        pool.wait_ge(y_full, (e - 1) * NT)
                    weights.split_down(pool, e)

            @block.tensor
            def _(pe):
                def unit(e, k, u):
                    n, c = divmod(u, HCHUNKS)
                    toks = slice(n * HALF, (n + 1) * HALF)
                    wait(pe, wholes, e * HC + (u - 1))
                    blocks = ([(gbank, c * P), (ubank, FULL_CHUNKS * P + c * P)] if c < FULL_CHUNKS
                              else [(gbank, 2 * FULL_CHUNKS * P)])
                    for bank, col in blocks:
                        for kc in range(KC):
                            last = products(nc, bank[u % 2][:, :], [x[:, kc, col:col + P] for x in weights.gu[k]],
                                            [x[:, kc, toks] for x in tokens], kc == 0, kc == KC - 1)
                    last.then_inc(units, 1)

                def down(e, k, n, t):
                    y = n * TILES + t
                    if t == 0:
                        wait(pe, hid_lo, e * HC + (n + 1) * HCHUNKS)
                    wait(pe, y_added, e * NT + (y - 1))
                    for c in range(HCHUNKS):
                        last = products(nc, ybank[y % 2][:, :], [x[rows_of(c), c, t * P:(t + 1) * P] for x in hid[n]],
                                        [x[rows_of(c), c, :] for x in weights.down[k]], c == 0, c == HCHUNKS - 1)
                    last.then_inc(y_full, 1)

                def expert(e, k):
                    wait(pe, weights.lo, e * 2 + 2)
                    for n in range(BATCH):
                        for c in range(HCHUNKS):
                            unit(e, k, n * HCHUNKS + c)
                            if isinstance(e, int) and (e, n, c) == (0, 0, 0):
                                pe.wait_ge(rows_out, 2)
                                logits_by_token(nc, core, ybank[0], logit_rows, logits_full)
                            t = tile_after(c)
                            if isinstance(e, int) and (e, n, t) == (0, 1, 0):
                                pe.wait_ge(combined, 1)
                            if t is not None and n:
                                down(e, k, 0, t)
                            elif t is not None and not (isinstance(e, int) and e == 0):
                                down(e - 1, 1 - k, 1, t)

                def two_experts(i):
                    for k in range(2):
                        expert(i * 2 + k, k)

                pe.wait_ge(wr_split, 2)
                logits_by_expert(nc, pe, by_expert, wr, tokens, by_expert_full)
                repeat(pe, EXPERTS // 2, two_experts)
                for t in range(TILES):
                    down(EXPERTS - 1, 1, 1, t)

            @block.scalar
            def _(act):
                def expert(e):
                    for u in range(HC):
                        n, c = divmod(u, HCHUNKS)
                        wait(act, units, e * HC + (u + 1))
                        wait(act, wholes, e * HC + (u - 1))
                        src = gbank[u % 2][:, :] if c < FULL_CHUNKS else gbank[u % 2][0:REST, :]
                        nc.scalar.activation(silu[rows_of(c), u % 2, :], src, ACT.Silu).then_inc(silus, 1)
                        wait(act, wholes, e * HC + (u + 1))
                        if c == 0:
                            wait(act, y_full, e * NT + (n - 1) * TILES)
                        nc.scalar.copy(hid[n][0][rows_of(c), c, :], whole[rows_of(c), u % 2, :]).then_inc(hid_hi, 1)
                        if isinstance(e, int) and u == 1:
                            act.wait_ge(e_ready, 1)
                            nc.scalar.activation(probs[:, :, :], probs[:, :, :], ACT.Exp).then_inc(exp_done, 1)

                for i in range(2):
                    act.wait_ge(by_expert_full, i + 1)
                    nc.scalar.copy(logit_rows[:, i * HALF:(i + 1) * HALF], by_expert[:, i, :]).then_inc(rows_out, 1)
                repeat(act, EXPERTS, expert)

            @block.vector
            def _(dve):
                def add(e, n, t):
                    y = n * TILES + t
                    wait(dve, y_full, e * NT + (y + 1))
                    nc.vector.scalar_tensor_tensor(h[:, y, :], ybank[y % 2][:, :], combine[:, y, bass.ts(e, 1)], h[:, y, :],
                                                   ALU.mult, ALU.add).then_inc(y_added, 1)

                chain = Chain(dve, steps)

                def route(part):
                    if part == 0:
                        router_probs(nc, core, dve, chain, logits_full, e_ready, exp_done, ybank[0], probs[:, :, :], small)
                    elif part <= 4:
                        best_experts(nc, chain, probs, top, where, range(2 * part - 2, 2 * part))
                    else:
                        chain.then(nc.vector.tensor_copy(wheref[:, :, :], where[:, :, :]))
                        chain.then(nc.vector.tensor_tensor(small[:, 3, :], top[:, :, 0], top[:, :, 1], ALU.add))
                        chain.then(nc.vector.reciprocal(small[:, 4, :], small[:, 3, :]))
                        chain.then(nc.vector.tensor_tensor(top[:, :, 0:2], top[:, :, 0:2],
                                                           small[:, 4, :].unsqueeze(2).to_broadcast([P, NT, 2]), ALU.mult))
                        for i in range(2):
                            chain.then(nc.vector.tensor_tensor(one[i][:, :, :], iota.unsqueeze(1).to_broadcast([P, NT, EXPERTS]),
                                                               wheref[:, :, i:i + 1].to_broadcast([P, NT, EXPERTS]), ALU.is_equal))
                            chain.then(nc.vector.tensor_tensor(one[i][:, :, :], one[i][:, :, :],
                                                               top[:, :, i:i + 1].to_broadcast([P, NT, EXPERTS]), ALU.mult))
                        nc.vector.tensor_tensor(combine[:, :, :], one[0][:, :, :], one[1][:, :, :], ALU.add).then_inc(combined, 1)
                        dve.wait_ge(combined, 1)

                def expert(e):
                    for u in range(HC):
                        n, c = divmod(u, HCHUNKS)
                        rows = rows_of(c)
                        wait(dve, silus, e * HC + (u + 1))
                        wait(dve, hid_lo, e * HC + (u - 1))
                        up = (ubank if c < FULL_CHUNKS else gbank)[u % 2][rows, :]
                        nc.vector.tensor_tensor(whole[rows, u % 2, :], up, silu[rows, u % 2, :], ALU.mult).then_inc(wholes, 1)
                        wait(dve, hid_hi, e * HC + (u + 1))
                        nc.vector.tensor_tensor(hid[n][1][rows, c, :], whole[rows, u % 2, :], hid[n][0][rows, c, :].bitcast(FP32),
                                                ALU.subtract).then_inc(hid_lo, 1)
                        if isinstance(e, int) and 1 <= u <= 6:
                            route(u - 1)
                        t = tile_after(c)
                        if t is not None and n:
                            add(e, 0, t)
                        elif t is not None and not (isinstance(e, int) and e == 0):
                            add(e - 1, 1, t)

                dve.wait_ge(router_loaded, 16)
                nc.vector.tensor_copy(wr[0][:, :, :], w_router[:, :, :]).then_inc(wr_split, 1)
                dve.wait_ge(wr_split, 1)
                nc.vector.tensor_tensor(wr[1][:, :, :], w_router[:, :, :], wr[0][:, :, :].bitcast(FP32), ALU.subtract).then_inc(wr_split, 1)
                repeat(dve, EXPERTS, expert)
                for t in range(TILES):
                    add(EXPERTS - 1, 1, t)
                dve.wait_ge(y_added, EXPERTS * NT)


def gated_add(nc, core, tag, h, gate):
    added = core.sem(f"{tag}_added")
    with nc.Block() as block:
        @block.vector
        def _(dve):
            nc.vector.scalar_tensor_tensor(core.x[:, :, :].rearrange("p t d -> p (t d)"), h[:, :, :].rearrange("p t d -> p (t d)"),
                                           gate, core.x[:, :, :].rearrange("p t d -> p (t d)"), ALU.mult, ALU.add).then_inc(added, 1)
            dve.wait_ge(added, 1)


def switch_stage(nc, core, tokens, wr_raw, bias, small_loaded, w, gate, out):
    with ExitStack() as ctx:
        def sb(name, shape, dt=FP32):
            return ctx.enter_context(nc.sbuf_tensor(f"switch_{name}", shape, dt))

        wr = [wr_raw, sb("wr_hi", [P, KC, EXPERTS], F32R), sb("wr_lo", [P, KC, EXPERTS], F32R)]
        probs, small = sb("probs", [P, NT, EXPERTS]), sb("small", [P, 3, NT])
        top, where, wheref = sb("top", [P, NT, 8]), sb("where", [P, NT, 8], U32), sb("wheref", [P, NT, 8])
        one, one_bf, kept = sb("one", [P, NT, EXPERTS]), sb("one_bf", [P, NT, EXPERTS], BF16), sb("kept", [P, NT, EXPERTS])
        tri_bf = sb("tri", [P, P], BF16)
        weights_t, logit_rows = sb("weights_t", [EXPERTS, TOK]), sb("logit_rows", [EXPERTS, TOK])
        y = sb("y", [P, NT, DIM])
        bank = ctx.enter_context(nc.psum_tensor("switch_bank", [P, HALF], FP32))
        locs = ctx.enter_context(nc.psum_tensor("switch_locs", [P, HALF], FP32))
        turn = ctx.enter_context(nc.psum_tensor("switch_turn", [EXPERTS, 2, HALF], FP32))
        acc = [ctx.enter_context(nc.psum_tensor(f"switch_acc{i}", [P, HALF], FP32)) for i in range(4)]
        names = "by_expert rows_out wr_split full e_ready exp_done steps one_ready located weights_ready turned turned_out y_full y_done stored".split()
        s = {n: core.sem(f"switch_{n}") for n in names}
        iota = core.const[:, C_IOTA:C_IOTA + EXPERTS]
        UNITS = 1 + EXPERTS // 2
        with nc.Block() as block:
            @block.sync
            def _(sp):
                for t in range(NT):
                    sp.wait_ge(s["y_done"], (t + 1) * (UNITS + 1))
                    sp.dma_start(out[t * P:(t + 1) * P, :], core.x[:, t, :]).then_inc(s["stored"], 16)
                sp.wait_ge(s["stored"], NT * 16)

            @block.tensor
            def _(pe):
                pe.wait_ge(s["wr_split"], 3)
                logits_by_expert(nc, pe, turn, wr[1:], tokens, s["by_expert"])
                pe.wait_ge(s["rows_out"], 2)
                logits_by_token(nc, core, bank, logit_rows, s["full"])
                pe.wait_ge(s["one_ready"], 1)
                for t in range(NT):
                    for e in range(t + 1):
                        last = nc.tensor.matmul(locs[:, t * EXPERTS:(t + 1) * EXPERTS], core.ones_bf if e < t else tri_bf[:, :],
                                                one_bf[:, e, :], start=e == 0, stop=e == t, skip_group_check=True)
                last.then_inc(s["located"], 1)
                pe.wait_ge(s["weights_ready"], 1)
                for t in range(NT):
                    last = nc.tensor.transpose(turn[:, t // 4, (t % 4) * P:(t % 4 + 1) * P], kept[:, t, :], core.ident)
                last.then_inc(s["turned"], 1)
                pe.wait_ge(s["turned_out"], 1)
                for u in range(NT * UNITS):
                    t, i = divmod(u, UNITS)
                    if u >= 4:
                        pe.wait_ge(s["y_done"], u - 3 + (u - 4) // UNITS)
                    if i == 0:
                        last = nc.tensor.matmul(acc[u % 4][:, 0:DIM], weights_t[:, t * P:(t + 1) * P], bias[:, :], start=True, stop=True)
                    else:
                        for c in range(KC):
                            last = products(nc, acc[u % 4][:, :], [x[:, c, t * P:(t + 1) * P] for x in tokens],
                                            [x[:, c, (2 * i - 2) * DIM:2 * i * DIM] for x in w], c == 0, c == KC - 1)
                    last.then_inc(s["y_full"], 1)

            @block.scalar
            def _(act):
                for i in range(2):
                    act.wait_ge(s["by_expert"], i + 1)
                    nc.scalar.copy(logit_rows[:, i * HALF:(i + 1) * HALF], turn[:, i, :]).then_inc(s["rows_out"], 1)
                act.wait_ge(s["e_ready"], 1)
                nc.scalar.activation(probs[:, :, :], probs[:, :, :], ACT.Exp).then_inc(s["exp_done"], 1)
                act.wait_ge(s["turned"], 1)
                nc.scalar.copy(weights_t[:, :], turn[:, :, :].rearrange("p a n -> p (a n)")).then_inc(s["turned_out"], 1)

            @block.vector
            def _(dve):
                chain = Chain(dve, s["steps"])
                nc.vector.tensor_copy(tri_bf[:, :], core.const[:, C_TRI:C_TRI + P]).then_inc(s["wr_split"], 1)
                dve.wait_ge(small_loaded, 32)
                nc.vector.tensor_copy(wr[1][:, :, :], wr[0][:, :, :]).then_inc(s["wr_split"], 1)
                dve.wait_ge(s["wr_split"], 2)
                nc.vector.tensor_tensor(wr[2][:, :, :], wr[0][:, :, :], wr[1][:, :, :].bitcast(FP32), ALU.subtract).then_inc(s["wr_split"], 1)
                router_probs(nc, core, dve, chain, s["full"], s["e_ready"], s["exp_done"], bank, probs[:, :, :], small)
                best_experts(nc, chain, probs, top, where, range(NT))
                chain.then(nc.vector.tensor_copy(wheref[:, :, :], where[:, :, :]))
                chain.then(nc.vector.tensor_tensor(one[:, :, :], iota.unsqueeze(1).to_broadcast([P, NT, EXPERTS]),
                                                   wheref[:, :, 0:1].to_broadcast([P, NT, EXPERTS]), ALU.is_equal))
                nc.vector.tensor_copy(one_bf[:, :, :], one[:, :, :]).then_inc(s["one_ready"], 1)
                dve.wait_ge(s["located"], 1)
                chain.then(nc.vector.scalar_tensor_tensor(
                    kept[:, :, :].rearrange("p t e -> p (t e)"), locs[:, 0:NT * EXPERTS], float(CAPACITY),
                    one[:, :, :].rearrange("p t e -> p (t e)"), ALU.is_lt, ALU.mult))
                nc.vector.tensor_tensor(kept[:, :, :], kept[:, :, :], probs[:, :, :], ALU.mult).then_inc(s["weights_ready"], 1)
                dve.wait_ge(s["weights_ready"], 1)
                done = 0
                for u in range(NT * UNITS):
                    t, i = divmod(u, UNITS)
                    dve.wait_ge(s["y_full"], u + 1)
                    if i == 0:
                        nc.vector.tensor_copy(y[:, t, :], acc[u % 4][:, 0:DIM]).then_inc(s["y_done"], 1)
                        done += 1
                        continue
                    dve.wait_ge(s["y_done"], done)
                    e = 2 * i - 2
                    chain.then(nc.vector.scalar_tensor_tensor(y[:, t, :], acc[u % 4][:, 0:DIM], kept[:, t, e:e + 1], y[:, t, :],
                                                              ALU.mult, ALU.add))
                    nc.vector.scalar_tensor_tensor(y[:, t, :], acc[u % 4][:, DIM:2 * DIM], kept[:, t, e + 1:e + 2], y[:, t, :],
                                                   ALU.mult, ALU.add).then_inc(s["y_done"], 1)
                    done += 1
                    if i == UNITS - 1:
                        dve.wait_ge(s["y_done"], done)
                        nc.vector.scalar_tensor_tensor(core.x[:, t, :], y[:, t, :], gate, core.x[:, t, :],
                                                       ALU.mult, ALU.add).then_inc(s["y_done"], 1)
                        done += 1


class Ahead:

    def __init__(self, nc, core, tag, loads=(), splits=(), pool_work=None):
        self.nc, self.loads, self.splits, self.pool_work = nc, loads, splits, pool_work
        self.hi_done, self.lo_done = core.sem(f"{tag}_ahead_hi"), core.sem(f"{tag}_ahead_lo")

    def sync(self, sp):
        for dst, src, sem in self.loads:
            sp.dma_start(dst, src).then_inc(sem, 16)

    def scalar(self, act):
        for raw, hi, _lo, loaded, value in self.splits:
            act.wait_ge(loaded, value)
            self.nc.scalar.copy(hi, raw).then_inc(self.hi_done, 1)

    def gpsimd(self, pool):
        for i, (raw, hi, lo, _loaded, _value) in enumerate(self.splits):
            pool.wait_ge(self.hi_done, i + 1)
            self.nc.gpsimd.tensor_tensor(lo, raw, hi.bitcast(FP32), ALU.subtract).then_inc(self.lo_done, 1)
        if self.splits:
            pool.wait_ge(self.lo_done, len(self.splits))
        if self.pool_work is not None:
            self.pool_work(pool)


def program(nc, a, out):
    with ExitStack() as ctx:
        core = Core(nc, ctx)
        par, gates = core.par, core.gates

        def buffer(stack, name, shape, dt=FP32):
            return stack.enter_context(nc.sbuf_tensor(name, shape, dt))

        def pair(stack, name, cols):
            return [buffer(stack, f"{name}_{x}", [P, KC, cols], F32R) for x in ("hi", "lo")]

        def lasting(name):
            return nc.alloc_semaphore(name=name)

        with ExitStack() as st:
            attn = buffer(st, "lat_attn", [P, PAIRS, TOK])
            lat, cn = pair(st, "lat", TOK), pair(st, "cn", CTOK)
            wo_loaded = core.sem("lat_wo_loaded")
            with ExitStack() as src:
                w_raw, rope = buffer(src, "lat_w_raw", [P, KC, 3 * P]), buffer(src, "lat_rope", [P, CTX // P, 3, 32])
                ctx_loaded, w_loaded, rope_loaded = core.sem("ctx_loaded"), core.sem("lat_w_loaded"), core.sem("lat_rope_loaded")
                with ExitStack() as rows:
                    ctx_rows = buffer(rows, "ctx_rows", [P, NCT, DIM])
                    load_stage(nc, core, a["x"], a["const"], a["par"], a["gates"], [
                        (ctx_rows[:, :, :], a["ctx"].rearrange("(t p) d -> p t d", p=P), ctx_loaded),
                        (w_raw[:, :, :], a["lat_w"][0], w_loaded),
                        (rope[:, :, 0, :], a["lat_rope"][0], rope_loaded), (rope[:, :, 2, :], a["lat_rope"][1], rope_loaded)])
                    norm_stage(nc, core, "nl", core.x, NT, [("ln", 0), ("ln", 0)], par[:, 0:2], par[:, 2:4], *lat, loaded=core.x_loaded)
                    norm_stage(nc, core, "nc", ctx_rows, NCT, [("ln", 0)], par[:, 4:6], par[:, 6:8], *cn, loaded=ctx_loaded)
                latent_stage(nc, core, lat, cn, a["lat_w"], w_raw, w_loaded, rope, rope_loaded, attn, a["lat_wo"], wo_loaded)
            latent_out(nc, core, attn, latent_wo(cn), a["lat_bo"], gates[:, 0:1])
        core.release()
        late = buffer(ctx, "late", [P, KC, CTOK])
        late_loaded = lasting("late_loaded")
        cross_wv_raw = buffer(ctx, "cross_wv_raw", [P, KC, DIM])
        with ExitStack() as st:
            h, attn = buffer(st, "ffn_h", [P, NT, DIM]), buffer(st, "self_attn", [P, GROUPS, TOK])
            with ExitStack() as src:
                r, wv, wv_raw = pair(src, "r1", TOK), pair(src, "self_wv", DIM), buffer(src, "self_wv_raw", [P, KC, DIM])
                wv_loaded = core.sem("self_wv_loaded")
                norm_stage(nc, core, "n1", core.x, NT, [("ln", 0), ("rms", 1)], par[:, 8:10], None, *r, keep=h,
                           ahead=Ahead(nc, core, "n1", [(wv_raw[:, :, :], a["self_wv"], wv_loaded)],
                                       [(wv_raw[:, :, :], wv[0][:, :, :], wv[1][:, :, :], wv_loaded, 16)]))
                v_all = buffer(src, "self_v", [P, NT, DIM])
                causal_attention(nc, core, "self", r, v_all, wv, a["self_w"], attn, a["self_cols"], a["self_rope"])
            core.release()
            experts = Experts(nc, core, st, a["moe_gu"], a["moe_down"])
            project_heads(nc, core, attn, a["self_wo"], h, experts,
                          [(late[:, :, :], a["ctx_t"], late_loaded), (cross_wv_raw[:, :, :], a["ctx_wv"], late_loaded)])
            with ExitStack() as src:
                r = pair(src, "r2", TOK)
                route_w = buffer(src, "route_w", [P, KC, EXPERTS])
                route_loaded = core.sem("route_w_loaded")
                norm_stage(nc, core, "n2", h, NT, [("rms", 1)], par[:, 10:12], None, *r,
                           ahead=Ahead(nc, core, "n2", [(route_w[:, :, :], a["route_w"], route_loaded)],
                                       pool_work=lambda pool: experts.split_down(pool, 0)))
                experts_stage(nc, core, experts, r, route_w, route_loaded, h, attn)
            gated_add(nc, core, "moe_add", h, gates[:, 2:3])
        core.release()
        with ExitStack() as st:
            attn = buffer(st, "ctx_attn", [P, GROUPS, TOK])
            with ExitStack() as src:
                r, c, wv = pair(src, "r3", TOK), pair(src, "ctx", CTOK), pair(src, "cross_wv", DIM)
                norm_stage(nc, core, "n3", core.x, NT, [("ln", 0)], None, None, *r,
                           ahead=Ahead(nc, core, "n3", splits=[
                               (cross_wv_raw[:, :, :], wv[0][:, :, :], wv[1][:, :, :], late_loaded, 32),
                               (late[:, :, :], c[0][:, :, :], c[1][:, :, :], late_loaded, 32)]))
                v_all = late[:, :, :].rearrange("p k (t d) -> p (k t) d", d=DIM)
                cross_attention(nc, core, "cross", r, c, v_all, wv, a["ctx_w"], attn, a["ctx_cols"], a["ctx_bv"],
                                loads=[(late[:, :, :], a["sw_w"], late_loaded)])
            add_heads(nc, core, attn, gates[:, 1:2])
        core.release()
        with ExitStack() as st:
            r, w = pair(st, "r4", TOK), pair(st, "switch_w", EXPERTS * DIM)
            router, bias = buffer(st, "switch_wr", [P, KC, EXPERTS]), buffer(st, "switch_bias", [EXPERTS, DIM])
            small_loaded = core.sem("switch_loaded")
            norm_stage(nc, core, "n4", core.x, NT, [("ln", 0)], None, None, *r,
                       ahead=Ahead(nc, core, "n4", [(router[:, :, :], a["sw_router"], small_loaded), (bias[:, :], a["sw_b"], small_loaded)],
                                   [(late[:, :, :], w[0][:, :, :], w[1][:, :, :], late_loaded, 48)]))
            switch_stage(nc, core, r, router, bias, small_loaded, w, gates[:, 3:4], out)


def constants():
    import numpy as np
    c = np.zeros((P, C_END), np.float32)
    r = np.arange(P)
    c[:, C_IDENT:C_IDENT + P] = np.eye(P)
    c[:, C_TRI:C_TRI + P] = r[:, None] < r[None, :]
    c[:, C_MASK:C_MASK + GH] = r[:, None] // HPAD == np.arange(GH)[None, :]
    c[:, C_LOW] = -1.0 * (r % QPAD // HD == 2)
    c[:, C_LOW + 1] = -1.0 * (r % QPAD // HD == 1)
    c[:, C_ONES:C_ONES + LAT_D] = 1.0
    c[:, C_IOTA:C_IOTA + EXPERTS] = np.arange(EXPERTS)
    c[:, C_CAUSQ:C_CAUSQ + P] = np.where(r[None, :] > r[:, None], -1e30, 0.0)
    c[:, C_CAUSK:C_CAUSK + P] = np.where(r[:, None] > r[None, :], -1e30, 0.0)
    return c


def rotary_table():
    import numpy as np
    inv_freq = 1.0 / 10000.0 ** (np.arange(0, HD, 2, dtype=np.float32) / HD)
    freqs = np.einsum("i,j->ij", np.arange(SEQ, dtype=np.float32), inv_freq).T
    table = np.zeros((GH, HPAD, 2, SEQ), np.float32)
    table[:, 0:HD, 0] = np.concatenate([np.cos(freqs), np.cos(freqs)])
    table[:, 0:HD, 1] = np.concatenate([-np.sin(freqs), np.sin(freqs)])
    table[:, HD, 0] = 1.0
    return table.reshape(P, 2, SEQ)


def layouts(i):
    import numpy as np

    def chunks(w):
        return np.ascontiguousarray(w.reshape(-1, P, w.shape[-1]).transpose(1, 0, 2))

    a = {k: np.asarray(v) for k, v in i.items()}
    f = {"x": a["x"].reshape(TOK, DIM), "ctx": a["ctx_1024"].reshape(CTOK, DIM), "const": constants()}
    f["ctx_t"] = chunks(f["ctx"].T)
    f["par"] = np.concatenate([a[n].reshape(2, P).T for n in (
        "L0_xattn_ln_lat_g", "L0_xattn_ln_lat_b", "L0_xattn_ln_ctx_g", "L0_xattn_ln_ctx_b", "L0_ffn_g1", "L0_ffn_g2")], 1)
    f["gates"] = np.concatenate([a["g_xattn"], a["g_ffn"]])
    wq, (wk, wv) = a["L0_xattn_Wq"], np.split(a["L0_xattn_Wkv"], 2, axis=1)
    f["lat_w"] = np.stack([np.concatenate([chunks(w[:, p * P:(p + 1) * P]) for w in (wq, wk, wv)], 2) for p in range(PAIRS)])
    f["lat_rope"] = np.stack([a[n].reshape(8, P, 32).transpose(1, 0, 2) for n in ("L0_xattn_cos", "L0_xattn_sin")])
    f["lat_wo"], f["lat_bo"] = chunks(a["L0_xattn_Wo"]), a["L0_xattn_bo"]

    def padded(w, swap=False):
        w = w.reshape(*w.shape[:-1], GROUPS, GH, 2, HD // 2)
        out = np.zeros((*w.shape[:-2], HPAD), w.dtype)
        out[..., 0:HD] = (w[..., ::-1, :] if swap else w).reshape(*w.shape[:-2], HD)
        return np.moveaxis(out.reshape(*w.shape[:-3], P), -2, 0)

    def thrice(w):
        w = w.reshape(*w.shape[:-1], GROUPS, GH, 1, HD)
        out = np.zeros((*w.shape[:-2], 4, HD), w.dtype)
        out[..., 0:3, :] = w
        return np.moveaxis(out.reshape(*w.shape[:-3], GH * QPAD), -2, 0)

    def by_group(*ws):
        return np.stack([np.concatenate([chunks(w[g]) for w in ws], 2) for g in range(GROUPS)])

    f["self_w"] = by_group(padded(a["L0_ffn_wq"]), padded(a["L0_ffn_wq"], True), padded(a["L0_ffn_wk"]), padded(a["L0_ffn_wk"], True))
    f["self_wv"] = chunks(a["L0_ffn_wv"])
    f["self_cols"] = np.broadcast_to(1.0 * (np.arange(P) % HPAD == HD)[:, None], (P, 1)).astype(np.float32)
    f["self_rope"] = rotary_table()
    f["self_wo"] = chunks(a["L0_ffn_wo"])
    f["route_w"] = chunks(a["L0_ffn_w_router"])
    g, u, d = a["L0_ffn_wg"], a["L0_ffn_wu"], a["L0_ffn_wd"]
    full = FULL_CHUNKS * P
    f["moe_gu"] = np.stack([chunks(np.concatenate([g[e, :, :full], u[e, :, :full], g[e, :, full:], u[e, :, full:]], 1))
                            for e in range(EXPERTS)])
    down = np.zeros((EXPERTS, HCHUNKS, P, DIM), np.float32)
    down[:, :FULL_CHUNKS] = d[:, :full].reshape(EXPERTS, FULL_CHUNKS, P, DIM)
    down[:, FULL_CHUNKS, P - REST:] = d[:, full:]
    f["moe_down"] = down.transpose(0, 2, 1, 3)
    f["ctx_w"] = by_group(thrice(a["L1_xattn_Wq"].T), thrice(a["L1_xattn_Wk"].T))
    f["ctx_wv"], f["ctx_bv"] = chunks(a["L1_xattn_Wv"].T), a["L1_xattn_bv"]
    ctx_cols = np.stack([thrice(a["L1_xattn_bq"]), thrice(a["L1_xattn_bk"])], 1).reshape(GROUPS, 2, 2, P)
    ctx_cols[:, 1, :, 3 * HD::QPAD] = 1.0
    f["ctx_cols"] = ctx_cols.reshape(GROUPS, 4, P).transpose(2, 0, 1)
    f["sw_router"] = chunks(a["L1_ffn_wg"])
    f["sw_w"] = a["L1_ffn_W"].transpose(2, 0, 1).reshape(2, P, EXPERTS * DIM).transpose(1, 0, 2)
    f["sw_b"] = a["L1_ffn_b"]
    return {k: np.ascontiguousarray(v) for k, v in f.items()}


def kernel(**inputs):
    import numpy as _np
    import concourse.bacc as _bacc
    from concourse import mybir as _mybir
    from concourse.bass_utils import run_bass_kernel_spmd as _run

    nc = _bacc.Bacc("TRN2", target_bir_lowering=False, num_devices=1)
    arrays, args = {}, {}
    for name, a in layouts(inputs).items():
        arrays[f"in_{name}"] = a
        args[name] = nc.dram_tensor(f"in_{name}", a.shape, _mybir.dt.from_np(a.dtype), kind="ExternalInput").ap()
    out = nc.dram_tensor("out_0", (TOK, DIM), _mybir.dt.float32, kind="ExternalOutput").ap()
    program(nc, args, out)
    r = _run(nc, [arrays], core_ids=[0])
    return _np.asarray(r.results[0]["out_0"]).reshape(BATCH, SEQ, DIM)
```
